# Optimizing a Trainium2 kernel written in Bass

```python
import numpy as np
import jax
import jax.numpy as jnp

def _softmax(x, axis=-1):
    return jax.nn.softmax(x, axis=axis)

def _gelu(x):
    return jax.nn.gelu(x, approximate=True)

def _silu(x):
    return jax.nn.silu(x)

def _sigmoid(x):
    return jax.nn.sigmoid(x)

def _layernorm(x, axis=-1, eps=1e-05):
    m = jnp.mean(x, axis=axis, keepdims=True)
    v = jnp.var(x, axis=axis, keepdims=True)
    return (x - m) / jnp.sqrt(v + eps)

def _scatter_add(tgt, idx, src, axis=0):
    return tgt.at[idx].add(src)

def _segment_sum(src, seg, n):
    return jax.ops.segment_sum(src, seg, n)
kernel_name = 'mk_flamingo_gated_d2_seqx_r8_aba2fa'

def setup_inputs(seed: int=0):
    np.random.seed(seed)
    _w = jnp.asarray

    def _rec_inputs():
        import jax
        import jax.numpy as jnp
        _rk = jax.random.key(seed)
        x = 7.22e-05 + 1 * jax.random.normal(jax.random.fold_in(_rk, 1), (4, 256, 256), jnp.float32)
        _lenS = 256 - jax.random.randint(jax.random.fold_in(_rk, 7), (4,), 0, max(1, 256 // 4) + 1, jnp.int32)
        _lenS2 = 256 - jax.random.randint(jax.random.fold_in(_rk, 8), (4,), 0, max(1, 256 // 4) + 1, jnp.int32)
        _ctx_1024P = jax.random.normal(jax.random.fold_in(_rk, 11), (4, 16, 128), jnp.float32)
        _ctx_1024c = jax.random.dirichlet(jax.random.fold_in(_rk, 511), 0.3 * jnp.ones((16,), jnp.float32), (4, 256))
        _ctx_1024t = jnp.einsum('bsk,bkd->bsd', _ctx_1024c, _ctx_1024P)
        _ctx_1024t = _ctx_1024t * jax.lax.rsqrt(jnp.mean(jnp.square(_ctx_1024t)) + 1e-12) * 0.953939
        ctx_1024 = 2.81802e-05 + 1.00001 * (_ctx_1024t + 0.3 * jax.random.normal(jax.random.fold_in(_rk, 611), (4, 256, 128), jnp.float32))
        _g = jax.random.normal(jax.random.fold_in(_rk, 9001), (2, 2), jnp.float32)
        _g = jnp.sign(_g) * jnp.maximum(jnp.abs(_g), 1.0) + (_g == 0) * 1.0
        g_xattn = _g[0]
        g_ffn = _g[1]
        return (x, ctx_1024, g_xattn, g_ffn)
    x, ctx_1024, g_xattn, g_ffn = _rec_inputs()

    def _L0_xattn_setup():
        import jax, jax.numpy as jnp
        import numpy as np
        key = jax.random.key(seed)
        ks = jax.random.split(key, 6)
        B, L, N, C, D = (8, 64, 256, 128, 128)
        return {'teacher_logits': jax.random.normal(ks[0], (B, L, N), dtype=jnp.float32), 'teacher_features': jax.random.normal(ks[1], (B, N, C), dtype=jnp.float32), 'Wq': jax.random.normal(ks[2], (D, C), dtype=jnp.float32) * (1.0 / np.sqrt(C)), 'bq': jnp.zeros((D,), dtype=jnp.float32), 'Wk': jax.random.normal(ks[3], (D, C), dtype=jnp.float32) * (1.0 / np.sqrt(C)), 'bk': jnp.zeros((D,), dtype=jnp.float32)}
    _L0_xattn_all = _L0_xattn_setup()
    _L0_xattn_in = {k: v for k, v in _L0_xattn_all.items() if k in ('Wq', 'bq', 'Wk', 'bk')}
    del _L0_xattn_all

    def _L0_ffn_setup():
        import jax, jax.numpy as jnp
        import numpy as np
        HIDDEN = 256
        INTER = 704
        EPS = 1e-05

        def rms_norm(x, g):
            var = jnp.mean(x * x, axis=-1, keepdims=True)
            return x * jax.lax.rsqrt(var + EPS) * g

        def activation_quant(x):
            scale = 127.0 / jnp.clip(jnp.max(jnp.abs(x), axis=-1, keepdims=True), 1e-05, None)
            return jnp.clip(jnp.round(x * scale), -128, 127) / scale

        def weight_quant(w):
            scale = 1.0 / jnp.clip(jnp.mean(jnp.abs(w)), 1e-05, None)
            return jnp.clip(jnp.round(w * scale), -1, 1) / scale

        def ste(x, q):
            return x + jax.lax.stop_gradient(q - x)

        def bit_linear(x, w, g):
            xn = rms_norm(x, g)
            xq = ste(xn, activation_quant(xn))
            wq = ste(w, weight_quant(w))
            return xq @ wq.T
        key = jax.random.key(seed)
        k1, k2, k3 = jax.random.split(key, 3)
        x = jax.random.normal(k1, (4, 256, HIDDEN), dtype=jnp.float32)
        gate_w = jax.random.normal(k2, (2 * INTER, HIDDEN), dtype=jnp.float32) * HIDDEN ** (-0.5)
        down_w = jax.random.normal(k3, (HIDDEN, INTER), dtype=jnp.float32) * INTER ** (-0.5)
        gate_norm_w = jnp.ones((HIDDEN,), dtype=jnp.float32)
        down_norm_w = jnp.ones((INTER,), dtype=jnp.float32)
        return {'x': x, 'gate_w': gate_w, 'down_w': down_w, 'gate_norm_w': gate_norm_w, 'down_norm_w': down_norm_w}
    _L0_ffn_all = _L0_ffn_setup()
    _L0_ffn_in = {k: v for k, v in _L0_ffn_all.items() if k in ('gate_w', 'down_w', 'gate_norm_w', 'down_norm_w')}
    del _L0_ffn_all

    def _L1_xattn_setup():
        import jax, jax.numpy as jnp
        import numpy as np
        EPS = 1e-05

        def rmsnorm(x, g, eps=EPS):
            var = jnp.mean(jnp.square(x), axis=-1, keepdims=True)
            return x * jax.lax.rsqrt(var + eps) * g
        key = jax.random.key(seed)
        ks = jax.random.split(key, 8)
        B, Sq, Skv = (2, 512, 64)
        dim, cdim, H, D = (256, 128, 16, 128)
        inner = H * D
        s = lambda f: 1.0 / np.sqrt(f)
        return {'hidden_states': jax.random.normal(ks[0], (B, Sq, dim), jnp.float32), 'encoder_hidden_states': jax.random.normal(ks[1], (B, Skv, cdim), jnp.float32), 'Wq': jax.random.normal(ks[2], (dim, inner), jnp.float32) * s(dim), 'Wk': jax.random.normal(ks[3], (cdim, inner), jnp.float32) * s(cdim), 'Wv': jax.random.normal(ks[4], (cdim, inner), jnp.float32) * s(cdim), 'Wo': jax.random.normal(ks[5], (inner, dim), jnp.float32) * s(inner), 'gq': jnp.ones((D,), jnp.float32), 'gk': jnp.ones((D,), jnp.float32)}
    _L1_xattn_all = _L1_xattn_setup()
    _L1_xattn_in = {k: v for k, v in _L1_xattn_all.items() if k in ('Wq', 'Wk', 'Wv', 'Wo', 'gq', 'gk')}
    del _L1_xattn_all

    def _L1_ffn_setup():
        import jax, jax.numpy as jnp
        import numpy as np
        H = 256
        E = 64
        I = 64
        SI = 64
        TOP_K = 8
        B, T = (2, 64)
        key = jax.random.key(seed)
        ks = jax.random.split(key, 8)
        s = 0.02
        return {'h': jax.random.normal(ks[0], (B, T, H), jnp.float32), 'gate_w': jax.random.normal(ks[1], (E, H), jnp.float32) * s, 'gu_w': jax.random.normal(ks[2], (E, 2 * I, H), jnp.float32) * s, 'dp_w': jax.random.normal(ks[3], (E, H, I), jnp.float32) * s, 'sh_gate_w': jax.random.normal(ks[4], (SI, H), jnp.float32) * s, 'sh_up_w': jax.random.normal(ks[5], (SI, H), jnp.float32) * s, 'sh_down_w': jax.random.normal(ks[6], (H, SI), jnp.float32) * s, 'sh_gate1_w': jax.random.normal(ks[7], (1, H), jnp.float32) * s}
    _L1_ffn_all = _L1_ffn_setup()
    _L1_ffn_in = {k: v for k, v in _L1_ffn_all.items() if k in ('gate_w', 'gu_w', 'dp_w', 'sh_gate_w', 'sh_up_w', 'sh_down_w', 'sh_gate1_w')}
    del _L1_ffn_all
    return {'x': x, 'ctx_1024': ctx_1024, 'g_xattn': g_xattn, 'g_ffn': g_ffn, 'L0_xattn_Wq': _L0_xattn_in['Wq'], 'L0_xattn_bq': _L0_xattn_in['bq'], 'L0_xattn_Wk': _L0_xattn_in['Wk'], 'L0_xattn_bk': _L0_xattn_in['bk'], 'L0_ffn_gate_w': _L0_ffn_in['gate_w'], 'L0_ffn_down_w': _L0_ffn_in['down_w'], 'L0_ffn_gate_norm_w': _L0_ffn_in['gate_norm_w'], 'L0_ffn_down_norm_w': _L0_ffn_in['down_norm_w'], 'L1_xattn_Wq': _L1_xattn_in['Wq'], 'L1_xattn_Wk': _L1_xattn_in['Wk'], 'L1_xattn_Wv': _L1_xattn_in['Wv'], 'L1_xattn_Wo': _L1_xattn_in['Wo'], 'L1_xattn_gq': _L1_xattn_in['gq'], 'L1_xattn_gk': _L1_xattn_in['gk'], 'L1_ffn_gate_w': _L1_ffn_in['gate_w'], 'L1_ffn_gu_w': _L1_ffn_in['gu_w'], 'L1_ffn_dp_w': _L1_ffn_in['dp_w'], 'L1_ffn_sh_gate_w': _L1_ffn_in['sh_gate_w'], 'L1_ffn_sh_up_w': _L1_ffn_in['sh_up_w'], 'L1_ffn_sh_down_w': _L1_ffn_in['sh_down_w'], 'L1_ffn_sh_gate1_w': _L1_ffn_in['sh_gate1_w']}

def reference(x, ctx_1024, g_xattn, g_ffn, L0_xattn_Wq, L0_xattn_bq, L0_xattn_Wk, L0_xattn_bk, L0_ffn_gate_w, L0_ffn_down_w, L0_ffn_gate_norm_w, L0_ffn_down_norm_w, L1_xattn_Wq, L1_xattn_Wk, L1_xattn_Wv, L1_xattn_Wo, L1_xattn_gq, L1_xattn_gk, L1_ffn_gate_w, L1_ffn_gu_w, L1_ffn_dp_w, L1_ffn_sh_gate_w, L1_ffn_sh_up_w, L1_ffn_sh_down_w, L1_ffn_sh_gate1_w):
    import jax
    import jax.numpy as jnp

    def _L0_xattn_ref(teacher_logits, teacher_features, Wq, bq, Wk, bk):
        import jax, jax.numpy as jnp
        import numpy as np
        query = jnp.einsum('bnc,dc->bnd', teacher_features, Wq) + bq
        key = jnp.einsum('bnc,dc->bnd', teacher_features, Wk) + bk
        energy = jnp.einsum('bnd,bmd->bnm', query, key)
        attention = jax.nn.softmax(energy, axis=-1)
        x_m = jnp.einsum('bln,bmn->blm', teacher_logits, attention)
        return x_m

    def _L0_ffn_ref(x, gate_w, down_w, gate_norm_w, down_norm_w):
        import jax, jax.numpy as jnp
        import numpy as np
        HIDDEN = 256
        INTER = 704
        EPS = 1e-05

        def rms_norm(x, g):
            var = jnp.mean(x * x, axis=-1, keepdims=True)
            return x * jax.lax.rsqrt(var + EPS) * g

        def activation_quant(x):
            scale = 127.0 / jnp.clip(jnp.max(jnp.abs(x), axis=-1, keepdims=True), 1e-05, None)
            return jnp.clip(jnp.round(x * scale), -128, 127) / scale

        def weight_quant(w):
            scale = 1.0 / jnp.clip(jnp.mean(jnp.abs(w)), 1e-05, None)
            return jnp.clip(jnp.round(w * scale), -1, 1) / scale

        def ste(x, q):
            return x + jax.lax.stop_gradient(q - x)

        def bit_linear(x, w, g):
            xn = rms_norm(x, g)
            xq = ste(xn, activation_quant(xn))
            wq = ste(w, weight_quant(w))
            return xq @ wq.T
        y = bit_linear(x, gate_w, gate_norm_w)
        gate, up = jnp.split(y, 2, axis=-1)
        h = gate * jax.nn.sigmoid(gate) * up
        return bit_linear(h, down_w, down_norm_w)

    def _L1_xattn_ref(hidden_states, encoder_hidden_states, Wq, Wk, Wv, Wo, gq, gk):
        import jax, jax.numpy as jnp
        import numpy as np
        EPS = 1e-05

        def rmsnorm(x, g, eps=EPS):
            var = jnp.mean(jnp.square(x), axis=-1, keepdims=True)
            return x * jax.lax.rsqrt(var + eps) * g
        B, Sq, _ = hidden_states.shape
        Skv = encoder_hidden_states.shape[1]
        D = gq.shape[0]
        H = Wq.shape[1] // D
        scale = 1.0 / np.sqrt(D)
        q = (hidden_states @ Wq).reshape(B, Sq, H, D)
        k = (encoder_hidden_states @ Wk).reshape(B, Skv, H, D)
        v = (encoder_hidden_states @ Wv).reshape(B, Skv, H, D)
        q = rmsnorm(q, gq)
        k = rmsnorm(k, gk)
        scores = jnp.einsum('bqhd,bkhd->bhqk', q, k) * scale
        attn = jax.nn.softmax(scores, axis=-1)
        out = jnp.einsum('bhqk,bkhd->bqhd', attn, v)
        out = out.reshape(B, Sq, H * D)
        return out @ Wo

    def _L1_ffn_ref(h, gate_w, gu_w, dp_w, sh_gate_w, sh_up_w, sh_down_w, sh_gate1_w):
        import jax, jax.numpy as jnp
        import numpy as np
        H = 256
        E = 64
        I = 64
        SI = 64
        TOP_K = 8
        B, T = (2, 64)
        Bb, Tt, Hh = h.shape
        x = h.reshape(Bb * Tt, Hh)
        N = x.shape[0]
        logits = x @ gate_w.T
        topv, topi = jax.lax.top_k(logits, TOP_K)
        rw = jax.nn.softmax(topv.astype(jnp.float32), axis=-1).astype(x.dtype)
        W = jnp.zeros((N, E), x.dtype).at[jnp.arange(N)[:, None], topi].set(rw)
        gu = jnp.einsum('nh,eih->nei', x, gu_w)
        gate, up = (gu[..., :I], gu[..., I:])
        inter = jax.nn.silu(gate) * up
        inter_w = inter * W[:, :, None]
        out = jnp.einsum('nei,ehi->nh', inter_w, dp_w)
        sh_inter = jax.nn.silu(x @ sh_gate_w.T) * (x @ sh_up_w.T)
        sh_out = sh_inter @ sh_down_w.T
        sh_g = jax.nn.sigmoid(x @ sh_gate1_w.T)
        out = out + sh_g * sh_out
        return out.reshape(Bb, Tt, Hh)
    x = x + jnp.tanh(g_xattn[0]) * _L0_xattn_ref(_layernorm(x, axis=-1), ctx_1024, L0_xattn_Wq, L0_xattn_bq, L0_xattn_Wk, L0_xattn_bk)
    x = x + jnp.tanh(g_ffn[0]) * _L0_ffn_ref(_layernorm(x, axis=-1), L0_ffn_gate_w, L0_ffn_down_w, L0_ffn_gate_norm_w, L0_ffn_down_norm_w)
    x = x + jnp.tanh(g_xattn[1]) * _L1_xattn_ref(_layernorm(x, axis=-1), ctx_1024, L1_xattn_Wq, L1_xattn_Wk, L1_xattn_Wv, L1_xattn_Wo, L1_xattn_gq, L1_xattn_gk)
    x = x + jnp.tanh(g_ffn[1]) * _L1_ffn_ref(_layernorm(x, axis=-1), L1_ffn_gate_w, L1_ffn_gu_w, L1_ffn_dp_w, L1_ffn_sh_gate_w, L1_ffn_sh_up_w, L1_ffn_sh_down_w, L1_ffn_sh_gate1_w)
    return x

_drawn_inputs = setup_inputs


def setup_inputs(seed=0):
    import zlib

    import numpy as np

    out = dict(_drawn_inputs(seed))
    spreads = {'g_ffn': (-1.0, 0.6),
     'L0_xattn_bq': (0.0, 0.1),
     'L0_xattn_bk': (0.0, 0.8),
     'L0_ffn_gate_norm_w': (1.0, 0.2),
     'L0_ffn_down_norm_w': (1.0, 0.2),
     'L1_xattn_gq': (1.0, 0.592),
     'L1_xattn_gk': (1.0, 0.6)}
    factors = {'L1_ffn_gate_w': 8.0,
     'L1_ffn_gu_w': 8.0,
     'L1_ffn_dp_w': 8.0,
     'L1_ffn_sh_gate_w': 8.0,
     'L1_ffn_sh_up_w': 8.0,
     'L1_ffn_sh_down_w': 8.0,
     'L1_ffn_sh_gate1_w': 8.0}
    for name, (base, spread) in spreads.items():
        noise = np.random.default_rng([zlib.crc32(name.encode()), seed]).standard_normal(out[name].shape)
        drawn = base * np.exp(spread * noise) if base else spread * noise
        out[name] = jnp.asarray(drawn.astype(out[name].dtype))
    for name, factor in factors.items():
        out[name] = (out[name] * factor).astype(out[name].dtype)
    return out
```

```python
from contextlib import ExitStack

import concourse.bass as bass
from concourse import mybir

F32 = mybir.dt.float32
F32R = mybir.dt.float32r
BF16 = mybir.dt.bfloat16
ALU = mybir.AluOpType
ACT = mybir.ActivationFunctionType
AX = mybir.AxisListType

P = 128
BATCH, SEQ, HID, CDIM = 4, 256, 256, 128
TOK = BATCH * SEQ
TILES = TOK // P
KH = HID // P
INTER = 704
HALF = INTER // 2
KI = 6
TAIL = INTER - 5 * P
HEADS, D = 16, 128
PAIRS = HEADS // 2
GROUPS = PAIRS * BATCH
EXPERTS, TOPK, EI = 64, 8, 64
EPAIRS = EXPERTS // 2
LOGC = 66
EPS = 1e-5
MAGIC = 12582912.0
LOWEST = -3.0e38


def flamingo_kernel(nc, x_tok, ctx_tok, ctxT, qk0, bias0, gains, gate_wT, down_wT, down_tail,
                    norm_g1, norm_g2, gqk, head_qk, head_vo, router_w, expert_w, shared_w,
                    shared_down, outT):
    with ExitStack() as ctx:
        def sb(name, shape, dt=F32):
            return ctx.enter_context(nc.sbuf_tensor(name, shape, dt))

        def sem(name):
            return ctx.enter_context(nc.semaphore(name))

        bank = [ctx.enter_context(nc.psum_tensor(f"bank{i}", [P, 512], F32)) for i in range(8)]

        ident = sb("ident", [P, P])
        ident_r = sb("ident_r", [P, P], F32R)
        ident_b = sb("ident_b", [P, P], BF16)
        ones = sb("ones", [P, P])
        ones_r = sb("ones_r", [P, EI], F32R)
        minus_half = sb("minus_half", [P, 8])
        expert_rows = sb("expert_rows", [P, EXPERTS])
        x = sb("x", [P, TILES, HID])
        ctxT_raw = sb("ctxT_raw", [P, TOK])
        ctxT_hi = sb("ctxT_hi", [P, TOK], F32R)
        ctxT_lo = sb("ctxT_lo", [P, TOK], F32R)
        ctx_raw = sb("ctx_raw", [P, TILES, CDIM])
        ctx_hi = sb("ctx_hi", [P, TILES, CDIM], F32R)
        ctx_lo = sb("ctx_lo", [P, TILES, CDIM], F32R)
        gains_raw = sb("gains_raw", [P, 4])
        tg = sb("tg", [P, 4])
        stats = sb("stats", [P, TILES, 6])
        mv = sb("mv", [P, TILES, 2])
        vare = sb("vare", [P, TILES])
        rstd = sb("rstd", [P, TILES])
        u = sb("u", [P, TILES, HID])
        xnT_hi = sb("xnT_hi", [P, KH, TOK], F32R)
        xnT_lo = sb("xnT_lo", [P, KH, TOK], F32R)
        xT = sb("xT", [P, KH, TOK])

        l_x, l_ctxT, l_ctx, l_qk0, l_bias, l_gains = (sem(n) for n in (
            "l_x", "l_ctxT", "l_ctx", "l_qk0", "l_bias", "l_gains"))
        l_gate, l_down, l_tail, l_g1, l_g2, l_gqk = (sem(n) for n in (
            "l_gate", "l_down", "l_tail", "l_g1", "l_g2", "l_gqk"))
        l_router, l_shared, l_shdown = sem("l_router"), sem("l_shared"), sem("l_shdown")
        l_hqk, l_hvo, l_out = sem("l_hqk"), sem("l_hvo"), sem("l_out")
        l_exp = [sem("l_exp0"), sem("l_exp1")]
        pool_const = sem("pool_const")
        v_const, v_ctx = sem("v_const"), sem("v_ctx")
        a_ctx, a_tg = sem("a_ctx"), sem("a_tg")
        v_link = sem("v_link")
        link_n = [0]

        def link(dve, ins):
            link_n[0] += 1
            ins.then_inc(v_link, 1)
            dve.wait_ge(v_link, link_n[0])

        v_pow, g_pow = sem("v_pow"), sem("g_pow")
        pow_n = [0]
        v_u, t_u, a_u, c_u = sem("v_u"), sem("t_u"), sem("a_u"), sem("c_u")

        wqk0 = sb("wqk0", [P, 2, D])
        bqk = sb("bqk", [P, 2])
        qkA = sb("qkA", [P, 2, TOK])
        attA = sb("attA", [P, 2, 2, SEQ])
        attT = sb("attT", [P, 2, 2, SEQ])
        nmA = sb("nmA", [P, BATCH, 2])
        sumA = sb("sumA", [P, BATCH, 2])
        invA = sb("invA", [P, BATCH, 2])
        t_qkA, a_qkA, t_eA, v_mA, a_eA, v_nA, t_aA, a_aA, t_oA, v_xA = (sem(n) for n in (
            "t_qkA", "a_qkA", "t_eA", "v_mA", "a_eA", "v_nA", "t_aA", "a_aA", "t_oA", "v_xA"))

        g1 = sb("g1", [P, HID])
        g2 = sb("g2", [P, INTER])
        absum = sb("absum", [P, 3])
        wsc = sb("wsc", [P, 2])
        wsi = sb("wsi", [P, 2])
        tinyB = sb("tinyB", [P, 8, TILES])
        sumh = sb("sumh", [P, TILES])
        amax2 = sb("amax2", [P, TILES])
        gqk_raw = sb("gqk_raw", [P, 2])
        gk = sb("gk", [P, 1])
        wqk_raw = sb("wqk_raw", [P, 768])
        wqk_hi = sb("wqk_hi", [P, 768], F32R)
        wqk_lo = sb("wqk_lo", [P, 768], F32R)
        wvo_raw = sb("wvo_raw", [P, 768])
        ssq8 = sb("ssq8", [P, 8])
        rqk = sb("rqk", [P, BATCH, 8])
        rk_hi, rk_lo = sb("rk_hi", [P, 4], F32R), sb("rk_lo", [P, 4], F32R)
        rowmax = sb("rowmax", [P, 2, 4])
        shift = sb("shift", [P, 2, 4])
        minus_rq = sb("minus_rq", [P, 2, 4])
        rowsum = sb("rowsum", [P, 2, 4])
        rowinv = sb("rowinv", [P, 2, 4])
        e_raw = sb("e_raw", [P, 2, 768])
        r_raw = sb("r_raw", [P, KH, LOGC])
        s_raw = sb("s_raw", [P, 2, KH, EI])
        sdn_raw = sb("sdn_raw", [EI, HID])
        bctx = ExitStack()
        gate_raw = bctx.enter_context(nc.sbuf_tensor("gate_raw", [P, KH, 2 * INTER], F32))
        down_raw = bctx.enter_context(nc.sbuf_tensor("down_raw", [P, KI, HID], F32))
        gate_t = bctx.enter_context(nc.sbuf_tensor("gate_t", [P, KH, 2 * INTER], BF16))
        down_t = bctx.enter_context(nc.sbuf_tensor("down_t", [P, KI, HID], BF16))
        w1 = bctx.enter_context(nc.sbuf_tensor("w1", [P, TILES, HID], F32))
        q1 = bctx.enter_context(nc.sbuf_tensor("q1", [P, TILES, HID], BF16))
        qT = bctx.enter_context(nc.sbuf_tensor("qT", [P, 2, KH, P], BF16))
        silu_g = bctx.enter_context(nc.sbuf_tensor("silu_g", [P, 2, INTER], F32))
        h_raw = bctx.enter_context(nc.sbuf_tensor("h_raw", [P, 2, INTER], F32))
        w2 = bctx.enter_context(nc.sbuf_tensor("w2", [P, TILES, INTER], F32))
        q2 = bctx.enter_context(nc.sbuf_tensor("q2", [P, 2, INTER], BF16))
        hT = bctx.enter_context(nc.sbuf_tensor("hT", [P, 2, KI, P], BF16))
        junk = bctx.enter_context(nc.sbuf_tensor("junk", [P, 2 * KH * INTER], F32))
        bctx.close()
        a_abs, t_abs, v_gw, v_dw = sem("a_abs"), sem("t_abs"), sem("v_gw"), sem("v_dw")
        v_q1, t_q1, a_q1, t_y1, a_s1, v_h1, a_h1 = (sem(n) for n in (
            "v_q1", "t_q1", "a_q1", "t_y1", "a_s1", "v_h1", "a_h1"))
        v_r2, v_q2, t_q2, a_q2, t_y2, v_xB = (sem(n) for n in ("v_r2", "v_q2", "t_q2", "a_q2", "t_y2", "v_xB"))

        cctx = ExitStack()

        def sc(name, shape, dt=F32):
            return cctx.enter_context(nc.sbuf_tensor(name, shape, dt))

        qh, ql = sc("qh", [P, 2, BATCH, SEQ], F32R), sc("ql", [P, 2, BATCH, SEQ], F32R)
        kh, kl = sc("kh", [P, 2, BATCH, SEQ], F32R), sc("kl", [P, 2, BATCH, SEQ], F32R)
        rk_row = sc("rk_row", [P, 2, BATCH, SEQ])
        squares = sc("squares", [P, 2, 2, SEQ])
        att = sc("att", [P, 2, 2, 2, SEQ])
        attT_hi = sc("attT_hi", [P, 2, 2, SEQ], F32R)
        attT_lo = sc("attT_lo", [P, 2, 2, SEQ], F32R)
        o_hi, o_lo = sc("o_hi", [P, 2, SEQ], F32R), sc("o_lo", [P, 2, SEQ], F32R)
        m_hi, m_lo = sc("m_hi", [P, 2, HID], F32R), sc("m_lo", [P, 2, HID], F32R)
        cctx.close()

        t_S, t_T, t_O, t_Y, t_Q, t_K, t_ssq, t_RK, t_M = (sem(n) for n in (
            "t_S", "t_T", "t_O", "t_Y", "t_Q", "t_K", "t_ssq", "t_RK", "t_M"))
        a_exp, a_Thi, a_sqQ, a_hiQ, a_sqK, a_hiK, a_RK, a_Mhi, a_Whi = (sem(n) for n in (
            "a_exp", "a_Thi", "a_sqQ", "a_hiQ", "a_sqK", "a_hiK", "a_RK", "a_Mhi", "a_Whi"))
        v_mm, v_nb, v_Tlo, v_Y, v_l, v_P, v_Qlo, v_Klo, v_r8, v_rh, v_rs, v_Ohi, v_Olo, v_Mlo, v_Wlo = (
            sem(n) for n in ("v_mm", "v_nb", "v_Tlo", "v_Y", "v_l", "v_P", "v_Qlo", "v_Klo", "v_r8",
                             "v_rh", "v_rs", "v_Ohi", "v_Olo", "v_Mlo", "v_Wlo"))
        g_r8 = sem("g_r8")
        v_gk, v_rq = sem("v_gk"), sem("v_rq")

        dctx = ExitStack()

        def sd(name, shape, dt=F32):
            return dctx.enter_context(nc.sbuf_tensor(name, shape, dt))

        e_hi, e_lo = sd("e_hi", [P, 2, 768], F32R), sd("e_lo", [P, 2, 768], F32R)
        selb = sd("selb", [P, 2, P], F32R)
        gate_s = sd("gate_s", [P, 2, 512])
        prod = sd("prod", [P, 2, 512])
        inter = sd("inter", [P, 2, 512])
        inter_hi, inter_lo = sd("inter_hi", [P, 2, 512], F32R), sd("inter_lo", [P, 2, 512], F32R)
        final = sd("final", [P, 2, 2, 512])
        r_hi, r_lo = sd("r_hi", [P, KH, LOGC], F32R), sd("r_lo", [P, KH, LOGC], F32R)
        s_hi, s_lo = sd("s_hi", [P, 2, KH, EI], F32R), sd("s_lo", [P, 2, KH, EI], F32R)
        sdn_hi, sdn_lo = sd("sdn_hi", [EI, HID], F32R), sd("sdn_lo", [EI, HID], F32R)
        logits = sd("logits", [P, TILES, LOGC])
        top8 = sd("top8", [P, TILES, TOPK])
        struck = sd("struck", [P, TILES, EXPERTS])
        chosen = sd("chosen", [P, TILES, EXPERTS])
        shifted = sd("shifted", [P, TILES, EXPERTS])
        wexp = sd("wexp", [P, TILES, EXPERTS])
        wcat = sd("wcat", [P, TILES, P])
        wsum = sd("wsum", [P, TILES])
        winv = sd("winv", [P, TILES])
        shg = sd("shg", [P, TILES])
        shcat = sd("shcat", [P, TILES, 2])
        wT = sd("wT", [P, TOK], F32R)
        shT = sd("shT", [2, TOK], F32R)
        dctx.close()
        t_log, v_log, v_shift, a_wexp, v_wcat, t_wT, v_wT, t_xT, a_xT, v_rw, a_rw = (sem(n) for n in (
            "t_log", "v_log", "v_shift", "a_wexp", "v_wcat", "t_wT", "v_wT", "t_xT", "a_xT", "v_rw", "a_rw"))
        t_G, t_U, t_W, t_D, a_silu, a_Ihi, a_Ehi, v_mul1, v_mul2, v_Ilo, v_Elo, v_sel, v_out = (sem(n) for n in (
            "t_G", "t_U", "t_W", "t_D", "a_silu", "a_Ihi", "a_Ehi", "v_mul1", "v_mul2", "v_Ilo", "v_Elo",
            "v_sel", "v_out"))

        GB, UB, WB = 0, 1, 2
        ACC = [[3, 4], [5, 6]]
        SBK, TBK, OBK, YBK, QBK, RBK = [0, 1], [2, 3], 4, 5, 6, 7

        def f(ap):
            return ap.bitcast(F32)

        def bank4(i):
            return bank[i][:, :].rearrange("p (a n) -> p a n", a=2)

        block = ctx.enter_context(nc.Block())

        def split_mm(pe, out, l_hi, l_lo, r_hi_, r_lo_, start, stop):
            pe.matmul(out, l_hi, r_hi_, start=start, stop=False, skip_group_check=True)
            pe.matmul(out, l_hi, r_lo_, start=False, stop=False, skip_group_check=True)
            return pe.matmul(out, l_lo, r_hi_, start=False, stop=stop, skip_group_check=True)

        @block.sync
        def _(sp):
            sp.dma_start(ctxT_raw[:, :], ctxT).then_inc(l_ctxT, 16)
            sp.dma_start(wqk0[:, :, :], qk0).then_inc(l_qk0, 16)
            sp.dma_start(x[:, 0:4, :], x_tok[:, 0:4, :]).then_inc(l_x, 16)
            sp.dma_start(x[:, 4:8, :], x_tok[:, 4:8, :]).then_inc(l_x, 16)
            sp.dma_start(ctx_raw[:, :, :], ctx_tok).then_inc(l_ctx, 16)
            sp.dma_start(gate_raw[:, :, :], gate_wT).then_inc(l_gate, 16)
            sp.dma_start(down_raw[:, 0:5, :], down_wT).then_inc(l_down, 16)
            sp.dma_start(down_raw[0:TAIL, 5, :], down_tail).then_inc(l_tail, 16)
            sp.dma_start(g1[:, :], norm_g1.partition_broadcast(P)).then_inc(l_g1, 16)
            sp.dma_start(g2[:, :], norm_g2.partition_broadcast(P)).then_inc(l_g2, 16)
            sp.dma_start(gqk_raw[:, :], gqk).then_inc(l_gqk, 16)
            sp.dma_start(wqk_raw[:, :], head_qk[0]).then_inc(l_hqk, 16)
            sp.dma_start(wvo_raw[:, :], head_vo[0]).then_inc(l_hvo, 16)
            sp.dma_start(r_raw[:, :, :], router_w).then_inc(l_router, 16)
            sp.dma_start(e_raw[:, 0, :], expert_w[0]).then_inc(l_exp[0], 16)
            sp.dma_start(e_raw[:, 1, :], expert_w[1]).then_inc(l_exp[1], 16)
            sp.dma_start(s_raw[:, :, :, :], shared_w).then_inc(l_shared, 16)
            sp.dma_start(sdn_raw[:, :], shared_down).then_inc(l_shdown, 16)
            with sp.Fori(1, PAIRS) as p:
                sp.wait_ge(v_Wlo, p)
                sp.dma_start(wqk_raw[:, :], head_qk[bass.ds(p, 1)].rearrange("a p n -> (a p) n")).then_inc(l_hqk, 16)
                sp.wait_ge(t_M, p)
                sp.dma_start(wvo_raw[:, :], head_vo[bass.ds(p, 1)].rearrange("a p n -> (a p) n")).then_inc(l_hvo, 16)
            with sp.Fori(1, EPAIRS // 2) as j:
                for par in range(2):
                    sp.wait_ge(v_Elo, j * 2 + par - 1)
                    sp.dma_start(e_raw[:, par, :],
                                 expert_w[bass.ds(j * 2 + par, 1)].rearrange("a p n -> (a p) n")).then_inc(l_exp[par], 16)
            for t in range(2):
                for hb in range(2):
                    sp.wait_ge(v_out, 2 * t + hb + 1)
                    sp.dma_start(outT[hb, :, t * 512:(t + 1) * 512], final[:, hb, t, :]).then_inc(l_out, 16)
            sp.wait_ge(l_out, 64)

        @block.gpsimd
        def _(pool):
            pool.memset(ident[:, :], 0.0).then_inc(pool_const, 1)
            pool.memset(ones[:, :], 1.0).then_inc(pool_const, 1)
            pool.memset(minus_half[:, :], -0.5).then_inc(pool_const, 1)
            pool.memset(expert_rows[:, :], 0.0).then_inc(pool_const, 1)
            pool.wait_ge(pool_const, 4)
            pool.affine_select(out=ident[:, :], in_=ident[:, :], compare_op=ALU.not_equal, fill=1.0, base=0,
                               pattern=[[-1, P]], channel_multiplier=1).then_inc(pool_const, 1)
            pool.affine_select(out=expert_rows[:, :], in_=expert_rows[:, :], compare_op=ALU.not_equal, fill=1.0,
                               base=0, pattern=[[-1, EXPERTS]], channel_multiplier=1).then_inc(pool_const, 1)
            pool.wait_ge(pool_const, 6)
            pool.affine_select(out=expert_rows[:, :], in_=expert_rows[:, :], compare_op=ALU.not_equal, fill=1.0,
                               base=-EXPERTS, pattern=[[-1, EXPERTS]], channel_multiplier=1).then_inc(pool_const, 1)
            pool.dma_start(bqk[:, :], bias0).then_inc(l_bias, 16)
            pool.dma_start(gains_raw[:, :], gains).then_inc(l_gains, 16)

            def power(k, src, dst, n):
                pool.wait_ge(v_pow, k + 1)
                pool.tensor_tensor(dst, src, minus_half[:, 0:n], ALU.pow).then_inc(g_pow, 1)

            power(0, vare[:, :], rstd[:, :], TILES)
            power(1, vare[:, :], rstd[:, :], TILES)
            power(2, tinyB[:, 0, :], tinyB[:, 1, :], TILES)
            power(3, tinyB[:, 5, :], tinyB[:, 6, :], TILES)
            power(4, vare[:, :], rstd[:, :], TILES)

            def rms(b, n, first):
                if not first:
                    pool.wait_ge(a_exp, n * 4 - 12)
                pool.wait_ge(v_r8, n + 1)
                pool.tensor_tensor(rqk[:, b, :], ssq8[:, :], minus_half[:, :], ALU.pow).then_inc(g_r8, 1)

            for n in range(4):
                rms(n, n, True)
            with pool.Fori(1, PAIRS) as p:
                for b in range(BATCH):
                    rms(b, p * 4 + b, False)
            power(5, vare[:, :], rstd[:, :], TILES)

        @block.tensor
        def _(pe):
            def transpose_rows(first, src, ready, free, count):
                for j in range(BATCH):
                    pe.wait_ge(ready, first * 8 + 2 * j + 2)
                    if first * 4 + j >= 2:
                        pe.wait_ge(free, first * 4 + j - 1)
                    for k in range(KH):
                        for t in range(2):
                            mm = pe.transpose(bank4(6 + j % 2)[:, k, t * P:(t + 1) * P],
                                              src[:, 2 * j + t, k * P:(k + 1) * P], ident[:, :])
                    mm.then_inc(count, 1)

            pe.wait_ge(l_ctxT, 16)
            pe.wait_ge(l_qk0, 16)
            for i in range(2):
                for h in range(2):
                    pe.matmul(bank[2 * i + h][:, :], wqk0[:, i, :], ctxT_raw[:, h * 512:(h + 1) * 512],
                              start=True, stop=True).then_inc(t_qkA, 1)
            pe.wait_ge(pool_const, 7)
            transpose_rows(0, u, v_u, c_u, t_u)

            def energy(b):
                pe.wait_ge(a_qkA, 4)
                if b >= 2:
                    pe.wait_ge(v_mA, b - 1)
                    pe.wait_ge(a_eA, 2 * (b - 1))
                for m in range(2):
                    c = b * SEQ + m * P
                    mm = pe.matmul(bank4(b % 2)[:, m, :], qkA[:, 0, c:c + P], qkA[:, 1, b * SEQ:(b + 1) * SEQ],
                                   start=True, stop=True)
                mm.then_inc(t_eA, 1)

            def turn_att(b):
                pe.wait_ge(v_nA, b + 1)
                if b >= 2:
                    pe.wait_ge(a_aA, b - 1)
                for j in range(2):
                    for m in range(2):
                        mm = pe.transpose(bank4(2 + b % 2)[:, j, m * P:(m + 1) * P],
                                          attA[:, b % 2, m, j * P:(j + 1) * P], ident[:, :])
                mm.then_inc(t_aA, 1)

            def mix(b):
                pe.wait_ge(a_aA, b + 1)
                pe.wait_ge(c_u, b + 1)
                if b >= 2:
                    pe.wait_ge(v_xA, b - 1)
                for t in range(2):
                    for j in range(2):
                        c = (2 * b + t) * P
                        mm = pe.matmul(bank4(4 + b % 2)[:, t, :], xT[:, j, c:c + P], attT[:, b % 2, j, :],
                                       start=j == 0, stop=j == 1)
                mm.then_inc(t_oA, 1)

            energy(0)
            energy(1)
            for b in range(BATCH):
                turn_att(b)
                mix(b)
                if b + 2 < BATCH:
                    energy(b + 2)

            pe.wait_ge(a_abs, 3)
            pe.wait_ge(v_xA, 4)
            pe.matmul(bank[7][:, 0:2], ones[:, :], absum[:, 0:2], start=True, stop=False, skip_group_check=True)
            pe.matmul(bank[7][:, 1:2], ones[0:TAIL, :], absum[0:TAIL, 2:3], start=False, stop=True,
                      skip_group_check=True).then_inc(t_abs, 1)

            def turn_q1(i):
                pe.wait_ge(v_q1, i + 1)
                if i >= 2:
                    pe.wait_ge(a_q1, i - 1)
                bk = bank[4 + i % 2][:, :].bitcast(BF16)
                for k in range(KH):
                    mm = pe.transpose(bk[:, k * P:(k + 1) * P], q1[:, i, k * P:(k + 1) * P], ident_b[:, :])
                mm.then_inc(t_q1, 1)

            def gate_up(i):
                pe.wait_ge(a_q1, i + 1)
                pe.wait_ge(v_gw, 1)
                if i >= 1:
                    pe.wait_ge(a_s1, i)
                for c in range(4):
                    if c == 2 and i >= 1:
                        pe.wait_ge(v_h1, 2 * i)
                    for k in range(KH):
                        mm = pe.matmul(bank[c][:, 0:HALF], qT[:, i % 2, k, :],
                                       gate_t[:, k, c * HALF:(c + 1) * HALF], start=k == 0, stop=k == KH - 1)
                mm.then_inc(t_y1, 1)

            pe.wait_ge(v_const, 3)
            turn_q1(0)
            for i in range(TILES):
                if i + 1 < TILES:
                    turn_q1(i + 1)
                gate_up(i)

            def turn_q2(i):
                pe.wait_ge(v_q2, i + 1)
                if i >= 2:
                    pe.wait_ge(a_q2, i - 1)
                bk = bank[6 + i % 2][:, :].bitcast(BF16)
                for k in range(KI):
                    n = P if k < 5 else TAIL
                    mm = pe.transpose(bk[0:n, k * P:(k + 1) * P], q2[:, i % 2, k * P:k * P + n], ident_b[:, :])
                mm.then_inc(t_q2, 1)

            def down(i):
                pe.wait_ge(a_q2, i + 1)
                pe.wait_ge(v_dw, 1)
                if i >= 2:
                    pe.wait_ge(v_xB, i - 1)
                for k in range(KI):
                    n = P if k < 5 else TAIL
                    mm = pe.matmul(bank[4 + i % 2][:, 0:HID], hT[0:n, i % 2, k, :], down_t[0:n, k, :],
                                   start=k == 0, stop=k == KI - 1)
                mm.then_inc(t_y2, 1)

            turn_q2(0)
            for i in range(TILES):
                if i + 1 < TILES:
                    turn_q2(i + 1)
                down(i)

            pe.wait_ge(v_xB, TILES)
            transpose_rows(1, u, v_u, c_u, t_u)
            pe.wait_ge(c_u, 8)
            pe.wait_ge(v_ctx, 2)

            def proj_q(b, n, w):
                pe.wait_ge(v_Wlo, w)
                if not (isinstance(n, int) and n == 0):
                    pe.wait_ge(v_Klo, n)
                for h in range(2):
                    for k in range(KH):
                        c = h * 256 + k * P
                        mm = split_mm(pe, bank4(QBK)[:, h, :], wqk_hi[:, c:c + P], wqk_lo[:, c:c + P],
                                      xnT_hi[:, k, b * SEQ:(b + 1) * SEQ], xnT_lo[:, k, b * SEQ:(b + 1) * SEQ],
                                      k == 0, k == KH - 1)
                mm.then_inc(t_Q, 1)

            def proj_k(b, n):
                pe.wait_ge(v_Qlo, n + 1)
                for h in range(2):
                    c = 512 + h * P
                    mm = split_mm(pe, bank4(QBK)[:, h, :], wqk_hi[:, c:c + P], wqk_lo[:, c:c + P],
                                  ctxT_hi[:, b * SEQ:(b + 1) * SEQ], ctxT_lo[:, b * SEQ:(b + 1) * SEQ], True, True)
                mm.then_inc(t_K, 1)

            def sum_squares(n, first=False):
                pe.wait_ge(a_sqK, n + 1)
                if not first:
                    pe.wait_ge(a_RK, n)
                for qk in range(2):
                    for h in range(2):
                        for t in range(2):
                            c = qk * 4 + h * 2 + t
                            mm = pe.matmul(bank[RBK][:, c:c + 1], squares[:, qk, h, t * P:(t + 1) * P],
                                           ones[:, 0:1], start=True, stop=True)
                mm.then_inc(t_ssq, 1)

            def spread_rk(n):
                pe.wait_ge(v_rs, n + 1)
                for h in range(2):
                    for t in range(2):
                        c = h * 2 + t
                        out = bank4(RBK)[:, h, t * P:(t + 1) * P]
                        pe.matmul(out, rk_hi[:, c:c + 1].broadcast_to([P, P]), ident_r[:, :], start=True,
                                  stop=False, skip_group_check=True)
                        mm = pe.matmul(out, rk_lo[:, c:c + 1].broadcast_to([P, P]), ident_r[:, :], start=False,
                                       stop=True, skip_group_check=True)
                mm.then_inc(t_RK, 1)

            def scores(b, g, first=False):
                pe.wait_ge(v_Qlo, g + 1)
                pe.wait_ge(v_Klo, g + 1)
                for h in range(2):
                    if not first:
                        pe.wait_ge(v_mm, g * 4 - 2 + 2 * h)
                    for t in range(2):
                        c = slice(t * P, (t + 1) * P)
                        mm = split_mm(pe, bank4(SBK[h])[:, t, :], qh[:, h, b, c], ql[:, h, b, c],
                                      kh[:, h, b, :], kl[:, h, b, :], True, True)
                    mm.then_inc(t_S, 1)

            def turn(b, g, first=False):
                pe.wait_ge(v_P, g * 4 + 4)
                for j in range(2):
                    if not first:
                        pe.wait_ge(v_Tlo, g * 2 - 1 + j)
                    for h in range(2):
                        for t in range(2):
                            mm = pe.transpose(bank4(TBK[j])[:, h, t * P:(t + 1) * P],
                                              att[:, b % 2, h, t, j * P:(j + 1) * P], ident[:, :])
                    mm.then_inc(t_T, 1)

            def values(b, g, first=False):
                pe.wait_ge(v_Tlo, g * 2 + 2)
                if not first:
                    pe.wait_ge(v_Olo, g)
                for j in range(2):
                    mm = split_mm(pe, bank[OBK][:, :], ctx_hi[:, 2 * b + j, :], ctx_lo[:, 2 * b + j, :],
                                  attT_hi[:, j, :, :].rearrange("p h n -> p (h n)"),
                                  attT_lo[:, j, :, :].rearrange("p h n -> p (h n)"), j == 0, j == 1)
                mm.then_inc(t_O, 1)

            def output(g, p_m, first=False):
                pe.wait_ge(v_Olo, g + 1)
                pe.wait_ge(v_Mlo, p_m)
                if not first:
                    pe.wait_ge(v_Y, g)
                for t in range(2):
                    for h in range(2):
                        c = slice(t * P, (t + 1) * P)
                        mm = split_mm(pe, bank4(YBK)[:, t, :], o_hi[:, h, c], o_lo[:, h, c],
                                      m_hi[:, h, :], m_lo[:, h, :], h == 0, h == 1)
                mm.then_inc(t_Y, 1)

            def fuse_vo(p, g, first=False):
                pe.wait_ge(l_hvo, p * 16 + 16)
                if not first:
                    pe.wait_ge(v_Y, g)
                for h in range(2):
                    mm = pe.matmul(bank4(YBK)[:, h, :], wvo_raw[:, h * P:(h + 1) * P],
                                   wvo_raw[:, 256 + h * 256:512 + h * 256], start=True, stop=True)
                mm.then_inc(t_M, 1)

            def pair(p, first=False, last=False):
                for b in range(BATCH):
                    g = p * 4 + b
                    n = g + 4
                    start = first and b == 0
                    if not (last and b == 3):
                        scores((b + 1) % 4, g + 1)
                    turn(b, g, start)
                    if not (last and b > 0):
                        sum_squares(n - 1)
                    if not start:
                        output(g - 1, p if b == 0 else p + 1, first and b == 1)
                    if not (last and b > 0):
                        spread_rk(n - 1)
                    if not last:
                        proj_q(b, n, p + 2)
                    values(b, g, start)
                    if b == 0:
                        fuse_vo(p, g, first)
                    if not last:
                        proj_k(b, n)

            for n in range(4):
                if n:
                    sum_squares(n - 1, n == 1)
                    spread_rk(n - 1)
                proj_q(n, n, 1)
                proj_k(n, n)
            scores(0, 0, True)
            pair(0, first=True)
            with pe.Fori(1, PAIRS - 1) as p:
                pair(p)
            pair(PAIRS - 1, last=True)
            output(GROUPS - 1, PAIRS)

            transpose_rows(2, u, v_u, c_u, t_u)
            for j in range(BATCH):
                if j >= 2:
                    pe.wait_ge(a_xT, j - 1)
                else:
                    pe.wait_ge(v_Y, GROUPS)
                for k in range(KH):
                    for t in range(2):
                        mm = pe.transpose(bank4(4 + j % 2)[:, k, t * P:(t + 1) * P],
                                          x[:, 2 * j + t, k * P:(k + 1) * P], ident[:, :])
                mm.then_inc(t_xT, 1)
            pe.wait_ge(v_rw, 1)
            pe.wait_ge(c_u, 12)
            for i in range(TILES):
                for k in range(KH):
                    mm = split_mm(pe, bank[2 + i // 4][:, (i % 4) * LOGC:(i % 4 + 1) * LOGC],
                                  xnT_hi[:, k, i * P:(i + 1) * P], xnT_lo[:, k, i * P:(i + 1) * P],
                                  r_hi[:, k, :], r_lo[:, k, :], k == 0, k == KH - 1)
            mm.then_inc(t_log, 1)

            def gates(par, e, t, s, bk, part, first=False):
                if t == 0:
                    pe.wait_ge(v_Elo, e + 1)
                if not first:
                    pe.wait_ge(a_silu if part == 0 else v_mul1, s)
                for k in range(KH):
                    c = part * 256 + k * P
                    mm = split_mm(pe, bank[bk][:, :], e_hi[:, par, c:c + P], e_lo[:, par, c:c + P],
                                  xnT_hi[:, k, t * 512:(t + 1) * 512], xnT_lo[:, k, t * 512:(t + 1) * 512],
                                  k == 0, k == KH - 1)
                mm.then_inc(t_G if part == 0 else t_U, 1)

            def spread_w(par, e, t, s, first=False):
                pe.wait_ge(v_sel, e + 1)
                if not first:
                    pe.wait_ge(v_mul2, s)
                pe.matmul(bank[WB][:, :], selb[:, par, :], wT[:, t * 512:(t + 1) * 512],
                          start=True, stop=True).then_inc(t_W, 1)

            def experts_down(par, t, s, start=False):
                pe.wait_ge(v_Ilo, s + 1)
                for hb in range(2):
                    c = 512 + hb * P
                    mm = split_mm(pe, bank[ACC[hb][t]][:, :], e_hi[:, par, c:c + P], e_lo[:, par, c:c + P],
                                  inter_hi[:, t, :], inter_lo[:, t, :], start, False)
                mm.then_inc(t_D, 1)

            def turn_weights():
                pe.wait_ge(v_wcat, 1)
                for src, n, at in ((wcat, P, 3), (shcat, 2, 5)):
                    for i in range(TILES):
                        mm = pe.transpose(bank[at + i // 4][0:n, (i % 4) * P:(i % 4 + 1) * P], src[:, i, :],
                                          ident[:, :])
                        if i % 4 == 3:
                            mm.then_inc(t_wT, 1)

            def two_pairs(j, first=False):
                for par in range(2):
                    for t in range(2):
                        e = j * 2 + par
                        s = j * 4 + par * 2 + t
                        start = first and par == 0 and t == 0
                        gates(par, e, t, s, GB, 0, start)
                        gates(par, e, t, s, UB, 1, start)
                        if start:
                            turn_weights()
                            pe.wait_ge(v_wT, 2)
                        spread_w(par, e, t, s, start)
                        if not start:
                            pt = (par * 2 + t - 1) % 4
                            experts_down(pt // 2, pt % 2, s - 1, first and par * 2 + t <= 2)

            two_pairs(0, True)
            with pe.Fori(1, EPAIRS // 2) as j:
                two_pairs(j)
            pe.wait_ge(a_rw, 3)
            pe.wait_ge(v_rw, 3)
            for t in range(2):
                s = 2 * EPAIRS + t
                for part, bk, free, done in ((0, GB, a_silu, t_G), (1, UB, v_mul1, t_U)):
                    pe.wait_ge(free, s)
                    for k in range(KH):
                        mm = split_mm(pe, bank[bk][0:EI, :], s_hi[:, part, k, :], s_lo[:, part, k, :],
                                      xnT_hi[:, k, t * 512:(t + 1) * 512], xnT_lo[:, k, t * 512:(t + 1) * 512],
                                      k == 0, k == KH - 1)
                    mm.then_inc(done, 1)
                pe.wait_ge(v_mul2, s)
                pe.matmul(bank[WB][0:EI, :], ones_r[0:2, :], shT[:, t * 512:(t + 1) * 512], start=True,
                          stop=True).then_inc(t_W, 1)
                if t == 0:
                    experts_down(1, 1, s - 1)
            for t in range(2):
                pe.wait_ge(v_Ilo, 2 * EPAIRS + t + 1)
                for hb in range(2):
                    mm = split_mm(pe, bank[ACC[hb][t]][:, :], sdn_hi[:, hb * P:(hb + 1) * P],
                                  sdn_lo[:, hb * P:(hb + 1) * P], inter_hi[0:EI, t, :], inter_lo[0:EI, t, :],
                                  False, True)
                    mm.then_inc(t_D, 1)

        @block.scalar
        def _(act):
            def copy_rows(first, lo):
                for j in range(BATCH):
                    act.wait_ge(t_u, first * 4 + j + 1)
                    dst = xnT_hi if lo else xT
                    act.activation(dst[:, :, j * 256:(j + 1) * 256], bank4(6 + j % 2), ACT.Copy).then_inc(
                        a_u if lo else c_u, 1)

            act.wait_ge(l_gains, 16)
            act.activation(tg[:, :], gains_raw[:, :], ACT.Tanh).then_inc(a_tg, 1)
            act.wait_ge(l_bias, 16)
            for i in range(2):
                for h in range(2):
                    act.wait_ge(t_qkA, 2 * i + h + 1)
                    act.activation(qkA[:, i, h * 512:(h + 1) * 512], bank[2 * i + h][:, :], ACT.Identity,
                                   bias=bqk[:, i:i + 1]).then_inc(a_qkA, 1)
            copy_rows(0, False)

            def exp_A(b):
                act.wait_ge(v_mA, b + 1)
                if b >= 2:
                    act.wait_ge(t_aA, b - 1)
                for m in range(2):
                    act.activation(attA[:, b % 2, m, :], bank4(b % 2)[:, m, :], ACT.Exp, bias=nmA[:, b, m:m + 1],
                                   accum_out=sumA[:, b, m:m + 1]).then_inc(a_eA, 1)

            exp_A(0)
            exp_A(1)
            for b in range(BATCH):
                act.wait_ge(t_aA, b + 1)
                if b >= 2:
                    act.wait_ge(t_oA, b - 1)
                act.activation(attT[:, b % 2, :, :], bank4(2 + b % 2), ACT.Copy).then_inc(a_aA, 1)
                if b + 2 < BATCH:
                    exp_A(b + 2)
            act.wait_ge(l_gate, 16)
            act.activation(junk[:, :], gate_raw[:, :, :].rearrange("p k n -> p (k n)"), ACT.Abs,
                           accum_out=absum[:, 0:1]).then_inc(a_abs, 1)
            act.wait_ge(l_down, 16)
            act.wait_ge(a_abs, 1)
            act.activation(junk[:, 0:5 * HID], down_raw[:, 0:5, :].rearrange("p k n -> p (k n)"), ACT.Abs,
                           accum_out=absum[:, 1:2]).then_inc(a_abs, 1)
            act.wait_ge(l_tail, 16)
            act.wait_ge(a_abs, 2)
            act.activation(junk[0:TAIL, 0:HID], down_raw[0:TAIL, 5, :], ACT.Abs,
                           accum_out=absum[0:TAIL, 2:3]).then_inc(a_abs, 1)
            act.wait_ge(l_ctxT, 16)
            act.activation(ctxT_hi[:, :], ctxT_raw[:, :], ACT.Copy).then_inc(a_ctx, 1)
            act.wait_ge(l_ctx, 16)
            act.activation(ctx_hi[:, :, :], ctx_raw[:, :, :], ACT.Copy).then_inc(a_ctx, 1)

            def copy_q1(i):
                act.wait_ge(t_q1, i + 1)
                if i >= 2:
                    act.wait_ge(t_y1, i - 1)
                act.activation(qT[:, i % 2, :, :].rearrange("p k n -> p (k n)"),
                               bank[4 + i % 2][:, :].bitcast(BF16)[:, 0:HID], ACT.Copy).then_inc(a_q1, 1)

            copy_q1(0)
            for i in range(TILES):
                if i + 1 < TILES:
                    copy_q1(i + 1)
                act.wait_ge(t_y1, i + 1)
                if i >= 2:
                    act.wait_ge(v_h1, 2 * (i - 1))
                for c in range(2):
                    ins = act.activation(silu_g[:, i % 2, c * HALF:(c + 1) * HALF], bank[c][:, 0:HALF], ACT.Silu,
                                         scale=tinyB[:, 4, i:i + 1])
                ins.then_inc(a_s1, 1)
                if i >= 1:
                    act.wait_ge(v_h1, 2 * i)
                    act.activation(junk[:, 0:INTER], h_raw[:, (i - 1) % 2, :], ACT.Square,
                                   accum_out=sumh[:, i - 1:i]).then_inc(a_h1, 1)
                    act.wait_ge(a_h1, i)
            act.wait_ge(v_h1, 2 * TILES)
            act.activation(junk[:, 0:INTER], h_raw[:, 1, :], ACT.Square,
                           accum_out=sumh[:, TILES - 1:TILES]).then_inc(a_h1, 1)
            for i in range(TILES):
                act.wait_ge(t_q2, i + 1)
                if i >= 2:
                    act.wait_ge(t_y2, i - 1)
                bk = bank[6 + i % 2][:, :].bitcast(BF16)
                act.activation(hT[:, i % 2, 0:5, :].rearrange("p k n -> p (k n)"), bk[:, 0:5 * P], ACT.Copy)
                act.activation(hT[0:TAIL, i % 2, 5, :], bk[0:TAIL, 5 * P:6 * P], ACT.Copy).then_inc(a_q2, 1)

            copy_rows(1, True)

            def split_w(w, first=False):
                act.wait_ge(l_hqk, w * 16 + 16)
                if not first:
                    act.wait_ge(t_K, w * 4)
                act.activation(wqk_hi[:, :], wqk_raw[:, :], ACT.Copy).then_inc(a_Whi, 1)

            def split_q(b, n, first=False):
                act.wait_ge(t_Q, n + 1)
                if not (isinstance(n, int) and n == 0):
                    act.wait_ge(t_ssq, n)
                act.activation(squares[:, 0, :, :], bank4(QBK), ACT.Square).then_inc(a_sqQ, 1)
                if not first:
                    act.wait_ge(t_S, n * 2 - 6)
                act.activation(qh[:, :, b, :], bank4(QBK), ACT.Copy).then_inc(a_hiQ, 1)

            def split_k(b, n):
                act.wait_ge(t_K, n + 1)
                act.activation(squares[:, 1, :, :], bank4(QBK), ACT.Square).then_inc(a_sqK, 1)
                act.activation(kh[:, :, b, :], bank4(QBK), ACT.Copy, scale=gk[:, 0:1]).then_inc(a_hiK, 1)

            def copy_rk(b, n, first=False):
                act.wait_ge(t_RK, n + 1)
                if not first:
                    act.wait_ge(v_mm, n * 4 - 12)
                act.activation(rk_row[:, :, b, :], bank4(RBK), ACT.Copy).then_inc(a_RK, 1)

            def exps(b, g):
                act.wait_ge(v_nb, g + 1)
                for h in range(2):
                    for t in range(2):
                        c = h * 2 + t
                        act.activation(att[:, b % 2, h, t, :], att[:, b % 2, h, t, :], ACT.Exp,
                                       bias=shift[:, b % 2, c:c + 1], scale=rqk[:, b, c:c + 1],
                                       accum_out=rowsum[:, b % 2, c:c + 1]).then_inc(a_exp, 1)

            def pair(p, first=False, last=False):
                for b in range(BATCH):
                    g = p * 4 + b
                    n = g + 4
                    start = first and b == 0
                    for j in range(2):
                        act.wait_ge(t_T, g * 2 + j + 1)
                        if not start:
                            act.wait_ge(t_O, g)
                        act.activation(attT_hi[:, j, :, :], bank4(TBK[j]), ACT.Copy).then_inc(a_Thi, 1)
                    if b == 0 and not last:
                        split_w(p + 1)
                    if not (last and b == 3):
                        exps((b + 1) % 4, g + 1)
                    if not (last and b > 0):
                        copy_rk((b + 3) % 4, n - 1, start)
                    if not last:
                        split_q(b, n)
                    if b == 0:
                        act.wait_ge(t_M, p + 1)
                        if not first:
                            act.wait_ge(t_Y, g)
                        act.activation(m_hi[:, :, :], bank4(YBK), ACT.Copy).then_inc(a_Mhi, 1)
                    if not last:
                        split_k(b, n)

            split_w(0, True)
            act.wait_ge(v_gk, 1)
            for n in range(4):
                split_q(n, n, True)
                split_k(n, n)
                if n:
                    copy_rk(n - 1, n - 1, True)
            exps(0, 0)
            pair(0, first=True)
            with act.Fori(1, PAIRS - 1) as p:
                pair(p)
            pair(PAIRS - 1, last=True)

            copy_rows(2, True)
            for j in range(BATCH):
                act.wait_ge(t_xT, j + 1)
                act.activation(xT[:, :, j * 256:(j + 1) * 256], bank4(4 + j % 2), ACT.Copy).then_inc(a_xT, 1)
            act.wait_ge(l_router, 16)
            act.activation(r_hi[:, :, :], r_raw[:, :, :], ACT.Copy).then_inc(a_rw, 1)

            def split_e(par, e, turn, first=False):
                act.wait_ge(l_exp[par], turn * 16 + 16)
                if not first:
                    act.wait_ge(t_D, e * 2 - 2)
                act.activation(e_hi[:, par, :], e_raw[:, par, :], ACT.Copy).then_inc(a_Ehi, 1)

            split_e(0, 0, 0, True)
            act.wait_ge(v_shift, 1)
            act.activation(wexp[:, :, :], shifted[:, :, :], ACT.Exp).then_inc(a_wexp, 1)
            act.activation(shg[:, :], logits[:, :, EXPERTS], ACT.Tanh, scale=0.5).then_inc(a_wexp, 1)
            act.wait_ge(l_shared, 16)
            act.activation(s_hi[:, :, :, :], s_raw[:, :, :, :], ACT.Copy).then_inc(a_rw, 1)
            act.wait_ge(l_shdown, 16)
            act.activation(sdn_hi[:, :], sdn_raw[:, :], ACT.Copy).then_inc(a_rw, 1)

            def silu_step(t, s, early, rows):
                act.wait_ge(t_G, s + 1)
                if not early:
                    act.wait_ge(v_mul1, s - 1)
                act.activation(gate_s[0:rows, t, :], bank[GB][0:rows, :], ACT.Silu).then_inc(a_silu, 1)
                act.wait_ge(v_mul2, s + 1)
                if not early:
                    act.wait_ge(t_D, s - 1)
                act.activation(inter_hi[0:rows, t, :], inter[0:rows, t, :], ACT.Copy).then_inc(a_Ihi, 1)

            def two_pairs(j, first=False, last=False):
                for par in range(2):
                    for t in range(2):
                        silu_step(t, j * 4 + par * 2 + t, first and par == 0, P)
                        if t == 0 and not (last and par == 1):
                            split_e(1 - par, j * 2 + par + 1, j + par, first and par == 0)

            two_pairs(0, first=True)
            with act.Fori(1, EPAIRS // 2 - 1) as j:
                two_pairs(j)
            two_pairs(EPAIRS // 2 - 1, last=True)
            for t in range(2):
                silu_step(t, 2 * EPAIRS + t, False, EI)

        @block.vector
        def _(dve):
            def ask_pow():
                pow_n[0] += 1
                dve.wait_ge(g_pow, pow_n[0])

            def row_stats():
                for i in range(TILES):
                    ins = dve.bn_stats(stats[:, i, :], x[:, i, :])
                link(dve, ins)
                for i in range(TILES):
                    ins = dve.bn_aggr(mv[:, i, :], stats[:, i, :])
                link(dve, ins)
                dve.tensor_scalar(vare[:, :], mv[:, :, 1], EPS, None, ALU.add).then_inc(v_pow, 1)
                ask_pow()

            def normalise():
                for i in range(TILES):
                    dve.tensor_scalar(u[:, i, :], x[:, i, :], mv[:, i, 0:1], rstd[:, i:i + 1], ALU.subtract,
                                      ALU.mult).then_inc(v_u, 1)

            def low_rows(first):
                for j in range(BATCH):
                    dve.wait_ge(a_u, (first - 1) * 4 + j + 1)
                    c = slice(j * 256, (j + 1) * 256)
                    dve.tensor_tensor(xnT_lo[:, :, c], bank4(6 + j % 2), f(xnT_hi[:, :, c]),
                                      ALU.subtract).then_inc(c_u, 1)

            dve.wait_ge(l_x, 32)
            row_stats()
            normalise()
            dve.wait_ge(pool_const, 7)
            dve.tensor_copy(ident_r[:, :], ident[:, :]).then_inc(v_const, 1)
            dve.tensor_copy(ident_b[:, :], ident[:, :]).then_inc(v_const, 1)
            dve.tensor_copy(ones_r[:, :], ones[:, 0:EI]).then_inc(v_const, 1)

            def max_A(b):
                dve.wait_ge(t_eA, b + 1)
                dve.tensor_reduce(nmA[:, b, :], bank4(b % 2), AX.X, ALU.max, negate=True).then_inc(v_mA, 1)

            max_A(0)
            for b in range(BATCH):
                if b + 1 < BATCH:
                    max_A(b + 1)
                dve.wait_ge(a_eA, 2 * b + 2)
                link(dve, dve.reciprocal(invA[:, b, :], sumA[:, b, :]))
                for m in range(2):
                    ins = dve.tensor_scalar(attA[:, b % 2, m, :], attA[:, b % 2, m, :], invA[:, b, m:m + 1], None,
                                            ALU.mult)
                ins.then_inc(v_nA, 1)
                dve.wait_ge(t_oA, b + 1)
                if b == 0:
                    dve.wait_ge(a_tg, 1)
                xb = x[:, 2 * b:2 * b + 2, :]
                dve.scalar_tensor_tensor(xb, bank4(4 + b % 2), tg[:, 0:1], xb, ALU.mult, ALU.add).then_inc(v_xA, 1)

            dve.wait_ge(t_abs, 1)
            for i, n in enumerate((2 * INTER * HID, INTER * HID)):
                ins = dve.tensor_scalar(wsc[:, i:i + 1], bank[7][:, i:i + 1], 1.0 / n, EPS, ALU.mult, ALU.max)
            link(dve, ins)
            link(dve, dve.reciprocal(wsi[:, :], wsc[:, :]))

            def ternary(dst, src, scale, done):
                link(dve, dve.tensor_scalar(src, src, scale, 1.0, ALU.mult, ALU.min))
                link(dve, dve.tensor_scalar(src, src, -1.0, MAGIC, ALU.max, ALU.add))
                ins = dve.tensor_scalar(dst, src, MAGIC, None, ALU.subtract)
                if done is None:
                    return
                ins.then_inc(done, 1)

            dve.wait_ge(a_abs, 3)
            ternary(gate_t[:, :, :], gate_raw[:, :, :], wsi[:, 0:1], v_gw)
            ternary(down_t[0:TAIL, 5, :], down_raw[0:TAIL, 5, :], wsi[0:TAIL, 1:2], None)
            ternary(down_t[:, 0:5, :], down_raw[:, 0:5, :], wsi[:, 1:2], v_dw)
            dve.wait_ge(v_xA, 4)
            row_stats()
            T = tinyB
            link(dve, dve.tensor_tensor(T[:, 2, :], mv[:, :, 1], rstd[:, :], ALU.mult))
            link(dve, dve.tensor_tensor(T[:, 3, :], T[:, 2, :], rstd[:, :], ALU.mult))
            dve.tensor_scalar(T[:, 0, :], T[:, 3, :], EPS, None, ALU.add).then_inc(v_pow, 1)
            dve.wait_ge(l_g1, 16)
            for i in range(TILES):
                ins = dve.scalar_tensor_tensor(w1[:, i, :], x[:, i, :], mv[:, i, 0:1], g1[:, :], ALU.subtract,
                                               ALU.mult)
            link(dve, ins)
            ask_pow()
            link(dve, dve.tensor_tensor(T[:, 2, :], T[:, 1, :], rstd[:, :], ALU.mult))
            link(dve, dve.tensor_reduce(T[:, 3, :], w1[:, :, :], AX.X, ALU.max, apply_absolute_value=True))
            link(dve, dve.tensor_tensor(T[:, 5, :], T[:, 3, :], T[:, 2, :], ALU.mult))
            link(dve, dve.tensor_scalar(T[:, 6, :], T[:, 5, :], EPS, None, ALU.max))
            link(dve, dve.reciprocal(T[:, 7, :], T[:, 6, :]))
            link(dve, dve.scalar_tensor_tensor(T[:, 3, :], T[:, 7, :], 127.0, T[:, 2, :], ALU.mult, ALU.mult))
            link(dve, dve.tensor_scalar(T[:, 4, :], T[:, 6, :], 1.0 / 127.0, wsc[:, 0:1], ALU.mult, ALU.mult))
            for i in range(TILES):
                ins = dve.tensor_scalar(w1[:, i, :], w1[:, i, :], T[:, 3, i:i + 1], MAGIC, ALU.mult, ALU.add)
            link(dve, ins)
            for i in range(TILES):
                dve.tensor_scalar(q1[:, i, :], w1[:, i, :], MAGIC, None, ALU.subtract).then_inc(v_q1, 1)
            dve.wait_ge(l_g2, 16)
            for i in range(TILES):
                dve.wait_ge(a_s1, i + 1)
                if i >= 2:
                    dve.wait_ge(a_h1, i - 1)
                for c in range(2):
                    cs = slice(c * HALF, (c + 1) * HALF)
                    dve.scalar_tensor_tensor(h_raw[:, i % 2, cs], bank[2 + c][:, 0:HALF], T[:, 4, i:i + 1],
                                             silu_g[:, i % 2, cs], ALU.mult, ALU.mult).then_inc(v_h1, 1)
                dve.wait_ge(v_h1, 2 * i + 2)
                link(dve, dve.tensor_tensor(w2[:, i, :], h_raw[:, i % 2, :], g2[:, :], ALU.mult))
                ins = dve.tensor_reduce(amax2[:, i:i + 1], w2[:, i, :], AX.X, ALU.max, apply_absolute_value=True)
            link(dve, ins)
            dve.wait_ge(a_h1, TILES)
            dve.tensor_scalar(T[:, 5, :], sumh[:, :], 1.0 / INTER, EPS, ALU.mult, ALU.add).then_inc(v_pow, 1)
            ask_pow()
            link(dve, dve.tensor_tensor(T[:, 2, :], T[:, 6, :], amax2[:, :], ALU.mult))
            link(dve, dve.tensor_scalar(T[:, 3, :], T[:, 2, :], EPS, None, ALU.max))
            link(dve, dve.reciprocal(T[:, 7, :], T[:, 3, :]))
            link(dve, dve.scalar_tensor_tensor(T[:, 2, :], T[:, 7, :], 127.0, T[:, 6, :], ALU.mult, ALU.mult))
            link(dve, dve.tensor_scalar(T[:, 5, :], T[:, 3, :], 1.0 / 127.0, wsc[:, 1:2], ALU.mult, ALU.mult))
            link(dve, dve.tensor_scalar(T[:, 7, :], T[:, 5, :], tg[:, 2:3], None, ALU.mult))

            def add_down(i):
                dve.wait_ge(t_y2, i + 1)
                dve.scalar_tensor_tensor(x[:, i, :], bank[4 + i % 2][:, 0:HID], T[:, 7, i:i + 1], x[:, i, :],
                                         ALU.mult, ALU.add).then_inc(v_xB, 1)

            for i in range(TILES):
                link(dve, dve.tensor_scalar(w2[:, i, :], w2[:, i, :], T[:, 2, i:i + 1], MAGIC, ALU.mult, ALU.add))
                if i >= 2:
                    dve.wait_ge(t_q2, i - 1)
                dve.tensor_scalar(q2[:, i % 2, :], w2[:, i, :], MAGIC, None, ALU.subtract).then_inc(v_q2, 1)
                if i:
                    add_down(i - 1)
            add_down(TILES - 1)
            dve.wait_ge(a_ctx, 2)
            dve.tensor_tensor(ctxT_lo[:, :], ctxT_raw[:, :], f(ctxT_hi[:, :]), ALU.subtract).then_inc(v_ctx, 1)
            dve.tensor_tensor(ctx_lo[:, :, :], ctx_raw[:, :, :], f(ctx_hi[:, :, :]), ALU.subtract).then_inc(v_ctx, 1)
            dve.wait_ge(l_gqk, 16)
            dve.tensor_scalar(gk[:, :], gqk_raw[:, 0:1], gqk_raw[:, 1:2], float(D) ** -0.5, ALU.mult,
                              ALU.mult).then_inc(v_gk, 1)

            dve.wait_ge(v_xB, TILES)
            row_stats()
            normalise()

            def low_w(w):
                dve.wait_ge(a_Whi, w + 1)
                dve.tensor_tensor(wqk_lo[:, :], wqk_raw[:, :], f(wqk_hi[:, :]), ALU.subtract).then_inc(v_Wlo, 1)

            def low_q(b, n):
                dve.wait_ge(a_hiQ, n + 1)
                dve.tensor_tensor(ql[:, :, b, :], bank4(QBK), f(qh[:, :, b, :]), ALU.subtract).then_inc(v_Qlo, 1)

            def low_k(b, n):
                dve.wait_ge(a_hiK, n + 1)
                dve.scalar_tensor_tensor(kl[:, :, b, :], bank4(QBK), gk[:, 0:1], f(kh[:, :, b, :]), ALU.mult,
                                         ALU.subtract).then_inc(v_Klo, 1)

            def mean_squares(n):
                dve.wait_ge(t_ssq, n + 1)
                if not (isinstance(n, int) and n == 0):
                    dve.wait_ge(g_r8, n)
                dve.tensor_scalar(ssq8[:, :], bank[RBK][:, 0:8], 1.0 / D, EPS, ALU.mult, ALU.add).then_inc(v_r8, 1)

            def split_rk(b, n):
                dve.wait_ge(g_r8, n + 1)
                if not (isinstance(n, int) and n == 0):
                    dve.wait_ge(t_RK, n)
                dve.tensor_copy(rk_hi[:, :], rqk[:, b, 4:8]).then_inc(v_rh, 1)
                dve.wait_ge(v_rh, n + 1)
                dve.tensor_tensor(rk_lo[:, :], rqk[:, b, 4:8], f(rk_hi[:, :]), ALU.subtract).then_inc(v_rs, 1)

            def scale_max(b, g, early=False):
                dve.wait_ge(a_RK, g + 1)
                if not early:
                    dve.wait_ge(t_T, g * 2 - 2)
                dve.wait_ge(t_S, g * 2 + 2)
                dve.tensor_scalar(minus_rq[:, b % 2, :], rqk[:, b, 0:4], -1.0, None, ALU.mult).then_inc(v_rq, 1)
                for h in range(2):
                    for t in range(2):
                        dve.tensor_tensor_reduce(out=att[:, b % 2, h, t, :], in0=bank4(SBK[h])[:, t, :],
                                                 in1=rk_row[:, h, b, :], scale=1.0, scalar=LOWEST, op0=ALU.mult,
                                                 op1=ALU.max,
                                                 accum_out=rowmax[:, b % 2, h * 2 + t:h * 2 + t + 1]).then_inc(v_mm, 1)
                dve.wait_ge(v_mm, g * 4 + 4)
                dve.wait_ge(v_rq, g + 1)
                dve.tensor_tensor(shift[:, b % 2, :], rowmax[:, b % 2, :], minus_rq[:, b % 2, :],
                                  ALU.mult).then_inc(v_nb, 1)

            def norm_rows(b, g):
                dve.wait_ge(a_exp, g * 4 + 4)
                dve.reciprocal(rowinv[:, b % 2, :], rowsum[:, b % 2, :]).then_inc(v_l, 1)
                dve.wait_ge(v_l, g + 1)
                for h in range(2):
                    for t in range(2):
                        c = h * 2 + t
                        dve.tensor_scalar(att[:, b % 2, h, t, :], att[:, b % 2, h, t, :],
                                          rowinv[:, b % 2, c:c + 1], None, ALU.mult).then_inc(v_P, 1)

            def add_output(b, g):
                dve.wait_ge(t_Y, g + 1)
                xb = x[:, 2 * b:2 * b + 2, :]
                dve.scalar_tensor_tensor(xb, bank4(YBK), tg[:, 1:2], xb, ALU.mult, ALU.add).then_inc(v_Y, 1)

            def pair(p, first=False, last=False):
                for b in range(BATCH):
                    g = p * 4 + b
                    n = g + 4
                    start = first and b == 0
                    if not (last and b == 3):
                        scale_max((b + 1) % 4, g + 1, start)
                    if not (last and b > 0):
                        mean_squares(n - 1)
                    for j in range(2):
                        dve.wait_ge(a_Thi, g * 2 + j + 1)
                        dve.tensor_tensor(attT_lo[:, j, :, :], bank4(TBK[j]), f(attT_hi[:, j, :, :]),
                                          ALU.subtract).then_inc(v_Tlo, 1)
                    if b == 0 and not last:
                        low_w(p + 1)
                    if not (last and b > 0):
                        split_rk((b + 3) % 4, n - 1)
                    if not start:
                        add_output((b + 3) % 4, g - 1)
                    if not (last and b == 3):
                        norm_rows((b + 1) % 4, g + 1)
                    if not last:
                        low_q(b, n)
                    dve.wait_ge(t_O, g + 1)
                    if not start:
                        dve.wait_ge(t_Y, g)
                    dve.tensor_copy(o_hi[:, :, :], bank4(OBK)).then_inc(v_Ohi, 1)
                    dve.wait_ge(v_Ohi, g + 1)
                    dve.tensor_tensor(o_lo[:, :, :], bank4(OBK), f(o_hi[:, :, :]), ALU.subtract).then_inc(v_Olo, 1)
                    if b == 0:
                        dve.wait_ge(a_Mhi, p + 1)
                        dve.tensor_tensor(m_lo[:, :, :], bank4(YBK), f(m_hi[:, :, :]),
                                          ALU.subtract).then_inc(v_Mlo, 1)
                    if not last:
                        low_k(b, n)

            low_rows(1)
            low_w(0)
            for n in range(4):
                if n:
                    mean_squares(n - 1)
                    split_rk(n - 1, n - 1)
                low_q(n, n)
                low_k(n, n)
            scale_max(0, 0, True)
            norm_rows(0, 0)
            pair(0, first=True)
            with dve.Fori(1, PAIRS - 1) as p:
                pair(p)
            pair(PAIRS - 1, last=True)
            add_output(3, GROUPS - 1)
            dve.wait_ge(v_Y, GROUPS)

            row_stats()
            normalise()
            low_rows(2)
            dve.wait_ge(a_rw, 1)
            dve.tensor_tensor(r_lo[:, :, :], r_raw[:, :, :], f(r_hi[:, :, :]), ALU.subtract).then_inc(v_rw, 1)

            def low_e(par, e):
                dve.wait_ge(a_Ehi, e + 1)
                dve.tensor_tensor(e_lo[:, par, :], e_raw[:, par, :], f(e_hi[:, par, :]),
                                  ALU.subtract).then_inc(v_Elo, 1)

            def select(par, e, first=False):
                if not first:
                    dve.wait_ge(t_W, e * 2 - 2)
                dve.tensor_copy(selb[:, par, :].rearrange("p (a n) -> p a n", a=2),
                                expert_rows[:, bass.ds(e * 2, 2)].unsqueeze(2).broadcast_to([P, 2, EI])
                                ).then_inc(v_sel, 1)

            low_e(0, 0)
            select(0, 0, True)
            dve.wait_ge(t_log, 1)
            for i in range(2):
                ins = dve.tensor_copy(logits[:, 4 * i:4 * i + 4, :],
                                      bank[2 + i][:, 0:4 * LOGC].rearrange("p (i n) -> p i n", i=4))
            link(dve, ins)
            for i in range(TILES):
                ins = dve.max(top8[:, i, :], logits[:, i, 0:EXPERTS])
            link(dve, ins)
            lg = logits[:, :, 0:EXPERTS]
            dve.tensor_tensor(shifted[:, :, :], lg, top8[:, :, 0:1].broadcast_to([P, TILES, EXPERTS]),
                              ALU.subtract).then_inc(v_shift, 1)
            for i in range(TILES):
                ins = dve.match_replace(out=struck[:, i, :], in_to_replace=top8[:, i, :],
                                        in_values=logits[:, i, 0:EXPERTS], imm_value=LOWEST)
            link(dve, ins)
            link(dve, dve.tensor_tensor(chosen[:, :, :], struck[:, :, :], lg, ALU.not_equal))
            dve.wait_ge(a_wexp, 2)
            link(dve, dve.tensor_tensor(chosen[:, :, :], chosen[:, :, :], wexp[:, :, :], ALU.mult))
            link(dve, dve.tensor_reduce(wsum[:, :], chosen[:, :, :], AX.X, ALU.add))
            link(dve, dve.reciprocal(winv[:, :], wsum[:, :]))
            link(dve, dve.tensor_tensor(chosen[:, :, :], chosen[:, :, :],
                                        winv[:, :].unsqueeze(2).broadcast_to([P, TILES, EXPERTS]), ALU.mult))
            link(dve, dve.tensor_copy(wcat[:, :, 0:EXPERTS].bitcast(F32R), chosen[:, :, :]))
            dve.tensor_tensor(wcat[:, :, EXPERTS:P].bitcast(F32R), chosen[:, :, :], wcat[:, :, 0:EXPERTS],
                              ALU.subtract)
            link(dve, dve.tensor_scalar(shg[:, :], shg[:, :], 0.5, 0.5, ALU.mult, ALU.add))
            link(dve, dve.tensor_copy(shcat[:, :, 0].bitcast(F32R), shg[:, :]))
            dve.tensor_tensor(shcat[:, :, 1].bitcast(F32R), shg[:, :], shcat[:, :, 0],
                              ALU.subtract).then_inc(v_wcat, 1)
            for i in range(2):
                dve.wait_ge(t_wT, i + 1)
                dve.tensor_copy(wT[:, i * 512:(i + 1) * 512], bank[3 + i][:, :])
            for i in range(2):
                dve.wait_ge(t_wT, 3 + i)
                dve.tensor_copy(shT[:, i * 512:(i + 1) * 512], bank[5 + i][0:2, :]).then_inc(v_wT, 1)
            dve.wait_ge(a_rw, 3)
            dve.tensor_tensor(s_lo[:, :, :, :], s_raw[:, :, :, :], f(s_hi[:, :, :, :]),
                              ALU.subtract).then_inc(v_rw, 1)
            dve.tensor_tensor(sdn_lo[:, :], sdn_raw[:, :], f(sdn_hi[:, :]), ALU.subtract).then_inc(v_rw, 1)

            def weigh(t, s, early, rows):
                dve.wait_ge(a_silu, s + 1)
                dve.wait_ge(t_U, s + 1)
                dve.tensor_tensor(prod[0:rows, t, :], gate_s[0:rows, t, :], bank[UB][0:rows, :],
                                  ALU.mult).then_inc(v_mul1, 1)
                dve.wait_ge(v_mul1, s + 1)
                dve.wait_ge(t_W, s + 1)
                if not early:
                    dve.wait_ge(a_Ihi, s - 1)
                dve.tensor_tensor(inter[0:rows, t, :], prod[0:rows, t, :], bank[WB][0:rows, :],
                                  ALU.mult).then_inc(v_mul2, 1)
                dve.wait_ge(a_Ihi, s + 1)
                dve.tensor_tensor(inter_lo[0:rows, t, :], inter[0:rows, t, :], f(inter_hi[0:rows, t, :]),
                                  ALU.subtract).then_inc(v_Ilo, 1)

            def two_pairs(j, first=False, last=False):
                for par in range(2):
                    for t in range(2):
                        weigh(t, j * 4 + par * 2 + t, first and par == 0, P)
                        if t == 0 and not (last and par == 1):
                            low_e(1 - par, j * 2 + par + 1)
                            select(1 - par, j * 2 + par + 1, first and par == 0)

            two_pairs(0, first=True)
            with dve.Fori(1, EPAIRS // 2 - 1) as j:
                two_pairs(j)
            two_pairs(EPAIRS // 2 - 1, last=True)
            for t in range(2):
                weigh(t, 2 * EPAIRS + t, False, EI)
            for t in range(2):
                for hb in range(2):
                    dve.wait_ge(t_D, 2 * EPAIRS + 2 * t + hb + 1)
                    dve.scalar_tensor_tensor(final[:, hb, t, :], bank[ACC[hb][t]][:, :], tg[:, 3:4],
                                             xT[:, hb, t * 512:(t + 1) * 512], ALU.mult, ALU.add).then_inc(v_out, 1)


def kernel(**inputs):
    import numpy as np
    import concourse.bacc as bacc
    from concourse.bass_utils import run_bass_kernel_spmd

    a = {k: np.asarray(v) for k, v in inputs.items()}

    def tiles(v):
        return v.reshape(TILES, P, v.shape[-1]).transpose(1, 0, 2)

    def parts(v):
        return v.reshape(-1, P, v.shape[-1]).transpose(1, 0, 2)

    ctx2 = a["ctx_1024"].reshape(TOK, CDIM)
    wq = a["L1_xattn_Wq"].reshape(KH, P, PAIRS, 2, D).transpose(2, 1, 3, 0, 4).reshape(PAIRS, P, 512)
    wk = a["L1_xattn_Wk"].reshape(P, PAIRS, 2 * D).transpose(1, 0, 2)
    wv = a["L1_xattn_Wv"].reshape(CDIM, PAIRS, 2, D).transpose(1, 3, 2, 0).reshape(PAIRS, D, 2 * CDIM)
    wo = a["L1_xattn_Wo"].reshape(PAIRS, 2, D, HID).transpose(0, 2, 1, 3).reshape(PAIRS, D, 2 * HID)
    gu = a["L1_ffn_gu_w"].reshape(EPAIRS, 2, 2, EI, KH, P).transpose(0, 5, 2, 4, 1, 3).reshape(EPAIRS, P, 512)
    dp = a["L1_ffn_dp_w"].reshape(EPAIRS, 2, HID, EI).transpose(0, 1, 3, 2).reshape(EPAIRS, P, HID)
    router = np.concatenate([a["L1_ffn_gate_w"], a["L1_ffn_sh_gate1_w"],
                             np.zeros((1, HID), np.float32)], 0).T
    downT = a["L0_ffn_down_w"].T
    arrays = {
        "x_tok": tiles(a["x"].reshape(TOK, HID)),
        "ctx_tok": tiles(ctx2),
        "ctxT": ctx2.T,
        "qk0": np.stack([a["L0_xattn_Wq"].T, a["L0_xattn_Wk"].T], 1),
        "bias0": np.stack([a["L0_xattn_bq"], a["L0_xattn_bk"]], 1),
        "gains": np.broadcast_to(np.concatenate([a["g_xattn"], a["g_ffn"]])[None, :], (P, 4)),
        "gate_wT": parts(a["L0_ffn_gate_w"].T),
        "down_wT": parts(downT[:5 * P]),
        "down_tail": downT[5 * P:],
        "norm_g1": a["L0_ffn_gate_norm_w"],
        "norm_g2": a["L0_ffn_down_norm_w"],
        "gqk": np.stack([a["L1_xattn_gq"], a["L1_xattn_gk"]], 1),
        "head_qk": np.concatenate([wq, wk], 2),
        "head_vo": np.concatenate([wv, wo], 2),
        "router_w": parts(router),
        "expert_w": np.concatenate([gu, dp], 2),
        "shared_w": np.stack([parts(a["L1_ffn_sh_gate_w"].T), parts(a["L1_ffn_sh_up_w"].T)], 1),
        "shared_down": a["L1_ffn_sh_down_w"].T,
    }
    arrays = {k: np.ascontiguousarray(v) for k, v in arrays.items()}
    nc = bacc.Bacc("TRN2", target_bir_lowering=False, num_devices=1)
    aps = [nc.dram_tensor(f"in_{k}", v.shape, mybir.dt.from_np(v.dtype), kind="ExternalInput").ap()
           for k, v in arrays.items()]
    out = nc.dram_tensor("outT", (KH, P, TOK), F32, kind="ExternalOutput").ap()
    flamingo_kernel(nc, *aps, out)
    r = run_bass_kernel_spmd(nc, [{f"in_{k}": v for k, v in arrays.items()}], core_ids=[0])
    outT = r.results[0]["outT"]
    return np.ascontiguousarray(outT.reshape(HID, TOK).T).reshape(BATCH, SEQ, HID)
```

```python
from contextlib import ExitStack

import concourse.bass as bass
from concourse import mybir

F32 = mybir.dt.float32
F32R = mybir.dt.float32r
BF16 = mybir.dt.bfloat16
ALU = mybir.AluOpType
ACT = mybir.ActivationFunctionType
AX = mybir.AxisListType

P = 128
BATCH, SEQ, HID, CDIM = 4, 256, 256, 128
TOK = BATCH * SEQ
TILES = TOK // P
KH = HID // P
INTER = 704
HALF = INTER // 2
KI = 6
TAIL = INTER - 5 * P
HEADS, D = 16, 128
PAIRS = HEADS // 2
GROUPS = PAIRS * BATCH
PIECES = GROUPS
EXPERTS, TOPK, EI = 64, 8, 64
EPAIRS = EXPERTS // 2
LOGC = 66
EPS = 1e-5
MAGIC = 12582912.0
LOWEST = -3.0e38


def flamingo_kernel(nc, x_tok, ctx_tok, ctxT, qk0, bias0, gains, gate_wT, down_wT, down_tail,
                    norm_g1, norm_g2, gqk, head_qk, head_vo, router_w, expert_w, shared_w,
                    shared_down, outT):
    with ExitStack() as ctx:
        def sb(name, shape, dt=F32):
            return ctx.enter_context(nc.sbuf_tensor(name, shape, dt))

        def sem(name):
            return ctx.enter_context(nc.semaphore(name))

        bank = [ctx.enter_context(nc.psum_tensor(f"bank{i}", [P, 512], F32)) for i in range(8)]

        def wait(engine, semaphore, value):
            if not (isinstance(value, int) and value <= 0):
                engine.wait_ge(semaphore, value)

        ident = sb("ident", [P, P])
        ident_r = sb("ident_r", [P, P], F32R)
        ident_b = sb("ident_b", [P, P], BF16)
        ones = sb("ones", [P, P])
        ones_r = sb("ones_r", [P, EI], F32R)
        minus_half = sb("minus_half", [P, 8])
        expert_rows = sb("expert_rows", [P, EXPERTS])
        x = sb("x", [P, TILES, HID])
        ctxT_raw = sb("ctxT_raw", [P, TOK])
        ctxT_hi = sb("ctxT_hi", [P, TOK], F32R)
        ctxT_lo = sb("ctxT_lo", [P, TOK], F32R)
        ctx_raw = sb("ctx_raw", [P, TILES, CDIM])
        ctx_hi = sb("ctx_hi", [P, TILES, CDIM], F32R)
        ctx_lo = sb("ctx_lo", [P, TILES, CDIM], F32R)
        gains_raw = sb("gains_raw", [P, 4])
        tg = sb("tg", [P, 4])
        stats = sb("stats", [P, TILES, 6])
        mv = sb("mv", [P, TILES, 2])
        vare = sb("vare", [P, TILES])
        rstd = sb("rstd", [P, TILES])
        u = sb("u", [P, TILES, HID])
        xnT_hi = sb("xnT_hi", [P, KH, TOK], F32R)
        xnT_lo = sb("xnT_lo", [P, KH, TOK], F32R)
        xT = sb("xT", [P, KH, TOK])

        l_x, l_ctxT, l_ctx, l_qk0, l_bias, l_gains = (sem(n) for n in (
            "l_x", "l_ctxT", "l_ctx", "l_qk0", "l_bias", "l_gains"))
        l_gate, l_down, l_tail, l_g1, l_g2, l_gqk = (sem(n) for n in (
            "l_gate", "l_down", "l_tail", "l_g1", "l_g2", "l_gqk"))
        l_router, l_shared, l_shdown = sem("l_router"), sem("l_shared"), sem("l_shdown")
        l_hqk, l_hvo, l_out = sem("l_hqk"), sem("l_hvo"), sem("l_out")
        l_exp = [sem("l_exp0"), sem("l_exp1")]
        pool_const = sem("pool_const")
        v_const, v_ctx = sem("v_const"), sem("v_ctx")
        a_ctx, a_tg = sem("a_ctx"), sem("a_tg")
        v_link = sem("v_link")
        link_n = [0]

        def link(dve, ins):
            link_n[0] += 1
            ins.then_inc(v_link, 1)
            dve.wait_ge(v_link, link_n[0])

        v_pow, g_pow = sem("v_pow"), sem("g_pow")
        pow_n = [0]
        v_u, t_u, a_u, c_u = sem("v_u"), sem("t_u"), sem("a_u"), sem("c_u")

        wqk0 = sb("wqk0", [P, 2, D])
        bqk = sb("bqk", [P, 2])
        qkA = sb("qkA", [P, 2, TOK])
        attA = sb("attA", [P, 2, 2, SEQ])
        attT = sb("attT", [P, 2, 2, SEQ])
        nmA = sb("nmA", [P, BATCH, 2])
        sumA = sb("sumA", [P, BATCH, 2])
        invA = sb("invA", [P, BATCH, 2])
        t_qkA, a_qkA, t_eA, v_mA, a_eA, v_nA, t_aA, a_aA, t_oA, v_xA = (sem(n) for n in (
            "t_qkA", "a_qkA", "t_eA", "v_mA", "a_eA", "v_nA", "t_aA", "a_aA", "t_oA", "v_xA"))

        g1 = sb("g1", [P, HID])
        g2 = sb("g2", [P, INTER])
        absum = sb("absum", [P, 3])
        wsc = sb("wsc", [P, 2])
        wsi = sb("wsi", [P, 2])
        tinyB = sb("tinyB", [P, 8, TILES])
        sumh = sb("sumh", [P, TILES])
        amax2 = sb("amax2", [P, TILES])
        gqk_raw = sb("gqk_raw", [P, 2])
        gk = sb("gk", [P, 1])
        wqk_raw = sb("wqk_raw", [P, 768])
        wqk_hi = sb("wqk_hi", [P, 2, 768], F32R)
        wqk_lo = sb("wqk_lo", [P, 2, 768], F32R)
        wvo_raw = sb("wvo_raw", [P, 768])
        ssq = sb("ssq", [P, 2, 8])
        msq = sb("msq", [P, 8])
        rqk = sb("rqk", [P, BATCH, 8])
        rowmax = sb("rowmax", [P, 2, 2, 2])
        shift = sb("shift", [P, 2, 2, 2])
        rowsum = sb("rowsum", [P, 2, 2, 2])
        rowinv = sb("rowinv", [P, BATCH, 2, 2])
        e_raw = sb("e_raw", [P, 2, 768])
        r_raw = sb("r_raw", [P, KH, LOGC])
        s_raw = sb("s_raw", [P, 2, KH, EI])
        sdn_raw = sb("sdn_raw", [EI, HID])
        bctx = ExitStack()
        gate_raw = bctx.enter_context(nc.sbuf_tensor("gate_raw", [P, KH, 2 * INTER], F32))
        down_raw = bctx.enter_context(nc.sbuf_tensor("down_raw", [P, KI, HID], F32))
        gate_t = bctx.enter_context(nc.sbuf_tensor("gate_t", [P, KH, 2 * INTER], BF16))
        down_t = bctx.enter_context(nc.sbuf_tensor("down_t", [P, KI, HID], BF16))
        w1 = bctx.enter_context(nc.sbuf_tensor("w1", [P, TILES, HID], F32))
        q1 = bctx.enter_context(nc.sbuf_tensor("q1", [P, TILES, HID], BF16))
        qT = bctx.enter_context(nc.sbuf_tensor("qT", [P, 2, KH, P], BF16))
        silu_g = bctx.enter_context(nc.sbuf_tensor("silu_g", [P, 2, INTER], F32))
        h_raw = bctx.enter_context(nc.sbuf_tensor("h_raw", [P, 2, INTER], F32))
        w2 = bctx.enter_context(nc.sbuf_tensor("w2", [P, TILES, INTER], F32))
        q2 = bctx.enter_context(nc.sbuf_tensor("q2", [P, 2, INTER], BF16))
        hT = bctx.enter_context(nc.sbuf_tensor("hT", [P, 2, KI, P], BF16))
        junk = bctx.enter_context(nc.sbuf_tensor("junk", [P, 2 * KH * INTER], F32))
        bctx.close()
        a_abs, t_abs, v_gw, v_dw = sem("a_abs"), sem("t_abs"), sem("v_gw"), sem("v_dw")
        v_q1, t_q1, a_q1, t_y1, a_s1, v_h1, a_h1 = (sem(n) for n in (
            "v_q1", "t_q1", "a_q1", "t_y1", "a_s1", "v_h1", "a_h1"))
        v_r2, v_q2, t_q2, a_q2, t_y2, v_xB = (sem(n) for n in ("v_r2", "v_q2", "t_q2", "a_q2", "t_y2", "v_xB"))

        cctx = ExitStack()

        def sc(name, shape, dt=F32):
            return cctx.enter_context(nc.sbuf_tensor(name, shape, dt))

        qh, ql = sc("qh", [P, 2, BATCH, SEQ], F32R), sc("ql", [P, 2, BATCH, SEQ], F32R)
        kh, kl = sc("kh", [P, 2, BATCH, SEQ], F32R), sc("kl", [P, 2, BATCH, SEQ], F32R)
        q_raw = sc("q_raw", [P, 2, 2, 2, D])
        k_raw = sc("k_raw", [P, 2, 2, 2, D])
        k_sq = sc("k_sq", [P, 2, 2, D])
        att = sc("att", [P, 2, 2, 2, SEQ])
        attT_hi = sc("attT_hi", [P, 2, 2, SEQ], F32R)
        attT_lo = sc("attT_lo", [P, 2, 2, SEQ], F32R)
        o_hi, o_lo = sc("o_hi", [P, 2, SEQ], F32R), sc("o_lo", [P, 2, SEQ], F32R)
        m_hi, m_lo = sc("m_hi", [P, 2, HID], F32R), sc("m_lo", [P, 2, HID], F32R)
        cctx.close()

        t_S, t_T, t_O, t_Y, t_Q, t_K, t_TQ, t_TK, t_M = (sem(n) for n in (
            "t_S", "t_T", "t_O", "t_Y", "t_Q", "t_K", "t_TQ", "t_TK", "t_M"))
        a_exp, a_Thi, a_rawQ, a_sqQ, a_rawK, a_hiQ, a_hiK, a_Ohi, a_Mhi, a_Whi = (sem(n) for n in (
            "a_exp", "a_Thi", "a_rawQ", "a_sqQ", "a_rawK", "a_hiQ", "a_hiK", "a_Ohi", "a_Mhi", "a_Whi"))
        v_max, v_shift_c, v_Tlo, v_Y, v_inv, v_Qlo, v_Klo, v_sqK, v_msq, v_Olo, v_Mlo, v_gk = (
            sem(n) for n in ("v_max", "v_shift_c", "v_Tlo", "v_Y", "v_inv", "v_Qlo", "v_Klo", "v_sqK", "v_msq",
                             "v_Olo", "v_Mlo", "v_gk"))
        g_rms, g_kn, g_Wlo = sem("g_rms"), sem("g_kn"), sem("g_Wlo")

        dctx = ExitStack()

        def sd(name, shape, dt=F32):
            return dctx.enter_context(nc.sbuf_tensor(name, shape, dt))

        e_hi, e_lo = sd("e_hi", [P, 2, 768], F32R), sd("e_lo", [P, 2, 768], F32R)
        selb = sd("selb", [P, 2, P], F32R)
        gate_s = sd("gate_s", [P, 2, 512])
        prod = sd("prod", [P, 2, 512])
        inter = sd("inter", [P, 2, 512])
        inter_hi, inter_lo = sd("inter_hi", [P, 2, 512], F32R), sd("inter_lo", [P, 2, 512], F32R)
        final = sd("final", [P, 2, 2, 512])
        r_hi, r_lo = sd("r_hi", [P, KH, LOGC], F32R), sd("r_lo", [P, KH, LOGC], F32R)
        s_hi, s_lo = sd("s_hi", [P, 2, KH, EI], F32R), sd("s_lo", [P, 2, KH, EI], F32R)
        sdn_hi, sdn_lo = sd("sdn_hi", [EI, HID], F32R), sd("sdn_lo", [EI, HID], F32R)
        logits = sd("logits", [P, TILES, LOGC])
        top8 = sd("top8", [P, TILES, TOPK])
        struck = sd("struck", [P, TILES, EXPERTS])
        chosen = sd("chosen", [P, TILES, EXPERTS])
        shifted = sd("shifted", [P, TILES, EXPERTS])
        wexp = sd("wexp", [P, TILES, EXPERTS])
        wcat = sd("wcat", [P, TILES, P])
        wsum = sd("wsum", [P, TILES])
        winv = sd("winv", [P, TILES])
        shg = sd("shg", [P, TILES])
        shcat = sd("shcat", [P, TILES, 2])
        wT = sd("wT", [P, TOK], F32R)
        shT = sd("shT", [2, TOK], F32R)
        dctx.close()
        t_log, v_log, v_shift, a_wexp, v_wcat, t_wT, v_wT, t_xT, a_xT, v_rw, a_rw = (sem(n) for n in (
            "t_log", "v_log", "v_shift", "a_wexp", "v_wcat", "t_wT", "v_wT", "t_xT", "a_xT", "v_rw", "a_rw"))
        t_G, t_U, t_W, t_D, a_silu, a_Ihi, a_Ehi, v_mul1, v_mul2, v_Ilo, v_Elo, v_sel, v_out = (sem(n) for n in (
            "t_G", "t_U", "t_W", "t_D", "a_silu", "a_Ihi", "a_Ehi", "v_mul1", "v_mul2", "v_Ilo", "v_Elo",
            "v_sel", "v_out"))

        GB, UB, WB = 0, 1, 2
        ACC = [[3, 4], [5, 6]]
        SBK, TBK, OBK, YBK, QBK, KBK = [0, 1], [2, 3], 4, 5, 6, 7

        def f(ap):
            return ap.bitcast(F32)

        def bank4(i):
            return bank[i][:, :].rearrange("p (a n) -> p a n", a=2)

        block = ctx.enter_context(nc.Block())

        def split_mm(pe, out, l_hi, l_lo, r_hi_, r_lo_, start, stop):
            pe.matmul(out, l_hi, r_hi_, start=start, stop=False, skip_group_check=True)
            pe.matmul(out, l_hi, r_lo_, start=False, stop=False, skip_group_check=True)
            return pe.matmul(out, l_lo, r_hi_, start=False, stop=stop, skip_group_check=True)

        @block.sync
        def _(sp):
            sp.dma_start(ctxT_raw[:, :], ctxT).then_inc(l_ctxT, 16)
            sp.dma_start(wqk0[:, :, :], qk0).then_inc(l_qk0, 16)
            sp.dma_start(x[:, 0:4, :], x_tok[:, 0:4, :]).then_inc(l_x, 16)
            sp.dma_start(x[:, 4:8, :], x_tok[:, 4:8, :]).then_inc(l_x, 16)
            sp.dma_start(ctx_raw[:, :, :], ctx_tok).then_inc(l_ctx, 16)
            sp.dma_start(gate_raw[:, :, :], gate_wT).then_inc(l_gate, 16)
            sp.dma_start(down_raw[:, 0:5, :], down_wT).then_inc(l_down, 16)
            sp.dma_start(down_raw[0:TAIL, 5, :], down_tail).then_inc(l_tail, 16)
            sp.dma_start(g1[:, :], norm_g1.partition_broadcast(P)).then_inc(l_g1, 16)
            sp.dma_start(g2[:, :], norm_g2.partition_broadcast(P)).then_inc(l_g2, 16)
            sp.dma_start(gqk_raw[:, :], gqk).then_inc(l_gqk, 16)
            sp.dma_start(wqk_raw[:, :], head_qk[0]).then_inc(l_hqk, 16)
            sp.dma_start(wvo_raw[:, :], head_vo[0]).then_inc(l_hvo, 16)
            sp.dma_start(r_raw[:, :, :], router_w).then_inc(l_router, 16)
            sp.dma_start(e_raw[:, 0, :], expert_w[0]).then_inc(l_exp[0], 16)
            sp.dma_start(e_raw[:, 1, :], expert_w[1]).then_inc(l_exp[1], 16)
            sp.dma_start(s_raw[:, :, :, :], shared_w).then_inc(l_shared, 16)
            sp.dma_start(sdn_raw[:, :], shared_down).then_inc(l_shdown, 16)
            with sp.Fori(1, PAIRS) as p:
                sp.wait_ge(g_Wlo, p)
                sp.dma_start(wqk_raw[:, :], head_qk[bass.ds(p, 1)].rearrange("a p n -> (a p) n")).then_inc(l_hqk, 16)
                sp.wait_ge(t_M, p)
                sp.dma_start(wvo_raw[:, :], head_vo[bass.ds(p, 1)].rearrange("a p n -> (a p) n")).then_inc(l_hvo, 16)
            with sp.Fori(1, EPAIRS // 2) as j:
                for par in range(2):
                    sp.wait_ge(v_Elo, j * 2 + par - 1)
                    sp.dma_start(e_raw[:, par, :],
                                 expert_w[bass.ds(j * 2 + par, 1)].rearrange("a p n -> (a p) n")).then_inc(l_exp[par], 16)
            for t in range(2):
                for hb in range(2):
                    sp.wait_ge(v_out, 2 * t + hb + 1)
                    sp.dma_start(outT[hb, :, t * 512:(t + 1) * 512], final[:, hb, t, :]).then_inc(l_out, 16)
            sp.wait_ge(l_out, 64)

        @block.gpsimd
        def _(pool):
            pool.memset(ident[:, :], 0.0).then_inc(pool_const, 1)
            pool.memset(ones[:, :], 1.0).then_inc(pool_const, 1)
            pool.memset(minus_half[:, :], -0.5).then_inc(pool_const, 1)
            pool.memset(expert_rows[:, :], 0.0).then_inc(pool_const, 1)
            pool.wait_ge(pool_const, 4)
            pool.affine_select(out=ident[:, :], in_=ident[:, :], compare_op=ALU.not_equal, fill=1.0, base=0,
                               pattern=[[-1, P]], channel_multiplier=1).then_inc(pool_const, 1)
            pool.affine_select(out=expert_rows[:, :], in_=expert_rows[:, :], compare_op=ALU.not_equal, fill=1.0,
                               base=0, pattern=[[-1, EXPERTS]], channel_multiplier=1).then_inc(pool_const, 1)
            pool.wait_ge(pool_const, 6)
            pool.affine_select(out=expert_rows[:, :], in_=expert_rows[:, :], compare_op=ALU.not_equal, fill=1.0,
                               base=-EXPERTS, pattern=[[-1, EXPERTS]], channel_multiplier=1).then_inc(pool_const, 1)
            pool.dma_start(bqk[:, :], bias0).then_inc(l_bias, 16)
            pool.dma_start(gains_raw[:, :], gains).then_inc(l_gains, 16)

            def power(k, src, dst, n):
                pool.wait_ge(v_pow, k + 1)
                pool.tensor_tensor(dst, src, minus_half[:, 0:n], ALU.pow).then_inc(g_pow, 1)

            power(0, vare[:, :], rstd[:, :], TILES)
            power(1, vare[:, :], rstd[:, :], TILES)
            power(2, tinyB[:, 0, :], tinyB[:, 1, :], TILES)
            power(3, tinyB[:, 5, :], tinyB[:, 6, :], TILES)
            power(4, vare[:, :], rstd[:, :], TILES)

            def rms(b, n):
                wait(pool, a_exp, n * 4 - 12)
                pool.wait_ge(v_msq, n + 1)
                pool.tensor_tensor(rqk[:, b, :], msq[:, :], minus_half[:, :], ALU.pow).then_inc(g_rms, 1)
                pool.wait_ge(g_rms, n + 1)
                k = k_raw[:, b % 2, :, :, :].rearrange("p t h d -> p (t h) d")
                pool.tensor_tensor(k, k, rqk[:, b, 4:8].unsqueeze(2).broadcast_to([P, 4, D]),
                                   ALU.mult).then_inc(g_kn, 1)

            def low_w(w, par):
                pool.wait_ge(a_Whi, w + 1)
                wait(pool, t_K, w * 4 - 4)
                wait(pool, t_Q, w * 4 - 4)
                pool.tensor_tensor(wqk_lo[:, par, :], wqk_raw[:, :], f(wqk_hi[:, par, :]),
                                   ALU.subtract).then_inc(g_Wlo, 1)

            low_w(0, 0)
            for n in range(4):
                rms(n, n)
            low_w(1, 1)

            def scale_pair(p, par, last=False):
                for b in range(BATCH):
                    rms(b, p * 4 + b)
                    if b == 2 and not last:
                        low_w(p + 1, 1 - par)

            with pool.Fori(1, PAIRS // 2) as i:
                scale_pair(i * 2 - 1, 1)
                scale_pair(i * 2, 0)
            scale_pair(PAIRS - 1, 1, last=True)
            power(5, vare[:, :], rstd[:, :], TILES)

        @block.tensor
        def _(pe):
            def transpose_rows(first, src, ready, free, count):
                for j in range(BATCH):
                    pe.wait_ge(ready, first * 8 + 2 * j + 2)
                    if first * 4 + j >= 2:
                        pe.wait_ge(free, first * 4 + j - 1)
                    for k in range(KH):
                        for t in range(2):
                            mm = pe.transpose(bank4(6 + j % 2)[:, k, t * P:(t + 1) * P],
                                              src[:, 2 * j + t, k * P:(k + 1) * P], ident[:, :])
                    mm.then_inc(count, 1)

            pe.wait_ge(l_ctxT, 16)
            pe.wait_ge(l_qk0, 16)
            for i in range(2):
                for h in range(2):
                    pe.matmul(bank[2 * i + h][:, :], wqk0[:, i, :], ctxT_raw[:, h * 512:(h + 1) * 512],
                              start=True, stop=True).then_inc(t_qkA, 1)
            pe.wait_ge(pool_const, 7)
            transpose_rows(0, u, v_u, c_u, t_u)

            def energy(b):
                pe.wait_ge(a_qkA, 4)
                if b >= 2:
                    pe.wait_ge(v_mA, b - 1)
                    pe.wait_ge(a_eA, 2 * (b - 1))
                for m in range(2):
                    c = b * SEQ + m * P
                    mm = pe.matmul(bank4(b % 2)[:, m, :], qkA[:, 0, c:c + P], qkA[:, 1, b * SEQ:(b + 1) * SEQ],
                                   start=True, stop=True)
                mm.then_inc(t_eA, 1)

            def turn_att(b):
                pe.wait_ge(v_nA, b + 1)
                if b >= 2:
                    pe.wait_ge(a_aA, b - 1)
                for j in range(2):
                    for m in range(2):
                        mm = pe.transpose(bank4(2 + b % 2)[:, j, m * P:(m + 1) * P],
                                          attA[:, b % 2, m, j * P:(j + 1) * P], ident[:, :])
                mm.then_inc(t_aA, 1)

            def mix(b):
                pe.wait_ge(a_aA, b + 1)
                pe.wait_ge(c_u, b + 1)
                if b >= 2:
                    pe.wait_ge(v_xA, b - 1)
                for t in range(2):
                    for j in range(2):
                        c = (2 * b + t) * P
                        mm = pe.matmul(bank4(4 + b % 2)[:, t, :], xT[:, j, c:c + P], attT[:, b % 2, j, :],
                                       start=j == 0, stop=j == 1)
                mm.then_inc(t_oA, 1)

            energy(0)
            energy(1)
            for b in range(BATCH):
                turn_att(b)
                mix(b)
                if b + 2 < BATCH:
                    energy(b + 2)

            pe.wait_ge(a_abs, 3)
            pe.wait_ge(v_xA, 4)
            pe.matmul(bank[7][:, 0:2], ones[:, :], absum[:, 0:2], start=True, stop=False, skip_group_check=True)
            pe.matmul(bank[7][:, 1:2], ones[0:TAIL, :], absum[0:TAIL, 2:3], start=False, stop=True,
                      skip_group_check=True).then_inc(t_abs, 1)

            def turn_q1(i):
                pe.wait_ge(v_q1, i + 1)
                if i >= 2:
                    pe.wait_ge(a_q1, i - 1)
                bk = bank[4 + i % 2][:, :].bitcast(BF16)
                for k in range(KH):
                    mm = pe.transpose(bk[:, k * P:(k + 1) * P], q1[:, i, k * P:(k + 1) * P], ident_b[:, :])
                mm.then_inc(t_q1, 1)

            def gate_up(i):
                pe.wait_ge(a_q1, i + 1)
                pe.wait_ge(v_gw, 1)
                if i >= 1:
                    pe.wait_ge(a_s1, i)
                for c in range(4):
                    if c == 2 and i >= 1:
                        pe.wait_ge(v_h1, 2 * i)
                    for k in range(KH):
                        mm = pe.matmul(bank[c][:, 0:HALF], qT[:, i % 2, k, :],
                                       gate_t[:, k, c * HALF:(c + 1) * HALF], start=k == 0, stop=k == KH - 1)
                mm.then_inc(t_y1, 1)

            pe.wait_ge(v_const, 3)
            turn_q1(0)
            for i in range(TILES):
                if i + 1 < TILES:
                    turn_q1(i + 1)
                gate_up(i)

            def turn_q2(i):
                pe.wait_ge(v_q2, i + 1)
                if i >= 2:
                    pe.wait_ge(a_q2, i - 1)
                bk = bank[6 + i % 2][:, :].bitcast(BF16)
                for k in range(KI):
                    n = P if k < 5 else TAIL
                    mm = pe.transpose(bk[0:n, k * P:(k + 1) * P], q2[:, i % 2, k * P:k * P + n], ident_b[:, :])
                mm.then_inc(t_q2, 1)

            def down(i):
                pe.wait_ge(a_q2, i + 1)
                pe.wait_ge(v_dw, 1)
                if i >= 2:
                    pe.wait_ge(v_xB, i - 1)
                for k in range(KI):
                    n = P if k < 5 else TAIL
                    mm = pe.matmul(bank[4 + i % 2][:, 0:HID], hT[0:n, i % 2, k, :], down_t[0:n, k, :],
                                   start=k == 0, stop=k == KI - 1)
                mm.then_inc(t_y2, 1)

            turn_q2(0)
            for i in range(TILES):
                if i + 1 < TILES:
                    turn_q2(i + 1)
                down(i)

            pe.wait_ge(v_xB, TILES)
            transpose_rows(1, u, v_u, c_u, t_u)
            pe.wait_ge(c_u, 8)
            pe.wait_ge(v_ctx, 2)

            def project(out, lhs_hi, lhs_lo, c, par, w0, k, last):
                return split_mm(pe, out, lhs_hi[:, c:c + P], lhs_lo[:, c:c + P], wqk_hi[:, par, w0:w0 + 256],
                                wqk_lo[:, par, w0:w0 + 256], k == 0, last)

            def proj_q(b, n, par, w):
                pe.wait_ge(g_Wlo, w)
                wait(pe, a_sqQ, n * 4)
                wait(pe, v_Qlo, n - 1)
                for t in range(2):
                    for k in range(KH):
                        mm = project(bank4(QBK)[:, t, :], xnT_hi[:, k, :], xnT_lo[:, k, :], (2 * b + t) * P, par,
                                     k * 256, k, k == KH - 1)
                mm.then_inc(t_Q, 1)

            def proj_k(b, n, par, w):
                pe.wait_ge(g_Wlo, w)
                wait(pe, a_rawK, n)
                wait(pe, v_Klo, n - 1)
                for t in range(2):
                    mm = project(bank4(KBK)[:, t, :], ctxT_hi, ctxT_lo, (2 * b + t) * P, par, 512, 0, True)
                mm.then_inc(t_K, 1)

            def turn_q(b, n, done):
                pe.wait_ge(a_sqQ, done * 4)
                pe.wait_ge(a_rawQ, n + 1)
                for h in range(2):
                    for t in range(2):
                        mm = pe.transpose(bank4(QBK)[:, h, t * P:(t + 1) * P], q_raw[:, b % 2, t, h, :],
                                          ident[:, :])
                mm.then_inc(t_TQ, 1)

            def turn_k(b, n, done):
                pe.wait_ge(a_rawK, done)
                pe.wait_ge(g_kn, n + 1)
                for h in range(2):
                    for t in range(2):
                        mm = pe.transpose(bank4(KBK)[:, h, t * P:(t + 1) * P], k_raw[:, b % 2, t, h, :],
                                          ident[:, :])
                mm.then_inc(t_TK, 1)

            def scores(b, g):
                pe.wait_ge(v_Qlo, g + 1)
                pe.wait_ge(v_Klo, g + 1)
                for h in range(2):
                    wait(pe, a_exp, g * 4 - 2 + 2 * h)
                    for t in range(2):
                        c = slice(t * P, (t + 1) * P)
                        mm = split_mm(pe, bank4(SBK[h])[:, t, :], qh[:, h, b, c], ql[:, h, b, c],
                                      kh[:, h, b, :], kl[:, h, b, :], True, True)
                    mm.then_inc(t_S, 1)

            def turn(b, g):
                pe.wait_ge(a_exp, g * 4 + 4)
                for j in range(2):
                    wait(pe, v_Tlo, g * 2 - 1 + j)
                    for h in range(2):
                        for t in range(2):
                            mm = pe.transpose(bank4(TBK[j])[:, h, t * P:(t + 1) * P],
                                              att[:, b % 2, h, t, j * P:(j + 1) * P], ident[:, :])
                    mm.then_inc(t_T, 1)

            def values(b, g):
                pe.wait_ge(v_Tlo, g * 2 + 2)
                wait(pe, v_Olo, g)
                for j in range(2):
                    mm = split_mm(pe, bank[OBK][:, :], ctx_hi[:, 2 * b + j, :], ctx_lo[:, 2 * b + j, :],
                                  attT_hi[:, j, :, :].rearrange("p h n -> p (h n)"),
                                  attT_lo[:, j, :, :].rearrange("p h n -> p (h n)"), j == 0, j == 1)
                mm.then_inc(t_O, 1)

            def output(g, h, p_m):
                pe.wait_ge(v_Olo, g + 1)
                pe.wait_ge(v_Mlo, p_m)
                wait(pe, v_Y, g * 4 + 2 * h)
                for t in range(2):
                    c = slice(t * P, (t + 1) * P)
                    mm = split_mm(pe, bank4(YBK)[:, t, :], o_hi[:, h, c], o_lo[:, h, c],
                                  m_hi[:, h, :], m_lo[:, h, :], True, True)
                mm.then_inc(t_Y, 1)

            def fuse_vo(p, g):
                pe.wait_ge(l_hvo, p * 16 + 16)
                wait(pe, v_Y, g * 4)
                for h in range(2):
                    mm = pe.matmul(bank4(YBK)[:, h, :], wvo_raw[:, h * P:(h + 1) * P],
                                   wvo_raw[:, 256 + h * 256:512 + h * 256], start=True, stop=True)
                mm.then_inc(t_M, 1)

            def pair(p, par, first=False, last=False):
                for b in range(BATCH):
                    g = p * 4 + b
                    n = g + 4
                    start = first and b == 0
                    turning = not (last and b >= 2)
                    if not (last and b == 3):
                        scores((b + 1) % 4, g + 1)
                    if turning:
                        turn_q((b + 2) % 4, n - 2, PIECES if last else n)
                    turn(b, g)
                    if not start:
                        output(g - 1, 0, p if b == 0 else p + 1)
                    if turning:
                        turn_k((b + 2) % 4, n - 2, PIECES if last else n)
                    if not last:
                        proj_q(b, n, 1 - par, p + 2)
                    values(b, g)
                    if not start:
                        output(g - 1, 1, p if b == 0 else p + 1)
                    if not last:
                        proj_k(b, n, 1 - par, p + 2)
                    if b == 0:
                        fuse_vo(p, g)

            proj_k(0, 0, 0, 1)
            proj_q(0, 0, 0, 1)
            proj_k(1, 1, 0, 1)
            proj_q(1, 1, 0, 1)
            for n in (2, 3):
                turn_q(n - 2, n - 2, n)
                turn_k(n - 2, n - 2, n)
                proj_q(n, n, 0, 1)
                proj_k(n, n, 0, 1)
            scores(0, 0)
            pair(0, 0, first=True)
            with pe.Fori(1, PAIRS // 2) as i:
                pair(i * 2 - 1, 1)
                pair(i * 2, 0)
            pair(PAIRS - 1, 1, last=True)
            for h in range(2):
                output(GROUPS - 1, h, PAIRS)

            transpose_rows(2, u, v_u, c_u, t_u)
            for j in range(BATCH):
                if j >= 2:
                    pe.wait_ge(a_xT, j - 1)
                else:
                    pe.wait_ge(v_Y, 4 * GROUPS)
                for k in range(KH):
                    for t in range(2):
                        mm = pe.transpose(bank4(4 + j % 2)[:, k, t * P:(t + 1) * P],
                                          x[:, 2 * j + t, k * P:(k + 1) * P], ident[:, :])
                mm.then_inc(t_xT, 1)
            pe.wait_ge(v_rw, 1)
            pe.wait_ge(c_u, 12)
            for i in range(TILES):
                for k in range(KH):
                    mm = split_mm(pe, bank[2 + i // 4][:, (i % 4) * LOGC:(i % 4 + 1) * LOGC],
                                  xnT_hi[:, k, i * P:(i + 1) * P], xnT_lo[:, k, i * P:(i + 1) * P],
                                  r_hi[:, k, :], r_lo[:, k, :], k == 0, k == KH - 1)
            mm.then_inc(t_log, 1)

            def gates(par, e, t, s, bk, part, first=False):
                if t == 0:
                    pe.wait_ge(v_Elo, e + 1)
                if not first:
                    pe.wait_ge(a_silu if part == 0 else v_mul1, s)
                for k in range(KH):
                    c = part * 256 + k * P
                    mm = split_mm(pe, bank[bk][:, :], e_hi[:, par, c:c + P], e_lo[:, par, c:c + P],
                                  xnT_hi[:, k, t * 512:(t + 1) * 512], xnT_lo[:, k, t * 512:(t + 1) * 512],
                                  k == 0, k == KH - 1)
                mm.then_inc(t_G if part == 0 else t_U, 1)

            def spread_w(par, e, t, s, first=False):
                pe.wait_ge(v_sel, e + 1)
                if not first:
                    pe.wait_ge(v_mul2, s)
                pe.matmul(bank[WB][:, :], selb[:, par, :], wT[:, t * 512:(t + 1) * 512],
                          start=True, stop=True).then_inc(t_W, 1)

            def experts_down(par, t, s, start=False):
                pe.wait_ge(v_Ilo, s + 1)
                for hb in range(2):
                    c = 512 + hb * P
                    mm = split_mm(pe, bank[ACC[hb][t]][:, :], e_hi[:, par, c:c + P], e_lo[:, par, c:c + P],
                                  inter_hi[:, t, :], inter_lo[:, t, :], start, False)
                mm.then_inc(t_D, 1)

            def turn_weights():
                pe.wait_ge(v_wcat, 1)
                for src, n, at in ((wcat, P, 3), (shcat, 2, 5)):
                    for i in range(TILES):
                        mm = pe.transpose(bank[at + i // 4][0:n, (i % 4) * P:(i % 4 + 1) * P], src[:, i, :],
                                          ident[:, :])
                        if i % 4 == 3:
                            mm.then_inc(t_wT, 1)

            def two_pairs(j, first=False):
                for par in range(2):
                    for t in range(2):
                        e = j * 2 + par
                        s = j * 4 + par * 2 + t
                        start = first and par == 0 and t == 0
                        gates(par, e, t, s, GB, 0, start)
                        gates(par, e, t, s, UB, 1, start)
                        if start:
                            turn_weights()
                            pe.wait_ge(v_wT, 2)
                        spread_w(par, e, t, s, start)
                        if not start:
                            pt = (par * 2 + t - 1) % 4
                            experts_down(pt // 2, pt % 2, s - 1, first and par * 2 + t <= 2)

            two_pairs(0, True)
            with pe.Fori(1, EPAIRS // 2) as j:
                two_pairs(j)
            pe.wait_ge(a_rw, 3)
            pe.wait_ge(v_rw, 3)
            for t in range(2):
                s = 2 * EPAIRS + t
                for part, bk, free, done in ((0, GB, a_silu, t_G), (1, UB, v_mul1, t_U)):
                    pe.wait_ge(free, s)
                    for k in range(KH):
                        mm = split_mm(pe, bank[bk][0:EI, :], s_hi[:, part, k, :], s_lo[:, part, k, :],
                                      xnT_hi[:, k, t * 512:(t + 1) * 512], xnT_lo[:, k, t * 512:(t + 1) * 512],
                                      k == 0, k == KH - 1)
                    mm.then_inc(done, 1)
                pe.wait_ge(v_mul2, s)
                pe.matmul(bank[WB][0:EI, :], ones_r[0:2, :], shT[:, t * 512:(t + 1) * 512], start=True,
                          stop=True).then_inc(t_W, 1)
                if t == 0:
                    experts_down(1, 1, s - 1)
            for t in range(2):
                pe.wait_ge(v_Ilo, 2 * EPAIRS + t + 1)
                for hb in range(2):
                    mm = split_mm(pe, bank[ACC[hb][t]][:, :], sdn_hi[:, hb * P:(hb + 1) * P],
                                  sdn_lo[:, hb * P:(hb + 1) * P], inter_hi[0:EI, t, :], inter_lo[0:EI, t, :],
                                  False, True)
                    mm.then_inc(t_D, 1)

        @block.scalar
        def _(act):
            def copy_rows(first, lo):
                for j in range(BATCH):
                    act.wait_ge(t_u, first * 4 + j + 1)
                    dst = xnT_hi if lo else xT
                    act.activation(dst[:, :, j * 256:(j + 1) * 256], bank4(6 + j % 2), ACT.Copy).then_inc(
                        a_u if lo else c_u, 1)

            act.wait_ge(l_gains, 16)
            act.activation(tg[:, :], gains_raw[:, :], ACT.Tanh).then_inc(a_tg, 1)
            act.wait_ge(l_bias, 16)
            for i in range(2):
                for h in range(2):
                    act.wait_ge(t_qkA, 2 * i + h + 1)
                    act.activation(qkA[:, i, h * 512:(h + 1) * 512], bank[2 * i + h][:, :], ACT.Identity,
                                   bias=bqk[:, i:i + 1]).then_inc(a_qkA, 1)
            copy_rows(0, False)

            def exp_A(b):
                act.wait_ge(v_mA, b + 1)
                if b >= 2:
                    act.wait_ge(t_aA, b - 1)
                for m in range(2):
                    act.activation(attA[:, b % 2, m, :], bank4(b % 2)[:, m, :], ACT.Exp, bias=nmA[:, b, m:m + 1],
                                   accum_out=sumA[:, b, m:m + 1]).then_inc(a_eA, 1)

            exp_A(0)
            exp_A(1)
            for b in range(BATCH):
                act.wait_ge(t_aA, b + 1)
                if b >= 2:
                    act.wait_ge(t_oA, b - 1)
                act.activation(attT[:, b % 2, :, :], bank4(2 + b % 2), ACT.Copy).then_inc(a_aA, 1)
                if b + 2 < BATCH:
                    exp_A(b + 2)
            act.wait_ge(l_gate, 16)
            act.activation(junk[:, :], gate_raw[:, :, :].rearrange("p k n -> p (k n)"), ACT.Abs,
                           accum_out=absum[:, 0:1]).then_inc(a_abs, 1)
            act.wait_ge(l_down, 16)
            act.wait_ge(a_abs, 1)
            act.activation(junk[:, 0:5 * HID], down_raw[:, 0:5, :].rearrange("p k n -> p (k n)"), ACT.Abs,
                           accum_out=absum[:, 1:2]).then_inc(a_abs, 1)
            act.wait_ge(l_tail, 16)
            act.wait_ge(a_abs, 2)
            act.activation(junk[0:TAIL, 0:HID], down_raw[0:TAIL, 5, :], ACT.Abs,
                           accum_out=absum[0:TAIL, 2:3]).then_inc(a_abs, 1)
            act.wait_ge(l_ctxT, 16)
            act.activation(ctxT_hi[:, :], ctxT_raw[:, :], ACT.Copy).then_inc(a_ctx, 1)
            act.wait_ge(l_ctx, 16)
            act.activation(ctx_hi[:, :, :], ctx_raw[:, :, :], ACT.Copy).then_inc(a_ctx, 1)

            def copy_q1(i):
                act.wait_ge(t_q1, i + 1)
                if i >= 2:
                    act.wait_ge(t_y1, i - 1)
                act.activation(qT[:, i % 2, :, :].rearrange("p k n -> p (k n)"),
                               bank[4 + i % 2][:, :].bitcast(BF16)[:, 0:HID], ACT.Copy).then_inc(a_q1, 1)

            copy_q1(0)
            for i in range(TILES):
                if i + 1 < TILES:
                    copy_q1(i + 1)
                act.wait_ge(t_y1, i + 1)
                if i >= 2:
                    act.wait_ge(v_h1, 2 * (i - 1))
                for c in range(2):
                    ins = act.activation(silu_g[:, i % 2, c * HALF:(c + 1) * HALF], bank[c][:, 0:HALF], ACT.Silu,
                                         scale=tinyB[:, 4, i:i + 1])
                ins.then_inc(a_s1, 1)
                if i >= 1:
                    act.wait_ge(v_h1, 2 * i)
                    act.activation(junk[:, 0:INTER], h_raw[:, (i - 1) % 2, :], ACT.Square,
                                   accum_out=sumh[:, i - 1:i]).then_inc(a_h1, 1)
                    act.wait_ge(a_h1, i)
            act.wait_ge(v_h1, 2 * TILES)
            act.activation(junk[:, 0:INTER], h_raw[:, 1, :], ACT.Square,
                           accum_out=sumh[:, TILES - 1:TILES]).then_inc(a_h1, 1)
            for i in range(TILES):
                act.wait_ge(t_q2, i + 1)
                if i >= 2:
                    act.wait_ge(t_y2, i - 1)
                bk = bank[6 + i % 2][:, :].bitcast(BF16)
                act.activation(hT[:, i % 2, 0:5, :].rearrange("p k n -> p (k n)"), bk[:, 0:5 * P], ACT.Copy)
                act.activation(hT[0:TAIL, i % 2, 5, :], bk[0:TAIL, 5 * P:6 * P], ACT.Copy).then_inc(a_q2, 1)

            copy_rows(1, True)

            def split_w(w, par):
                act.wait_ge(l_hqk, w * 16 + 16)
                wait(act, t_K, w * 4 - 4)
                wait(act, t_Q, w * 4 - 4)
                act.activation(wqk_hi[:, par, :], wqk_raw[:, :], ACT.Copy).then_inc(a_Whi, 1)

            def raw_q(b, n):
                act.wait_ge(t_Q, n + 1)
                wait(act, t_TQ, n - 1)
                act.activation(q_raw[:, b % 2, :, :, :].rearrange("p t h d -> p (t h d)"), bank[QBK][:, :],
                               ACT.Copy).then_inc(a_rawQ, 1)

            def square_q(b, n):
                act.wait_ge(a_rawQ, n + 1)
                wait(act, v_msq, n - 1)
                for c in range(4):
                    sq = bank[QBK][:, c * D:(c + 1) * D]
                    act.activation(sq, sq, ACT.Square,
                                   accum_out=ssq[:, b % 2, c:c + 1]).then_inc(a_sqQ, 1)

            def raw_k(b, n):
                act.wait_ge(t_K, n + 1)
                wait(act, t_TK, n - 1)
                act.activation(k_raw[:, b % 2, :, :, :].rearrange("p t h d -> p (t h d)"), bank[KBK][:, :],
                               ACT.Copy).then_inc(a_rawK, 1)

            def high_q(b, n):
                act.wait_ge(t_TQ, n + 1)
                wait(act, t_S, n * 2 - 6)
                act.activation(qh[:, :, b, :], bank4(QBK), ACT.Copy).then_inc(a_hiQ, 1)

            def high_k(b, n):
                act.wait_ge(t_TK, n + 1)
                wait(act, t_S, n * 2 - 6)
                act.activation(kh[:, :, b, :], bank4(KBK), ACT.Copy, scale=gk[:, 0:1]).then_inc(a_hiK, 1)

            def exps(b, g, h):
                act.wait_ge(v_shift_c, g + 1)
                wait(act, t_T, g * 2 - 2)
                for t in range(2):
                    act.activation(att[:, b % 2, h, t, :], bank4(SBK[h])[:, t, :], ACT.Exp,
                                   bias=shift[:, b % 2, t, h:h + 1], scale=rqk[:, b, t * 2 + h:t * 2 + h + 1],
                                   accum_out=rowsum[:, b % 2, t, h:h + 1]).then_inc(a_exp, 1)

            def high_m(p, g):
                act.wait_ge(t_M, p + 1)
                wait(act, t_Y, g * 2)
                act.activation(m_hi[:, :, :], bank4(YBK), ACT.Copy, scale=tg[:, 1:2]).then_inc(a_Mhi, 1)

            def pair(p, par, last=False, more=True):
                for b in range(BATCH):
                    g = p * 4 + b
                    n = g + 4
                    if not (last and b >= 2):
                        high_q((b + 2) % 4, n - 2)
                    for j in range(2):
                        act.wait_ge(t_T, g * 2 + j + 1)
                        wait(act, t_O, g)
                        act.activation(attT_hi[:, j, :, :], bank4(TBK[j]), ACT.Copy).then_inc(a_Thi, 1)
                    if not (last and b >= 2):
                        high_k((b + 2) % 4, n - 2)
                    if not (last and b == 3):
                        exps((b + 1) % 4, g + 1, 0)
                    if not last:
                        raw_q(b, n)
                    if not (last and b == 3):
                        exps((b + 1) % 4, g + 1, 1)
                    if not last:
                        square_q(b, n)
                    act.wait_ge(t_O, g + 1)
                    wait(act, t_Y, g * 2)
                    act.activation(o_hi[:, :, :], bank4(OBK), ACT.Copy).then_inc(a_Ohi, 1)
                    if not last:
                        raw_k(b, n)
                    if b == 0:
                        high_m(p, g)
                    if b == 1 and more:
                        split_w(p + 2, par)

            split_w(0, 0)
            act.wait_ge(v_gk, 1)
            for n in range(4):
                if n >= 2:
                    high_q(n - 2, n - 2)
                    high_k(n - 2, n - 2)
                    raw_q(n, n)
                    square_q(n, n)
                    raw_k(n, n)
                else:
                    raw_k(n, n)
                    raw_q(n, n)
                    square_q(n, n)
            for h in range(2):
                exps(0, 0, h)
            split_w(1, 1)
            pair(0, 0)
            pair(1, 1)
            with act.Fori(1, PAIRS // 2 - 1) as i:
                pair(i * 2, 0)
                pair(i * 2 + 1, 1)
            pair(PAIRS - 2, 0, more=False)
            pair(PAIRS - 1, 1, last=True, more=False)

            copy_rows(2, True)
            for j in range(BATCH):
                act.wait_ge(t_xT, j + 1)
                act.activation(xT[:, :, j * 256:(j + 1) * 256], bank4(4 + j % 2), ACT.Copy).then_inc(a_xT, 1)
            act.wait_ge(l_router, 16)
            act.activation(r_hi[:, :, :], r_raw[:, :, :], ACT.Copy).then_inc(a_rw, 1)

            def split_e(par, e, turn, first=False):
                act.wait_ge(l_exp[par], turn * 16 + 16)
                if not first:
                    act.wait_ge(t_D, e * 2 - 2)
                act.activation(e_hi[:, par, :], e_raw[:, par, :], ACT.Copy).then_inc(a_Ehi, 1)

            split_e(0, 0, 0, True)
            act.wait_ge(v_shift, 1)
            act.activation(wexp[:, :, :], shifted[:, :, :], ACT.Exp).then_inc(a_wexp, 1)
            act.activation(shg[:, :], logits[:, :, EXPERTS], ACT.Tanh, scale=0.5).then_inc(a_wexp, 1)
            act.wait_ge(l_shared, 16)
            act.activation(s_hi[:, :, :, :], s_raw[:, :, :, :], ACT.Copy).then_inc(a_rw, 1)
            act.wait_ge(l_shdown, 16)
            act.activation(sdn_hi[:, :], sdn_raw[:, :], ACT.Copy).then_inc(a_rw, 1)

            def silu_step(t, s, early, rows):
                act.wait_ge(t_G, s + 1)
                if not early:
                    act.wait_ge(v_mul1, s - 1)
                act.activation(gate_s[0:rows, t, :], bank[GB][0:rows, :], ACT.Silu).then_inc(a_silu, 1)
                act.wait_ge(v_mul2, s + 1)
                if not early:
                    act.wait_ge(t_D, s - 1)
                act.activation(inter_hi[0:rows, t, :], inter[0:rows, t, :], ACT.Copy).then_inc(a_Ihi, 1)

            def two_pairs(j, first=False, last=False):
                for par in range(2):
                    for t in range(2):
                        silu_step(t, j * 4 + par * 2 + t, first and par == 0, P)
                        if t == 0 and not (last and par == 1):
                            split_e(1 - par, j * 2 + par + 1, j + par, first and par == 0)

            two_pairs(0, first=True)
            with act.Fori(1, EPAIRS // 2 - 1) as j:
                two_pairs(j)
            two_pairs(EPAIRS // 2 - 1, last=True)
            for t in range(2):
                silu_step(t, 2 * EPAIRS + t, False, EI)

        @block.vector
        def _(dve):
            def ask_pow():
                pow_n[0] += 1
                dve.wait_ge(g_pow, pow_n[0])

            def row_stats():
                for i in range(TILES):
                    ins = dve.bn_stats(stats[:, i, :], x[:, i, :])
                link(dve, ins)
                for i in range(TILES):
                    ins = dve.bn_aggr(mv[:, i, :], stats[:, i, :])
                link(dve, ins)
                dve.tensor_scalar(vare[:, :], mv[:, :, 1], EPS, None, ALU.add).then_inc(v_pow, 1)
                ask_pow()

            def normalise():
                for i in range(TILES):
                    dve.tensor_scalar(u[:, i, :], x[:, i, :], mv[:, i, 0:1], rstd[:, i:i + 1], ALU.subtract,
                                      ALU.mult).then_inc(v_u, 1)

            def low_rows(first):
                for j in range(BATCH):
                    dve.wait_ge(a_u, (first - 1) * 4 + j + 1)
                    c = slice(j * 256, (j + 1) * 256)
                    dve.tensor_tensor(xnT_lo[:, :, c], bank4(6 + j % 2), f(xnT_hi[:, :, c]),
                                      ALU.subtract).then_inc(c_u, 1)

            dve.wait_ge(l_x, 32)
            row_stats()
            normalise()
            dve.wait_ge(pool_const, 7)
            dve.tensor_copy(ident_r[:, :], ident[:, :]).then_inc(v_const, 1)
            dve.tensor_copy(ident_b[:, :], ident[:, :]).then_inc(v_const, 1)
            dve.tensor_copy(ones_r[:, :], ones[:, 0:EI]).then_inc(v_const, 1)

            def max_A(b):
                dve.wait_ge(t_eA, b + 1)
                dve.tensor_reduce(nmA[:, b, :], bank4(b % 2), AX.X, ALU.max, negate=True).then_inc(v_mA, 1)

            max_A(0)
            for b in range(BATCH):
                if b + 1 < BATCH:
                    max_A(b + 1)
                dve.wait_ge(a_eA, 2 * b + 2)
                link(dve, dve.reciprocal(invA[:, b, :], sumA[:, b, :]))
                for m in range(2):
                    ins = dve.tensor_scalar(attA[:, b % 2, m, :], attA[:, b % 2, m, :], invA[:, b, m:m + 1], None,
                                            ALU.mult)
                ins.then_inc(v_nA, 1)
                dve.wait_ge(t_oA, b + 1)
                if b == 0:
                    dve.wait_ge(a_tg, 1)
                xb = x[:, 2 * b:2 * b + 2, :]
                dve.scalar_tensor_tensor(xb, bank4(4 + b % 2), tg[:, 0:1], xb, ALU.mult, ALU.add).then_inc(v_xA, 1)

            dve.wait_ge(t_abs, 1)
            for i, n in enumerate((2 * INTER * HID, INTER * HID)):
                ins = dve.tensor_scalar(wsc[:, i:i + 1], bank[7][:, i:i + 1], 1.0 / n, EPS, ALU.mult, ALU.max)
            link(dve, ins)
            link(dve, dve.reciprocal(wsi[:, :], wsc[:, :]))

            def ternary(dst, src, scale, done):
                link(dve, dve.tensor_scalar(src, src, scale, 1.0, ALU.mult, ALU.min))
                link(dve, dve.tensor_scalar(src, src, -1.0, MAGIC, ALU.max, ALU.add))
                ins = dve.tensor_scalar(dst, src, MAGIC, None, ALU.subtract)
                if done is None:
                    return
                ins.then_inc(done, 1)

            dve.wait_ge(a_abs, 3)
            ternary(gate_t[:, :, :], gate_raw[:, :, :], wsi[:, 0:1], v_gw)
            ternary(down_t[0:TAIL, 5, :], down_raw[0:TAIL, 5, :], wsi[0:TAIL, 1:2], None)
            ternary(down_t[:, 0:5, :], down_raw[:, 0:5, :], wsi[:, 1:2], v_dw)
            dve.wait_ge(v_xA, 4)
            row_stats()
            T = tinyB
            link(dve, dve.tensor_tensor(T[:, 2, :], mv[:, :, 1], rstd[:, :], ALU.mult))
            link(dve, dve.tensor_tensor(T[:, 3, :], T[:, 2, :], rstd[:, :], ALU.mult))
            dve.tensor_scalar(T[:, 0, :], T[:, 3, :], EPS, None, ALU.add).then_inc(v_pow, 1)
            dve.wait_ge(l_g1, 16)
            for i in range(TILES):
                ins = dve.scalar_tensor_tensor(w1[:, i, :], x[:, i, :], mv[:, i, 0:1], g1[:, :], ALU.subtract,
                                               ALU.mult)
            link(dve, ins)
            ask_pow()
            link(dve, dve.tensor_tensor(T[:, 2, :], T[:, 1, :], rstd[:, :], ALU.mult))
            link(dve, dve.tensor_reduce(T[:, 3, :], w1[:, :, :], AX.X, ALU.max, apply_absolute_value=True))
            link(dve, dve.tensor_tensor(T[:, 5, :], T[:, 3, :], T[:, 2, :], ALU.mult))
            link(dve, dve.tensor_scalar(T[:, 6, :], T[:, 5, :], EPS, None, ALU.max))
            link(dve, dve.reciprocal(T[:, 7, :], T[:, 6, :]))
            link(dve, dve.scalar_tensor_tensor(T[:, 3, :], T[:, 7, :], 127.0, T[:, 2, :], ALU.mult, ALU.mult))
            link(dve, dve.tensor_scalar(T[:, 4, :], T[:, 6, :], 1.0 / 127.0, wsc[:, 0:1], ALU.mult, ALU.mult))
            for i in range(TILES):
                ins = dve.tensor_scalar(w1[:, i, :], w1[:, i, :], T[:, 3, i:i + 1], MAGIC, ALU.mult, ALU.add)
            link(dve, ins)
            for i in range(TILES):
                dve.tensor_scalar(q1[:, i, :], w1[:, i, :], MAGIC, None, ALU.subtract).then_inc(v_q1, 1)
            dve.wait_ge(l_g2, 16)
            for i in range(TILES):
                dve.wait_ge(a_s1, i + 1)
                if i >= 2:
                    dve.wait_ge(a_h1, i - 1)
                for c in range(2):
                    cs = slice(c * HALF, (c + 1) * HALF)
                    dve.scalar_tensor_tensor(h_raw[:, i % 2, cs], bank[2 + c][:, 0:HALF], T[:, 4, i:i + 1],
                                             silu_g[:, i % 2, cs], ALU.mult, ALU.mult).then_inc(v_h1, 1)
                dve.wait_ge(v_h1, 2 * i + 2)
                link(dve, dve.tensor_tensor(w2[:, i, :], h_raw[:, i % 2, :], g2[:, :], ALU.mult))
                ins = dve.tensor_reduce(amax2[:, i:i + 1], w2[:, i, :], AX.X, ALU.max, apply_absolute_value=True)
            link(dve, ins)
            dve.wait_ge(a_h1, TILES)
            dve.tensor_scalar(T[:, 5, :], sumh[:, :], 1.0 / INTER, EPS, ALU.mult, ALU.add).then_inc(v_pow, 1)
            ask_pow()
            link(dve, dve.tensor_tensor(T[:, 2, :], T[:, 6, :], amax2[:, :], ALU.mult))
            link(dve, dve.tensor_scalar(T[:, 3, :], T[:, 2, :], EPS, None, ALU.max))
            link(dve, dve.reciprocal(T[:, 7, :], T[:, 3, :]))
            link(dve, dve.scalar_tensor_tensor(T[:, 2, :], T[:, 7, :], 127.0, T[:, 6, :], ALU.mult, ALU.mult))
            link(dve, dve.tensor_scalar(T[:, 5, :], T[:, 3, :], 1.0 / 127.0, wsc[:, 1:2], ALU.mult, ALU.mult))
            link(dve, dve.tensor_scalar(T[:, 7, :], T[:, 5, :], tg[:, 2:3], None, ALU.mult))

            def add_down(i):
                dve.wait_ge(t_y2, i + 1)
                dve.scalar_tensor_tensor(x[:, i, :], bank[4 + i % 2][:, 0:HID], T[:, 7, i:i + 1], x[:, i, :],
                                         ALU.mult, ALU.add).then_inc(v_xB, 1)

            for i in range(TILES):
                link(dve, dve.tensor_scalar(w2[:, i, :], w2[:, i, :], T[:, 2, i:i + 1], MAGIC, ALU.mult, ALU.add))
                if i >= 2:
                    dve.wait_ge(t_q2, i - 1)
                dve.tensor_scalar(q2[:, i % 2, :], w2[:, i, :], MAGIC, None, ALU.subtract).then_inc(v_q2, 1)
                if i:
                    add_down(i - 1)
            add_down(TILES - 1)
            dve.wait_ge(a_ctx, 2)
            dve.tensor_tensor(ctxT_lo[:, :], ctxT_raw[:, :], f(ctxT_hi[:, :]), ALU.subtract).then_inc(v_ctx, 1)
            dve.tensor_tensor(ctx_lo[:, :, :], ctx_raw[:, :, :], f(ctx_hi[:, :, :]), ALU.subtract).then_inc(v_ctx, 1)
            dve.wait_ge(l_gqk, 16)
            dve.tensor_scalar(gk[:, :], gqk_raw[:, 0:1], gqk_raw[:, 1:2], float(D) ** -0.5, ALU.mult,
                              ALU.mult).then_inc(v_gk, 1)

            dve.wait_ge(v_xB, TILES)
            row_stats()
            normalise()

            def low_q(b, n):
                dve.wait_ge(a_hiQ, n + 1)
                dve.tensor_tensor(ql[:, :, b, :], bank4(QBK), f(qh[:, :, b, :]), ALU.subtract).then_inc(v_Qlo, 1)

            def low_k(b, n):
                dve.wait_ge(a_hiK, n + 1)
                dve.scalar_tensor_tensor(kl[:, :, b, :], bank4(KBK), gk[:, 0:1], f(kh[:, :, b, :]), ALU.mult,
                                         ALU.subtract).then_inc(v_Klo, 1)

            def mean_squares(b, n):
                dve.wait_ge(a_rawK, n + 1)
                wait(dve, v_sqK, n * 4)
                for c in range(4):
                    k = k_raw[:, b % 2, c // 2, c % 2, :]
                    dve.tensor_tensor_reduce(out=k_sq[:, c // 2, c % 2, :], in0=k, in1=k, scale=1.0, scalar=0.0,
                                             op0=ALU.mult, op1=ALU.add,
                                             accum_out=ssq[:, b % 2, 4 + c:5 + c]).then_inc(v_sqK, 1)
                dve.wait_ge(a_sqQ, n * 4 + 4)
                wait(dve, g_rms, n)
                dve.wait_ge(v_sqK, n * 4 + 4)
                dve.tensor_scalar(msq[:, :], ssq[:, b % 2, :], 1.0 / D, EPS, ALU.mult, ALU.add).then_inc(v_msq, 1)

            def row_max(b, g, h):
                dve.wait_ge(t_S, g * 2 + h + 1)
                wait(dve, a_exp, g * 4 - 4)
                dve.tensor_reduce(rowmax[:, b % 2, :, h], bank4(SBK[h]), AX.X, ALU.max,
                                  negate=True).then_inc(v_max, 1)

            def row_shift(b, g):
                dve.wait_ge(v_max, g * 2 + 2)
                dve.wait_ge(g_rms, g + 1)
                dve.tensor_tensor(shift[:, b % 2, :, :].rearrange("p t h -> p (t h)"),
                                  rowmax[:, b % 2, :, :].rearrange("p t h -> p (t h)"), rqk[:, b, 0:4],
                                  ALU.mult).then_inc(v_shift_c, 1)

            def low_att(g, j):
                dve.wait_ge(a_Thi, g * 2 + j + 1)
                dve.tensor_tensor(attT_lo[:, j, :, :], bank4(TBK[j]), f(attT_hi[:, j, :, :]),
                                  ALU.subtract).then_inc(v_Tlo, 1)

            def row_inverse(b, g):
                dve.wait_ge(a_exp, g * 4 + 4)
                wait(dve, v_Y, g * 4 - 12)
                dve.reciprocal(rowinv[:, b, :, :], rowsum[:, b % 2, :, :]).then_inc(v_inv, 1)

            def add_output(b, g, h):
                dve.wait_ge(t_Y, g * 2 + h + 1)
                if h == 0:
                    dve.wait_ge(v_inv, g + 1)
                wait(dve, v_Y, g * 4 + 2 * h)
                for t in range(2):
                    xb = x[:, 2 * b + t, :]
                    dve.scalar_tensor_tensor(xb, bank4(YBK)[:, t, :], rowinv[:, b, t, h:h + 1], xb, ALU.mult,
                                             ALU.add).then_inc(v_Y, 1)

            def low_o(g):
                dve.wait_ge(a_Ohi, g + 1)
                dve.tensor_tensor(o_lo[:, :, :], bank4(OBK), f(o_hi[:, :, :]), ALU.subtract).then_inc(v_Olo, 1)

            def low_m(p):
                dve.wait_ge(a_Mhi, p + 1)
                dve.scalar_tensor_tensor(m_lo[:, :, :], bank4(YBK), tg[:, 1:2], f(m_hi[:, :, :]), ALU.mult,
                                         ALU.subtract).then_inc(v_Mlo, 1)

            def pair(p, first=False, last=False):
                for b in range(BATCH):
                    g = p * 4 + b
                    n = g + 4
                    start = first and b == 0
                    final_group = last and b == 3
                    turning = not (last and b >= 2)
                    if not final_group:
                        row_max((b + 1) % 4, g + 1, 0)
                    if not start:
                        low_o(g - 1)
                    if b == 1:
                        low_m(p)
                    if not final_group:
                        row_max((b + 1) % 4, g + 1, 1)
                    if turning:
                        low_q((b + 2) % 4, n - 2)
                    low_att(g, 0)
                    if not final_group:
                        row_shift((b + 1) % 4, g + 1)
                    low_att(g, 1)
                    if not start:
                        add_output((b + 3) % 4, g - 1, 0)
                    if turning:
                        low_k((b + 2) % 4, n - 2)
                    if not (last and b > 0):
                        mean_squares((b + 3) % 4, n - 1)
                    if not final_group:
                        row_inverse((b + 1) % 4, g + 1)
                    if not start:
                        add_output((b + 3) % 4, g - 1, 1)

            low_rows(1)
            for n in range(4):
                if n >= 2:
                    low_q(n - 2, n - 2)
                    low_k(n - 2, n - 2)
                if n < 3:
                    mean_squares(n, n)
            for h in range(2):
                row_max(0, 0, h)
            row_shift(0, 0)
            row_inverse(0, 0)
            pair(0, first=True)
            with dve.Fori(1, PAIRS - 1) as p:
                pair(p)
            pair(PAIRS - 1, last=True)
            low_o(GROUPS - 1)
            for h in range(2):
                add_output(3, GROUPS - 1, h)
            dve.wait_ge(v_Y, 4 * GROUPS)

            row_stats()
            normalise()
            low_rows(2)
            dve.wait_ge(a_rw, 1)
            dve.tensor_tensor(r_lo[:, :, :], r_raw[:, :, :], f(r_hi[:, :, :]), ALU.subtract).then_inc(v_rw, 1)

            def low_e(par, e):
                dve.wait_ge(a_Ehi, e + 1)
                dve.tensor_tensor(e_lo[:, par, :], e_raw[:, par, :], f(e_hi[:, par, :]),
                                  ALU.subtract).then_inc(v_Elo, 1)

            def select(par, e, first=False):
                if not first:
                    dve.wait_ge(t_W, e * 2 - 2)
                dve.tensor_copy(selb[:, par, :].rearrange("p (a n) -> p a n", a=2),
                                expert_rows[:, bass.ds(e * 2, 2)].unsqueeze(2).broadcast_to([P, 2, EI])
                                ).then_inc(v_sel, 1)

            low_e(0, 0)
            select(0, 0, True)
            dve.wait_ge(t_log, 1)
            for i in range(2):
                ins = dve.tensor_copy(logits[:, 4 * i:4 * i + 4, :],
                                      bank[2 + i][:, 0:4 * LOGC].rearrange("p (i n) -> p i n", i=4))
            link(dve, ins)
            for i in range(TILES):
                ins = dve.max(top8[:, i, :], logits[:, i, 0:EXPERTS])
            link(dve, ins)
            lg = logits[:, :, 0:EXPERTS]
            dve.tensor_tensor(shifted[:, :, :], lg, top8[:, :, 0:1].broadcast_to([P, TILES, EXPERTS]),
                              ALU.subtract).then_inc(v_shift, 1)
            for i in range(TILES):
                ins = dve.match_replace(out=struck[:, i, :], in_to_replace=top8[:, i, :],
                                        in_values=logits[:, i, 0:EXPERTS], imm_value=LOWEST)
            link(dve, ins)
            link(dve, dve.tensor_tensor(chosen[:, :, :], struck[:, :, :], lg, ALU.not_equal))
            dve.wait_ge(a_wexp, 2)
            link(dve, dve.tensor_tensor(chosen[:, :, :], chosen[:, :, :], wexp[:, :, :], ALU.mult))
            link(dve, dve.tensor_reduce(wsum[:, :], chosen[:, :, :], AX.X, ALU.add))
            link(dve, dve.reciprocal(winv[:, :], wsum[:, :]))
            link(dve, dve.tensor_tensor(chosen[:, :, :], chosen[:, :, :],
                                        winv[:, :].unsqueeze(2).broadcast_to([P, TILES, EXPERTS]), ALU.mult))
            link(dve, dve.tensor_copy(wcat[:, :, 0:EXPERTS].bitcast(F32R), chosen[:, :, :]))
            dve.tensor_tensor(wcat[:, :, EXPERTS:P].bitcast(F32R), chosen[:, :, :], wcat[:, :, 0:EXPERTS],
                              ALU.subtract)
            link(dve, dve.tensor_scalar(shg[:, :], shg[:, :], 0.5, 0.5, ALU.mult, ALU.add))
            link(dve, dve.tensor_copy(shcat[:, :, 0].bitcast(F32R), shg[:, :]))
            dve.tensor_tensor(shcat[:, :, 1].bitcast(F32R), shg[:, :], shcat[:, :, 0],
                              ALU.subtract).then_inc(v_wcat, 1)
            for i in range(2):
                dve.wait_ge(t_wT, i + 1)
                dve.tensor_copy(wT[:, i * 512:(i + 1) * 512], bank[3 + i][:, :])
            for i in range(2):
                dve.wait_ge(t_wT, 3 + i)
                dve.tensor_copy(shT[:, i * 512:(i + 1) * 512], bank[5 + i][0:2, :]).then_inc(v_wT, 1)
            dve.wait_ge(a_rw, 3)
            dve.tensor_tensor(s_lo[:, :, :, :], s_raw[:, :, :, :], f(s_hi[:, :, :, :]),
                              ALU.subtract).then_inc(v_rw, 1)
            dve.tensor_tensor(sdn_lo[:, :], sdn_raw[:, :], f(sdn_hi[:, :]), ALU.subtract).then_inc(v_rw, 1)

            def weigh(t, s, early, rows):
                dve.wait_ge(a_silu, s + 1)
                dve.wait_ge(t_U, s + 1)
                dve.tensor_tensor(prod[0:rows, t, :], gate_s[0:rows, t, :], bank[UB][0:rows, :],
                                  ALU.mult).then_inc(v_mul1, 1)
                dve.wait_ge(v_mul1, s + 1)
                dve.wait_ge(t_W, s + 1)
                if not early:
                    dve.wait_ge(a_Ihi, s - 1)
                dve.tensor_tensor(inter[0:rows, t, :], prod[0:rows, t, :], bank[WB][0:rows, :],
                                  ALU.mult).then_inc(v_mul2, 1)
                dve.wait_ge(a_Ihi, s + 1)
                dve.tensor_tensor(inter_lo[0:rows, t, :], inter[0:rows, t, :], f(inter_hi[0:rows, t, :]),
                                  ALU.subtract).then_inc(v_Ilo, 1)

            def two_pairs(j, first=False, last=False):
                for par in range(2):
                    for t in range(2):
                        weigh(t, j * 4 + par * 2 + t, first and par == 0, P)
                        if t == 0 and not (last and par == 1):
                            low_e(1 - par, j * 2 + par + 1)
                            select(1 - par, j * 2 + par + 1, first and par == 0)

            two_pairs(0, first=True)
            with dve.Fori(1, EPAIRS // 2 - 1) as j:
                two_pairs(j)
            two_pairs(EPAIRS // 2 - 1, last=True)
            for t in range(2):
                weigh(t, 2 * EPAIRS + t, False, EI)
            for t in range(2):
                for hb in range(2):
                    dve.wait_ge(t_D, 2 * EPAIRS + 2 * t + hb + 1)
                    dve.scalar_tensor_tensor(final[:, hb, t, :], bank[ACC[hb][t]][:, :], tg[:, 3:4],
                                             xT[:, hb, t * 512:(t + 1) * 512], ALU.mult, ALU.add).then_inc(v_out, 1)


def kernel(**inputs):
    import numpy as np
    import concourse.bacc as bacc
    from concourse.bass_utils import run_bass_kernel_spmd

    a = {k: np.asarray(v) for k, v in inputs.items()}

    def tiles(v):
        return v.reshape(TILES, P, v.shape[-1]).transpose(1, 0, 2)

    def parts(v):
        return v.reshape(-1, P, v.shape[-1]).transpose(1, 0, 2)

    ctx2 = a["ctx_1024"].reshape(TOK, CDIM)
    wq = a["L1_xattn_Wq"].reshape(KH, P, PAIRS, 2, D).transpose(2, 1, 0, 3, 4).reshape(PAIRS, P, 512)
    wk = a["L1_xattn_Wk"].reshape(P, PAIRS, 2 * D).transpose(1, 0, 2)
    wv = a["L1_xattn_Wv"].reshape(CDIM, PAIRS, 2, D).transpose(1, 3, 2, 0).reshape(PAIRS, D, 2 * CDIM)
    wo = a["L1_xattn_Wo"].reshape(PAIRS, 2, D, HID).transpose(0, 2, 1, 3).reshape(PAIRS, D, 2 * HID)
    gu = a["L1_ffn_gu_w"].reshape(EPAIRS, 2, 2, EI, KH, P).transpose(0, 5, 2, 4, 1, 3).reshape(EPAIRS, P, 512)
    dp = a["L1_ffn_dp_w"].reshape(EPAIRS, 2, HID, EI).transpose(0, 1, 3, 2).reshape(EPAIRS, P, HID)
    router = np.concatenate([a["L1_ffn_gate_w"], a["L1_ffn_sh_gate1_w"],
                             np.zeros((1, HID), np.float32)], 0).T
    downT = a["L0_ffn_down_w"].T
    arrays = {
        "x_tok": tiles(a["x"].reshape(TOK, HID)),
        "ctx_tok": tiles(ctx2),
        "ctxT": ctx2.T,
        "qk0": np.stack([a["L0_xattn_Wq"].T, a["L0_xattn_Wk"].T], 1),
        "bias0": np.stack([a["L0_xattn_bq"], a["L0_xattn_bk"]], 1),
        "gains": np.broadcast_to(np.concatenate([a["g_xattn"], a["g_ffn"]])[None, :], (P, 4)),
        "gate_wT": parts(a["L0_ffn_gate_w"].T),
        "down_wT": parts(downT[:5 * P]),
        "down_tail": downT[5 * P:],
        "norm_g1": a["L0_ffn_gate_norm_w"],
        "norm_g2": a["L0_ffn_down_norm_w"],
        "gqk": np.stack([a["L1_xattn_gq"], a["L1_xattn_gk"]], 1),
        "head_qk": np.concatenate([wq, wk], 2),
        "head_vo": np.concatenate([wv, wo], 2),
        "router_w": parts(router),
        "expert_w": np.concatenate([gu, dp], 2),
        "shared_w": np.stack([parts(a["L1_ffn_sh_gate_w"].T), parts(a["L1_ffn_sh_up_w"].T)], 1),
        "shared_down": a["L1_ffn_sh_down_w"].T,
    }
    arrays = {k: np.ascontiguousarray(v) for k, v in arrays.items()}
    nc = bacc.Bacc("TRN2", target_bir_lowering=False, num_devices=1)
    aps = [nc.dram_tensor(f"in_{k}", v.shape, mybir.dt.from_np(v.dtype), kind="ExternalInput").ap()
           for k, v in arrays.items()]
    out = nc.dram_tensor("outT", (KH, P, TOK), F32, kind="ExternalOutput").ap()
    flamingo_kernel(nc, *aps, out)
    r = run_bass_kernel_spmd(nc, [{f"in_{k}": v for k, v in arrays.items()}], core_ids=[0])
    outT = r.results[0]["outT"]
    return np.ascontiguousarray(outT.reshape(HID, TOK).T).reshape(BATCH, SEQ, HID)
```

```python
from contextlib import ExitStack

import concourse.bass as bass
from concourse import mybir

F32 = mybir.dt.float32
F32R = mybir.dt.float32r
BF16 = mybir.dt.bfloat16
ALU = mybir.AluOpType
ACT = mybir.ActivationFunctionType
AX = mybir.AxisListType

P = 128
BATCH, SEQ, HID, CDIM = 4, 256, 256, 128
TOK = BATCH * SEQ
TILES = TOK // P
KH = HID // P
INTER = 704
HALF = INTER // 2
KI = 6
TAIL = INTER - 5 * P
HEADS, D = 16, 128
PAIRS = HEADS // 2
GROUPS = PAIRS * BATCH
PIECES = GROUPS
EXPERTS, TOPK, EI = 64, 8, 64
EPAIRS = EXPERTS // 2
LOGC = 66
EPS = 1e-5
MAGIC = 12582912.0
LOWEST = -3.0e38


def flamingo_kernel(nc, x_tok, ctx_tok, ctxT, qk0, bias0, gains, gate_wT, down_wT, down_tail,
                    norm_g1, norm_g2, gqk, head_qk, head_vo, router_w, expert_w, shared_w,
                    shared_down, outT, w_rows):
    with ExitStack() as ctx:
        def sb(name, shape, dt=F32):
            return ctx.enter_context(nc.sbuf_tensor(name, shape, dt))

        def sem(name):
            return ctx.enter_context(nc.semaphore(name))

        bank = [ctx.enter_context(nc.psum_tensor(f"bank{i}", [P, 512], F32)) for i in range(8)]

        def wait(engine, semaphore, value):
            if not (isinstance(value, int) and value <= 0):
                engine.wait_ge(semaphore, value)

        ident = sb("ident", [P, P])
        ident_b = sb("ident_b", [P, P], BF16)
        ones = sb("ones", [P, P])
        ones_r = sb("ones_r", [P, EI], F32R)
        minus_half = sb("minus_half", [P, 8])
        minus_magic = sb("minus_magic", [P, 1])
        expert_rows = sb("expert_rows", [P, EXPERTS])
        x = sb("x", [P, TILES, HID])
        ctxT_raw = sb("ctxT_raw", [P, TOK])
        ctxT_hi = sb("ctxT_hi", [P, TOK], F32R)
        ctxT_lo = sb("ctxT_lo", [P, TOK], F32R)
        ctx_raw = sb("ctx_raw", [P, TILES, CDIM])
        ctx_hi = sb("ctx_hi", [P, TILES, CDIM], F32R)
        ctx_lo = sb("ctx_lo", [P, TILES, CDIM], F32R)
        gains_raw = sb("gains_raw", [P, 4])
        tg = sb("tg", [P, 4])
        spare = sb("spare", [P, 1])
        stats = sb("stats", [P, TILES, 6])
        mv = sb("mv", [P, TILES, 2])
        vare = sb("vare", [P, TILES])
        rstd = sb("rstd", [P, TILES])
        u = sb("u", [P, TILES, HID])
        xnT_hi = sb("xnT_hi", [P, KH, TOK], F32R)
        xnT_lo = sb("xnT_lo", [P, KH, TOK], F32R)
        xT = sb("xT", [P, KH, TOK])

        l_x, l_ctxT, l_ctx, l_qk0, l_bias, l_gains = (sem(n) for n in (
            "l_x", "l_ctxT", "l_ctx", "l_qk0", "l_bias", "l_gains"))
        l_gate, l_down, l_tail, l_g1, l_g2, l_gqk = (sem(n) for n in (
            "l_gate", "l_down", "l_tail", "l_g1", "l_g2", "l_gqk"))
        l_router, l_shared, l_shdown = sem("l_router"), sem("l_shared"), sem("l_shdown")
        l_hqk, l_hvo, l_out = sem("l_hqk"), sem("l_hvo"), sem("l_out")
        l_exp = [sem("l_exp0"), sem("l_exp1")]
        pool_const = sem("pool_const")
        v_const, g_ctx = sem("v_const"), sem("g_ctx")
        a_ctx, a_tg = sem("a_ctx"), sem("a_tg")
        v_link = sem("v_link")
        link_n = [0]

        def link(dve, ins):
            link_n[0] += 1
            ins.then_inc(v_link, 1)
            dve.wait_ge(v_link, link_n[0])

        v_pow, g_pow = sem("v_pow"), sem("g_pow")
        pow_n = [0]
        v_u, t_u, a_u, c_u = sem("v_u"), sem("t_u"), sem("a_u"), sem("c_u")

        wqk0 = sb("wqk0", [P, 2, D])
        bqk = sb("bqk", [P, 2])
        qkA = sb("qkA", [P, 2, TOK])
        attA = sb("attA", [P, BATCH, 2, SEQ])
        attT = sb("attT", [P, 2, 2, SEQ])
        nmA = sb("nmA", [P, BATCH, 2])
        sumA = sb("sumA", [P, BATCH, 2])
        invA = sb("invA", [P, BATCH, 2])
        t_qkA, a_qkA, t_eA, v_mA, a_eA, v_nA, t_aA, a_aA, t_oA, v_xA = (sem(n) for n in (
            "t_qkA", "a_qkA", "t_eA", "v_mA", "a_eA", "v_nA", "t_aA", "a_aA", "t_oA", "v_xA"))

        g1 = sb("g1", [P, HID])
        g2 = sb("g2", [P, INTER])
        absum = sb("absum", [P, 3])
        wsc = sb("wsc", [P, 2])
        wsi = sb("wsi", [P, 2])
        tinyB = sb("tinyB", [P, 8, TILES])
        sumh = sb("sumh", [P, TILES])
        amax2 = sb("amax2", [P, TILES])
        gqk_raw = sb("gqk_raw", [P, 2])
        gk = sb("gk", [P, 1])
        wqk_raw = sb("wqk_raw", [P, 768])
        wqk_hi = sb("wqk_hi", [P, 2, 768], F32R)
        wqk_lo = sb("wqk_lo", [P, 2, 768], F32R)
        wvo_raw = sb("wvo_raw", [P, 768])
        ssq = sb("ssq", [P, 2, 8])
        msq = sb("msq", [P, 8])
        rqk = sb("rqk", [P, BATCH, 8])
        rowmax = sb("rowmax", [P, 2, 2, 2])
        shift = sb("shift", [P, 2, 2, 2])
        rowsum = sb("rowsum", [P, 2, 2, 2])
        rowinv = sb("rowinv", [P, BATCH, 2, 2])
        e_raw = sb("e_raw", [P, 2, 768])
        r_raw = sb("r_raw", [P, KH, LOGC])
        s_raw = sb("s_raw", [P, 2, KH, EI])
        sdn_raw = sb("sdn_raw", [EI, HID])
        bctx = ExitStack()
        gate_raw = bctx.enter_context(nc.sbuf_tensor("gate_raw", [P, KH, 2 * INTER], F32))
        down_raw = bctx.enter_context(nc.sbuf_tensor("down_raw", [P, KI, HID], F32))
        gate_t = bctx.enter_context(nc.sbuf_tensor("gate_t", [P, KH, 2 * INTER], BF16))
        down_t = bctx.enter_context(nc.sbuf_tensor("down_t", [P, KI, HID], BF16))
        w1 = bctx.enter_context(nc.sbuf_tensor("w1", [P, TILES, HID], F32))
        q1 = bctx.enter_context(nc.sbuf_tensor("q1", [P, TILES, HID], BF16))
        qT = bctx.enter_context(nc.sbuf_tensor("qT", [P, 2, KH, P], BF16))
        silu_g = bctx.enter_context(nc.sbuf_tensor("silu_g", [P, 2, INTER], F32))
        h_raw = bctx.enter_context(nc.sbuf_tensor("h_raw", [P, 2, INTER], F32))
        w2 = bctx.enter_context(nc.sbuf_tensor("w2", [P, TILES, INTER], F32))
        q2 = bctx.enter_context(nc.sbuf_tensor("q2", [P, 2, INTER], BF16))
        hT = bctx.enter_context(nc.sbuf_tensor("hT", [P, 2, KI, P], BF16))
        junk = bctx.enter_context(nc.sbuf_tensor("junk", [P, 2 * KH * INTER], F32))
        bctx.close()
        a_abs, t_abs, a_gw, a_dw = sem("a_abs"), sem("t_abs"), sem("a_gw"), sem("a_dw")
        v_q1, t_q1, a_q1, t_y1, t_z1, a_s1, v_h1, a_h1 = (sem(n) for n in (
            "v_q1", "t_q1", "a_q1", "t_y1", "t_z1", "a_s1", "v_h1", "a_h1"))
        v_r2, a_r2, t_q2, a_q2, t_y2, v_xB = (sem(n) for n in ("v_r2", "a_r2", "t_q2", "a_q2", "t_y2", "v_xB"))
        v_gr, v_dr, v_r1, v_amax, g_w2, v_abs = (sem(n) for n in ("v_gr", "v_dr", "v_r1", "v_amax", "g_w2", "v_abs"))

        cctx = ExitStack()

        def sc(name, shape, dt=F32):
            return cctx.enter_context(nc.sbuf_tensor(name, shape, dt))

        qh, ql = sc("qh", [P, 2, BATCH, SEQ], F32R), sc("ql", [P, 2, BATCH, SEQ], F32R)
        kh, kl = sc("kh", [P, 2, BATCH, SEQ], F32R), sc("kl", [P, 2, BATCH, SEQ], F32R)
        q_raw = sc("q_raw", [P, 2, 2, 2, D])
        k_raw = sc("k_raw", [P, 2, 2, 2, D])
        k_sq = sc("k_sq", [P, 2, 2, D])
        att = sc("att", [P, 2, 2, 2, SEQ])
        attT_hi = sc("attT_hi", [P, 2, 2, SEQ], F32R)
        attT_lo = sc("attT_lo", [P, 2, 2, SEQ], F32R)
        o_hi, o_lo = sc("o_hi", [P, 2, SEQ], F32R), sc("o_lo", [P, 2, SEQ], F32R)
        m_hi, m_lo = sc("m_hi", [P, 2, 2, HID], F32R), sc("m_lo", [P, 2, 2, HID], F32R)
        cctx.close()

        t_S, t_T, t_O, t_Y, t_Q, t_K, t_TQ, t_TK, t_M = (sem(n) for n in (
            "t_S", "t_T", "t_O", "t_Y", "t_Q", "t_K", "t_TQ", "t_TK", "t_M"))
        a_exp, a_Thi, a_rawQ, a_sqQ, a_rawK, a_hiQ, a_hiK, a_Ohi, a_Mhi, a_Whi = (sem(n) for n in (
            "a_exp", "a_Thi", "a_rawQ", "a_sqQ", "a_rawK", "a_hiQ", "a_hiK", "a_Ohi", "a_Mhi", "a_Whi"))
        v_max, v_shift_c, v_Tlo, v_Y, v_inv, v_Qlo, v_Klo, v_sqK, v_msq, v_Olo, v_Mlo, v_gk = (
            sem(n) for n in ("v_max", "v_shift_c", "v_Tlo", "v_Y", "v_inv", "v_Qlo", "v_Klo", "v_sqK", "v_msq",
                             "v_Olo", "v_Mlo", "v_gk"))
        g_rms, g_kn, g_Wlo = sem("g_rms"), sem("g_kn"), sem("g_Wlo")

        dctx = ExitStack()

        def sd(name, shape, dt=F32):
            return dctx.enter_context(nc.sbuf_tensor(name, shape, dt))

        r_hi, r_lo = sd("r_hi", [P, KH, LOGC], F32R), sd("r_lo", [P, KH, LOGC], F32R)
        e_hi, e_lo = sd("e_hi", [P, 3, 768], F32R), sd("e_lo", [P, 3, 768], F32R)
        logits = sd("logits", [P, TILES, LOGC])
        top8 = sd("top8", [P, TILES, TOPK])
        struck = sd("struck", [P, TILES, EXPERTS])
        chosen = sd("chosen", [P, TILES, EXPERTS])
        shifted = sd("shifted", [P, TILES, EXPERTS])
        wexp = sd("wexp", [P, TILES, EXPERTS])
        wsum = sd("wsum", [P, TILES])
        winv = sd("winv", [P, TILES])
        shg = sd("shg", [P, TILES])
        shcat = sd("shcat", [P, TILES, 2])
        selb = sd("selb", [P, 2, P], F32R)
        wcat = sd("wcat", [P, TILES, P])
        s_hi, s_lo = sd("s_hi", [P, 2, KH, EI], F32R), sd("s_lo", [P, 2, KH, EI], F32R)
        sdn_hi, sdn_lo = sd("sdn_hi", [EI, HID], F32R), sd("sdn_lo", [EI, HID], F32R)
        wT = sd("wT", [P, TOK], F32R)
        shT = sd("shT", [2, TOK], F32R)
        w_keep = sd("w_keep", [EXPERTS, TOK])
        w_all = sd("w_all", [P, 2, TOK])
        gate_s = sd("gate_s", [P, 2, 512])
        prod = sd("prod", [P, 2, 512])
        inter = sd("inter", [P, 2, 512])
        inter_hi, inter_lo = sd("inter_hi", [P, 2, 512], F32R), sd("inter_lo", [P, 2, 512], F32R)
        final = sd("final", [P, 2, 2, 512])
        dctx.close()
        t_log, v_shift, a_wexp, v_wcat, t_wT, a_wT, t_xT, a_xT, g_rw, a_rw, g_Elo = (sem(n) for n in (
            "t_log", "v_shift", "a_wexp", "v_wcat", "t_wT", "a_wT", "t_xT", "a_xT", "g_rw", "a_rw",
            "g_Elo"))
        t_wk, a_wk, l_wrows = sem("t_wk"), sem("a_wk"), sem("l_wrows")
        l_wall = [sem("l_wall0"), sem("l_wall1")]
        t_G, t_U, t_W, t_D, a_silu, a_Ihi, a_Ehi, v_mul1, v_mul2, v_Ilo, v_Elo, v_sel, v_out = (sem(n) for n in (
            "t_G", "t_U", "t_W", "t_D", "a_silu", "a_Ihi", "a_Ehi", "v_mul1", "v_mul2", "v_Ilo", "v_Elo",
            "v_sel", "v_out"))

        GB, UB, WB = 0, 1, 2
        ACC = [[3, 4], [5, 6]]
        SBK, TBK, OBK, YBK, QBK, KBK = [0, 1], [2, 3], 4, 5, 6, 7

        def f(ap):
            return ap.bitcast(F32)

        def bank4(i):
            return bank[i][:, :].rearrange("p (a n) -> p a n", a=2)

        block = ctx.enter_context(nc.Block())

        def split_mm(pe, out, l_hi, l_lo, r_hi_, r_lo_, start, stop):
            pe.matmul(out, l_hi, r_hi_, start=start, stop=False, skip_group_check=True)
            pe.matmul(out, l_hi, r_lo_, start=False, stop=False, skip_group_check=True)
            return pe.matmul(out, l_lo, r_hi_, start=False, stop=stop, skip_group_check=True)

        @block.sync
        def _(sp):
            sp.dma_start(ctxT_raw[:, :], ctxT).then_inc(l_ctxT, 16)
            sp.dma_start(wqk0[:, :, :], qk0).then_inc(l_qk0, 16)
            sp.dma_start(bqk[:, :], bias0).then_inc(l_bias, 16)
            sp.dma_start(gains_raw[:, :], gains).then_inc(l_gains, 16)
            sp.dma_start(x[:, 0:4, :], x_tok[:, 0:4, :]).then_inc(l_x, 16)
            sp.dma_start(x[:, 4:8, :], x_tok[:, 4:8, :]).then_inc(l_x, 16)
            sp.dma_start(ctx_raw[:, :, :], ctx_tok).then_inc(l_ctx, 16)
            sp.dma_start(gate_raw[:, :, :], gate_wT).then_inc(l_gate, 16)
            sp.dma_start(down_raw[:, 0:5, :], down_wT).then_inc(l_down, 16)
            sp.dma_start(down_raw[0:TAIL, 5, :], down_tail).then_inc(l_tail, 16)
            sp.dma_start(g1[:, :], norm_g1.partition_broadcast(P)).then_inc(l_g1, 16)
            sp.dma_start(g2[:, :], norm_g2.partition_broadcast(P)).then_inc(l_g2, 16)
            sp.dma_start(gqk_raw[:, :], gqk).then_inc(l_gqk, 16)
            sp.dma_start(wqk_raw[:, :], head_qk[0]).then_inc(l_hqk, 16)
            sp.dma_start(wvo_raw[:, :], head_vo[0]).then_inc(l_hvo, 16)
            sp.dma_start(r_raw[:, :, :], router_w).then_inc(l_router, 16)
            sp.dma_start(e_raw[:, 0, :], expert_w[0]).then_inc(l_exp[0], 16)
            sp.dma_start(e_raw[:, 1, :], expert_w[1]).then_inc(l_exp[1], 16)
            sp.dma_start(s_raw[:, :, :, :], shared_w).then_inc(l_shared, 16)
            sp.dma_start(sdn_raw[:, :], shared_down).then_inc(l_shdown, 16)
            with sp.Fori(1, PAIRS) as p:
                sp.wait_ge(g_Wlo, p)
                sp.dma_start(wqk_raw[:, :], head_qk[bass.ds(p, 1)].rearrange("a p n -> (a p) n")).then_inc(l_hqk, 16)
                sp.wait_ge(t_M, p)
                sp.dma_start(wvo_raw[:, :], head_vo[bass.ds(p, 1)].rearrange("a p n -> (a p) n")).then_inc(l_hvo, 16)
            for par in range(2):
                sp.wait_ge(g_Elo, par + 1)
                sp.dma_start(e_raw[:, par, :], expert_w[2 + par]).then_inc(l_exp[par], 16)
            sp.wait_ge(a_wk, 2)
            sp.dma_start(w_rows, w_keep[:, :]).then_inc(l_wrows, 16)
            sp.wait_ge(l_wrows, 16)

            def spread_rows(par, e):
                for h in range(2):
                    row = w_rows[bass.ds(e * 2 + h, 1)].rearrange("a n -> (a n)")
                    sp.dma_start(w_all[h * EI:(h + 1) * EI, par, :],
                                 row.partition_broadcast(EI)).then_inc(l_wall[par], 16)

            spread_rows(0, 2)
            spread_rows(1, 3)
            with sp.Fori(2, EPAIRS // 2) as j:
                for par in range(2):
                    sp.wait_ge(v_Elo, j * 2 + par - 3)
                    sp.dma_start(e_raw[:, par, :],
                                 expert_w[bass.ds(j * 2 + par, 1)].rearrange("a p n -> (a p) n")
                                 ).then_inc(l_exp[par], 16)
                    sp.wait_ge(v_mul2, j * 4 + par * 2 - 2)
                    spread_rows(par, j * 2 + par)
            for t in range(2):
                for hb in range(2):
                    sp.wait_ge(v_out, 2 * t + hb + 1)
                    sp.dma_start(outT[hb, :, t * 512:(t + 1) * 512], final[:, hb, t, :]).then_inc(l_out, 16)
            sp.wait_ge(l_out, 64)

        @block.gpsimd
        def _(pool):
            pool.memset(ident[:, :], 0.0).then_inc(pool_const, 1)
            pool.memset(ones[:, :], 1.0).then_inc(pool_const, 1)
            pool.memset(minus_half[:, :], -0.5).then_inc(pool_const, 1)
            pool.memset(expert_rows[:, :], 0.0).then_inc(pool_const, 1)
            pool.memset(minus_magic[:, :], -MAGIC).then_inc(pool_const, 1)
            pool.wait_ge(pool_const, 5)
            pool.affine_select(out=ident[:, :], in_=ident[:, :], compare_op=ALU.not_equal, fill=1.0, base=0,
                               pattern=[[-1, P]], channel_multiplier=1).then_inc(pool_const, 1)
            pool.affine_select(out=expert_rows[:, :], in_=expert_rows[:, :], compare_op=ALU.not_equal, fill=1.0,
                               base=0, pattern=[[-1, EXPERTS]], channel_multiplier=1).then_inc(pool_const, 1)
            pool.wait_ge(pool_const, 7)
            pool.affine_select(out=expert_rows[:, :], in_=expert_rows[:, :], compare_op=ALU.not_equal, fill=1.0,
                               base=-EXPERTS, pattern=[[-1, EXPERTS]], channel_multiplier=1).then_inc(pool_const, 1)

            def power(k, src, dst, n):
                pool.wait_ge(v_pow, k + 1)
                pool.tensor_tensor(dst, src, minus_half[:, 0:n], ALU.pow).then_inc(g_pow, 1)

            power(0, vare[:, :], rstd[:, :], TILES)
            pool.wait_ge(a_ctx, 1)
            pool.tensor_tensor(ctxT_lo[:, :], ctxT_raw[:, :], f(ctxT_hi[:, :]), ALU.subtract).then_inc(g_ctx, 1)
            power(1, tinyB[:, 0, :], tinyB[:, 1, :], TILES)

            def low_w(w, par):
                pool.wait_ge(a_Whi, w + 1)
                wait(pool, t_K, w * 4 - 4)
                wait(pool, t_Q, w * 4 - 4)
                pool.tensor_tensor(wqk_lo[:, par, :], wqk_raw[:, :], f(wqk_hi[:, par, :]),
                                   ALU.subtract).then_inc(g_Wlo, 1)

            low_w(0, 0)
            pool.wait_ge(l_g2, 16)
            for i in range(TILES):
                pool.wait_ge(v_h1, 2 * i + 2)
                pool.tensor_tensor(w2[:, i, :], h_raw[:, i % 2, :], g2[:, :], ALU.mult).then_inc(g_w2, 1)
                if i == 4:
                    power(2, tinyB[:, 5, 0:4], tinyB[:, 6, 0:4], 4)
            power(3, tinyB[:, 5, 4:8], tinyB[:, 6, 4:8], 4)
            pool.wait_ge(a_ctx, 2)
            pool.tensor_tensor(ctx_lo[:, :, :], ctx_raw[:, :, :], f(ctx_hi[:, :, :]), ALU.subtract).then_inc(g_ctx, 1)
            power(4, vare[:, 0:4], rstd[:, 0:4], 4)
            power(5, vare[:, 4:8], rstd[:, 4:8], 4)
            low_w(1, 1)

            def rms(b, n):
                wait(pool, a_exp, n * 4 - 12)
                pool.wait_ge(v_msq, n + 1)
                pool.tensor_tensor(rqk[:, b, :], msq[:, :], minus_half[:, :], ALU.pow).then_inc(g_rms, 1)
                pool.wait_ge(g_rms, n + 1)
                k = k_raw[:, b % 2, :, :, :].rearrange("p t h d -> p (t h) d")
                pool.tensor_tensor(k, k, rqk[:, b, 4:8].unsqueeze(2).broadcast_to([P, 4, D]),
                                   ALU.mult).then_inc(g_kn, 1)

            for n in range(4):
                rms(n, n)

            def scale_pair(p, par, last=False):
                for b in range(BATCH):
                    rms(b, p * 4 + b)
                    if b == 1 and not last:
                        low_w(p + 1, 1 - par)

            with pool.Fori(1, PAIRS // 2) as i:
                scale_pair(i * 2 - 1, 1)
                scale_pair(i * 2, 0)
            scale_pair(PAIRS - 1, 1, last=True)
            power(6, vare[:, 0:4], rstd[:, 0:4], 4)
            pool.wait_ge(t_S, 2 * GROUPS)
            pool.wait_ge(a_rw, 1)
            pool.tensor_tensor(r_lo[:, :, :], r_raw[:, :, :], f(r_hi[:, :, :]), ALU.subtract).then_inc(g_rw, 1)
            pool.wait_ge(a_Ehi, 1)
            pool.tensor_tensor(e_lo[:, 2, :], e_raw[:, 0, :], f(e_hi[:, 2, :]), ALU.subtract).then_inc(g_Elo, 1)
            power(7, vare[:, 4:8], rstd[:, 4:8], 4)
            pool.wait_ge(a_Ehi, 2)
            pool.tensor_tensor(e_lo[:, 1, :], e_raw[:, 1, :], f(e_hi[:, 1, :]), ALU.subtract).then_inc(g_Elo, 1)
            pool.wait_ge(a_rw, 3)
            pool.tensor_tensor(s_lo[:, :, :, :], s_raw[:, :, :, :], f(s_hi[:, :, :, :]),
                               ALU.subtract).then_inc(g_rw, 1)
            pool.tensor_tensor(sdn_lo[:, :], sdn_raw[:, :], f(sdn_hi[:, :]), ALU.subtract).then_inc(g_rw, 1)

        @block.tensor
        def _(pe):
            def turn_rows(first, j, banks):
                pe.wait_ge(v_u, first * 8 + 2 * j + 2)
                if j >= 2:
                    pe.wait_ge(c_u, first * 4 + j - 1)
                for k in range(KH):
                    for t in range(2):
                        mm = pe.transpose(bank4(banks[j % 2])[:, k, t * P:(t + 1) * P],
                                          u[:, 2 * j + t, k * P:(k + 1) * P], ident[:, :])
                mm.then_inc(t_u, 1)

            pe.wait_ge(l_ctxT, 16)
            pe.wait_ge(l_qk0, 16)
            for i in range(2):
                for h in range(2):
                    pe.matmul(bank[2 * i + h][:, :], wqk0[:, i, :], ctxT_raw[:, h * 512:(h + 1) * 512],
                              start=True, stop=True).then_inc(t_qkA, 1)
            pe.wait_ge(a_qkA, 4)
            for b in range(BATCH):
                for m in range(2):
                    c = b * SEQ + m * P
                    mm = pe.matmul(bank4(b)[:, m, :], qkA[:, 0, c:c + P], qkA[:, 1, b * SEQ:(b + 1) * SEQ],
                                   start=True, stop=True)
                mm.then_inc(t_eA, 1)
            pe.wait_ge(pool_const, 8)
            for j in range(BATCH):
                turn_rows(0, j, [6, 7])

            def turn_att(b):
                pe.wait_ge(v_nA, b + 1)
                if b >= 2:
                    pe.wait_ge(a_aA, b - 1)
                for j in range(2):
                    for m in range(2):
                        mm = pe.transpose(bank4(4 + b % 2)[:, j, m * P:(m + 1) * P],
                                          attA[:, b, m, j * P:(j + 1) * P], ident[:, :])
                mm.then_inc(t_aA, 1)

            def mix(b):
                pe.wait_ge(a_aA, b + 1)
                pe.wait_ge(c_u, 4)
                if b >= 2:
                    pe.wait_ge(v_xA, b - 1)
                for t in range(2):
                    for j in range(2):
                        c = (2 * b + t) * P
                        mm = pe.matmul(bank4(6 + b % 2)[:, t, :], xT[:, j, c:c + P], attT[:, b % 2, j, :],
                                       start=j == 0, stop=j == 1)
                mm.then_inc(t_oA, 1)

            def sum_abs(parts, column):
                for n, (rows, c) in enumerate(parts):
                    mm = pe.matmul(bank[[3, 7][column]][:, 0:1], ones[0:rows, :], absum[0:rows, c:c + 1],
                                   start=n == 0, stop=n == len(parts) - 1, skip_group_check=True)
                mm.then_inc(t_abs, 1)

            turn_att(0)
            turn_att(1)
            mix(0)
            turn_att(2)
            mix(1)
            turn_att(3)
            pe.wait_ge(a_abs, 1)
            pe.wait_ge(a_eA, 8)
            sum_abs([(P, 0)], 0)
            mix(2)
            mix(3)
            pe.wait_ge(a_abs, 3)
            pe.wait_ge(v_xA, 4)
            sum_abs([(P, 1), (TAIL, 2)], 1)

            def turn_q1(i):
                pe.wait_ge(v_q1, i + 1)
                if i >= 2:
                    pe.wait_ge(a_q1, i - 1)
                bk = bank[4 + i % 2][:, :].bitcast(BF16)
                for k in range(KH):
                    mm = pe.transpose(bk[:, k * P:(k + 1) * P], q1[:, i, k * P:(k + 1) * P], ident_b[:, :])
                mm.then_inc(t_q1, 1)

            def gate_up(i):
                pe.wait_ge(a_q1, i + 1)
                pe.wait_ge(a_gw, 1)
                if i >= 1:
                    pe.wait_ge(a_s1, i)
                for c in range(4):
                    if c == 2 and i >= 1:
                        pe.wait_ge(v_h1, 2 * i)
                    for k in range(KH):
                        mm = pe.matmul(bank[c][:, 0:HALF], qT[:, i % 2, k, :],
                                       gate_t[:, k, c * HALF:(c + 1) * HALF], start=k == 0, stop=k == KH - 1)
                    if c == 1:
                        mm.then_inc(t_y1, 1)
                mm.then_inc(t_z1, 1)

            pe.wait_ge(v_const, 2)
            turn_q1(0)
            for i in range(TILES):
                if i + 1 < TILES:
                    turn_q1(i + 1)
                gate_up(i)

            def turn_q2(i):
                pe.wait_ge(a_r2, i + 1)
                if i >= 2:
                    pe.wait_ge(a_q2, i - 1)
                bk = bank[6 + i % 2][:, :].bitcast(BF16)
                for k in range(KI):
                    n = P if k < 5 else TAIL
                    mm = pe.transpose(bk[0:n, k * P:(k + 1) * P], q2[:, i % 2, k * P:k * P + n], ident_b[:, :])
                mm.then_inc(t_q2, 1)

            def down(i):
                pe.wait_ge(a_q2, i + 1)
                pe.wait_ge(a_dw, 1)
                if i >= 2:
                    pe.wait_ge(v_xB, i - 1)
                else:
                    pe.wait_ge(a_q1, TILES)
                for k in range(KI):
                    n = P if k < 5 else TAIL
                    mm = pe.matmul(bank[4 + i % 2][:, 0:HID], hT[0:n, i % 2, k, :], down_t[0:n, k, :],
                                   start=k == 0, stop=k == KI - 1)
                mm.then_inc(t_y2, 1)

            turn_q2(0)
            for i in range(TILES):
                if i + 1 < TILES:
                    turn_q2(i + 1)
                down(i)

            def project(out, lhs_hi, lhs_lo, c, par, w0, k, last):
                return split_mm(pe, out, lhs_hi[:, c:c + P], lhs_lo[:, c:c + P], wqk_hi[:, par, w0:w0 + 256],
                                wqk_lo[:, par, w0:w0 + 256], k == 0, last)

            def proj_q(b, n, par, w, bk=QBK, fresh=False):
                pe.wait_ge(g_Wlo, w)
                if not fresh:
                    wait(pe, a_sqQ, n * 4)
                    wait(pe, v_Qlo, n - 1)
                for t in range(2):
                    for k in range(KH):
                        mm = project(bank4(bk)[:, t, :], xnT_hi[:, k, :], xnT_lo[:, k, :], (2 * b + t) * P, par,
                                     k * 256, k, k == KH - 1)
                mm.then_inc(t_Q, 1)

            def proj_k(b, n, par, w, bk=KBK, fresh=False):
                pe.wait_ge(g_Wlo, w)
                if not fresh:
                    wait(pe, a_rawK, n)
                    wait(pe, v_Klo, n - 1)
                for t in range(2):
                    mm = project(bank4(bk)[:, t, :], ctxT_hi, ctxT_lo, (2 * b + t) * P, par, 512, 0, True)
                mm.then_inc(t_K, 1)

            def turn_q(b, n, done):
                wait(pe, a_sqQ, done * 4)
                pe.wait_ge(a_rawQ, n + 1)
                for h in range(2):
                    for t in range(2):
                        mm = pe.transpose(bank4(QBK)[:, h, t * P:(t + 1) * P], q_raw[:, b % 2, t, h, :],
                                          ident[:, :])
                mm.then_inc(t_TQ, 1)

            def turn_k(b, n, done):
                wait(pe, a_rawK, done)
                pe.wait_ge(g_kn, n + 1)
                for h in range(2):
                    for t in range(2):
                        mm = pe.transpose(bank4(KBK)[:, h, t * P:(t + 1) * P], k_raw[:, b % 2, t, h, :],
                                          ident[:, :])
                mm.then_inc(t_TK, 1)

            def scores(b, g):
                pe.wait_ge(v_Qlo, g + 1)
                pe.wait_ge(v_Klo, g + 1)
                for h in range(2):
                    wait(pe, a_exp, g * 4 - 2 + 2 * h)
                    for t in range(2):
                        c = slice(t * P, (t + 1) * P)
                        mm = split_mm(pe, bank4(SBK[h])[:, t, :], qh[:, h, b, c], ql[:, h, b, c],
                                      kh[:, h, b, :], kl[:, h, b, :], True, True)
                    mm.then_inc(t_S, 1)

            def turn(b, g):
                pe.wait_ge(a_exp, g * 4 + 4)
                for j in range(2):
                    wait(pe, v_Tlo, g * 2 - 1 + j)
                    for h in range(2):
                        for t in range(2):
                            mm = pe.transpose(bank4(TBK[j])[:, h, t * P:(t + 1) * P],
                                              att[:, b % 2, h, t, j * P:(j + 1) * P], ident[:, :])
                    mm.then_inc(t_T, 1)

            def values(b, g):
                pe.wait_ge(v_Tlo, g * 2 + 2)
                wait(pe, v_Olo, g)
                for j in range(2):
                    mm = split_mm(pe, bank[OBK][:, :], ctx_hi[:, 2 * b + j, :], ctx_lo[:, 2 * b + j, :],
                                  attT_hi[:, j, :, :].rearrange("p h n -> p (h n)"),
                                  attT_lo[:, j, :, :].rearrange("p h n -> p (h n)"), j == 0, j == 1)
                mm.then_inc(t_O, 1)

            def output(g, h, par, p_m):
                pe.wait_ge(v_Olo, g + 1)
                pe.wait_ge(v_Mlo, p_m)
                wait(pe, v_Y, g * 4 + 2 * h)
                for t in range(2):
                    c = slice(t * P, (t + 1) * P)
                    mm = split_mm(pe, bank4(YBK)[:, t, :], o_hi[:, h, c], o_lo[:, h, c],
                                  m_hi[:, par, h, :], m_lo[:, par, h, :], True, True)
                mm.then_inc(t_Y, 1)

            def fuse_vo(p, bk):
                pe.wait_ge(l_hvo, p * 16 + 16)
                for h in range(2):
                    mm = pe.matmul(bank4(bk)[:, h, :], wvo_raw[:, h * P:(h + 1) * P],
                                   wvo_raw[:, 256 + h * 256:512 + h * 256], start=True, stop=True)
                mm.then_inc(t_M, 1)

            def pair(p, par, first=False, last=False):
                for b in range(BATCH):
                    g = p * 4 + b
                    n = g + 4
                    start = first and b == 0
                    turning = not (last and b >= 2)
                    if not (last and b == 3):
                        scores((b + 1) % 4, g + 1)
                    if turning:
                        turn_q((b + 2) % 4, n - 2, PIECES if last else n)
                    if b == 1 and not last:
                        pe.wait_ge(a_rawK, n)
                        fuse_vo(p + 1, KBK)
                    turn(b, g)
                    if not start:
                        output(g - 1, 0, *((1 - par, p) if b == 0 else (par, p + 1)))
                    if b == 1 and not last:
                        pe.wait_ge(v_Mlo, p + 2)
                    if turning:
                        turn_k((b + 2) % 4, n - 2, PIECES if last else n)
                    if not last:
                        proj_q(b, n, 1 - par, p + 2)
                    values(b, g)
                    if not start:
                        output(g - 1, 1, *((1 - par, p) if b == 0 else (par, p + 1)))
                    if not last:
                        proj_k(b, n, 1 - par, p + 2)

            fuse_vo(0, 0)
            pe.wait_ge(g_ctx, 1)
            pe.wait_ge(a_q2, TILES)
            first_banks = [(QBK, KBK), (4, 5), (0, 1), (4, 5)]
            proj_k(0, 0, 0, 1, KBK, True)
            turn_rows(1, 0, TBK)
            turn_rows(1, 1, TBK)
            pe.wait_ge(v_xB, TILES)
            proj_k(1, 1, 0, 1, 5, True)
            pe.wait_ge(c_u, 5)
            proj_q(0, 0, 0, 1, QBK, True)
            proj_k(2, 2, 0, 1, 1, True)
            pe.wait_ge(c_u, 6)
            proj_q(1, 1, 0, 1, 4, True)
            turn_rows(1, 2, TBK)
            turn_rows(1, 3, TBK)
            turn_q(0, 0, 1)
            pe.wait_ge(a_rawK, 2)
            proj_k(3, 3, 0, 1, 5, True)
            turn_k(0, 0, 1)
            pe.wait_ge(c_u, 7)
            pe.wait_ge(v_Mlo, 1)
            proj_q(2, 2, 0, 1, 0, True)
            pe.wait_ge(c_u, 8)
            pe.wait_ge(a_sqQ, 8)
            proj_q(3, 3, 0, 1, 4, True)
            pe.wait_ge(v_Qlo, 1)
            turn_q(1, 1, 1)
            pe.wait_ge(v_Klo, 1)
            turn_k(1, 1, 1)
            pe.wait_ge(a_sqQ, 12)
            pe.wait_ge(a_rawK, 3)
            scores(0, 0)
            pe.wait_ge(a_sqQ, 16)
            pe.wait_ge(a_rawK, 4)
            pe.wait_ge(g_ctx, 2)
            pair(0, 0, first=True)
            with pe.Fori(1, PAIRS // 2) as i:
                pair(i * 2 - 1, 1)
                pair(i * 2, 0)
            pair(PAIRS - 1, 1, last=True)

            def router(half):
                pe.wait_ge(g_rw, 1)
                pe.wait_ge(c_u, 8 + 2 * half + 2)
                if half == 0:
                    pe.wait_ge(v_Tlo, 2 * GROUPS)
                for i in range(4):
                    c = (half * 4 + i) * P
                    for k in range(KH):
                        mm = split_mm(pe, bank[3 + half][:, i * LOGC:(i + 1) * LOGC],
                                      xnT_hi[:, k, c:c + P], xnT_lo[:, k, c:c + P],
                                      r_hi[:, k, :], r_lo[:, k, :], k == 0, k == KH - 1)
                mm.then_inc(t_log, 1)

            def turn_weights(half):
                pe.wait_ge(v_wcat, half + 1)
                wbank = [WB, 6][half]
                for i in range(4):
                    mm = pe.transpose(bank[wbank][:, i * P:(i + 1) * P], wcat[:, half * 4 + i, :], ident[:, :])
                for i in range(4):
                    mm = pe.transpose(bank[3 + half][0:2, i * P:(i + 1) * P], shcat[:, half * 4 + i, :], ident[:, :])
                mm.then_inc(t_wT, 1)

            def turn_rows_w(half):
                for i in range(4):
                    mm = pe.transpose(bank[7][0:EXPERTS, i * P:(i + 1) * P], chosen[:, half * 4 + i, :],
                                      ident[:, :])
                mm.then_inc(t_wk, 1)

            def turn_x(j):
                if j:
                    pe.wait_ge(a_xT, j)
                else:
                    pe.wait_ge(a_wk, 2)
                for k in range(KH):
                    for t in range(2):
                        mm = pe.transpose(bank4(7)[:, k, t * P:(t + 1) * P],
                                          x[:, 2 * j + t, k * P:(k + 1) * P], ident[:, :])
                mm.then_inc(t_xT, 1)

            def gates(par, t, s, bk, part, first=False):
                if not first:
                    pe.wait_ge(a_silu if part == 0 else v_mul1, s)
                for k in range(KH):
                    c = part * 256 + k * P
                    mm = split_mm(pe, bank[bk][:, :], e_hi[:, par, c:c + P], e_lo[:, par, c:c + P],
                                  xnT_hi[:, k, t * 512:(t + 1) * 512], xnT_lo[:, k, t * 512:(t + 1) * 512],
                                  k == 0, k == KH - 1)
                mm.then_inc(t_G if part == 0 else t_U, 1)

            def spread_w(par, e, t, s, first=False):
                pe.wait_ge(v_sel, e + 1)
                if not first:
                    pe.wait_ge(v_mul2, s)
                pe.matmul(bank[WB][:, :], selb[:, par, :], wT[:, t * 512:(t + 1) * 512],
                          start=True, stop=True).then_inc(t_W, 1)

            def experts_down(par, slot, t, s, start=False):
                pe.wait_ge(v_Ilo, s + 1)
                for hb in range(2):
                    c = 512 + hb * P
                    mm = split_mm(pe, bank[ACC[hb][t]][:, :], e_hi[:, par, c:c + P], e_lo[:, par, c:c + P],
                                  inter_hi[:, slot, :], inter_lo[:, slot, :], start, False)
                mm.then_inc(t_D, 1)

            turn_rows(2, 0, [QBK, KBK])
            turn_rows(2, 1, [QBK, KBK])
            output(GROUPS - 1, 0, 1, PAIRS)
            router(0)
            output(GROUPS - 1, 1, 1, PAIRS)
            def first_gate(s):
                gates(2 - s % 2, s // 2, s, GB, 0, s == 0)

            def first_up(s):
                gates(2 - s % 2, s // 2, s, UB, 1, s == 0)

            def first_spread(s):
                pe.wait_ge(a_wT, s // 2 + 1)
                spread_w(s % 2, s % 2, s // 2, s, s == 0)

            pe.wait_ge(g_Elo, 1)
            first_gate(0)
            first_up(0)
            turn_rows(2, 2, [QBK, KBK])
            turn_rows(2, 3, [QBK, KBK])
            pe.wait_ge(g_Elo, 2)
            first_gate(1)
            turn_weights(0)
            pe.wait_ge(c_u, 12)
            turn_rows_w(0)
            first_up(1)
            first_spread(0)
            pe.wait_ge(v_Y, 4 * GROUPS)
            router(1)
            first_spread(1)
            experts_down(2, 0, 0, 0, True)
            first_gate(2)
            first_up(2)
            experts_down(1, 1, 0, 1)
            first_gate(3)
            turn_weights(1)
            pe.wait_ge(a_wk, 1)
            turn_rows_w(1)
            first_up(3)
            first_spread(2)
            first_spread(3)
            experts_down(2, 0, 1, 2, True)
            with pe.Fori(1, EPAIRS // 2) as j:
                for par in range(2):
                    for t in range(2):
                        s = j * 4 + par * 2 + t
                        if t == 0:
                            pe.wait_ge(v_Elo, j * 2 + par - 1)
                        gates(par, t, s, GB, 0)
                        gates(par, t, s, UB, 1)
                        before = (par * 2 + t - 1) % 4
                        experts_down(before // 2, before % 2, before % 2, s - 1)
            pe.wait_ge(g_rw, 3)
            for t in range(2):
                s = 2 * EPAIRS + t
                for part, bk, free, done in ((0, GB, a_silu, t_G), (1, UB, v_mul1, t_U)):
                    pe.wait_ge(free, s)
                    for k in range(KH):
                        mm = split_mm(pe, bank[bk][0:EI, :], s_hi[:, part, k, :], s_lo[:, part, k, :],
                                      xnT_hi[:, k, t * 512:(t + 1) * 512], xnT_lo[:, k, t * 512:(t + 1) * 512],
                                      k == 0, k == KH - 1)
                    mm.then_inc(done, 1)
                    turn_x(2 * t + part)
                pe.wait_ge(v_mul2, s)
                pe.matmul(bank[WB][0:EI, :], ones_r[0:2, :], shT[:, t * 512:(t + 1) * 512], start=True,
                          stop=True).then_inc(t_W, 1)
                if t == 0:
                    experts_down(1, 1, 1, s - 1)
            for t in range(2):
                pe.wait_ge(v_Ilo, 2 * EPAIRS + t + 1)
                for hb in range(2):
                    mm = split_mm(pe, bank[ACC[hb][t]][:, :], sdn_hi[:, hb * P:(hb + 1) * P],
                                  sdn_lo[:, hb * P:(hb + 1) * P], inter_hi[0:EI, t, :], inter_lo[0:EI, t, :],
                                  False, True)
                    mm.then_inc(t_D, 1)

        @block.scalar
        def _(act):
            def copy_rows(first, j, banks):
                act.wait_ge(t_u, first * 4 + j + 1)
                dst = xnT_hi if first else xT
                act.activation(dst[:, :, j * 256:(j + 1) * 256], bank4(banks[j % 2]), ACT.Copy).then_inc(
                    a_u if first else c_u, 1)

            act.wait_ge(l_gains, 16)
            act.activation(tg[:, :], gains_raw[:, :], ACT.Tanh).then_inc(a_tg, 1)
            act.wait_ge(l_bias, 16)
            for i in range(2):
                for h in range(2):
                    act.wait_ge(t_qkA, 2 * i + h + 1)
                    act.activation(qkA[:, i, h * 512:(h + 1) * 512], bank[2 * i + h][:, :], ACT.Identity,
                                   bias=bqk[:, i:i + 1]).then_inc(a_qkA, 1)
            act.activation(ctxT_hi[:, :], ctxT_raw[:, :], ACT.Copy).then_inc(a_ctx, 1)
            def exp_A(b):
                act.wait_ge(v_mA, b + 1)
                for m in range(2):
                    act.activation(attA[:, b, m, :], bank4(b)[:, m, :], ACT.Exp, bias=nmA[:, b, m:m + 1],
                                   accum_out=sumA[:, b, m:m + 1]).then_inc(a_eA, 1)

            def copy_att(b):
                act.wait_ge(t_aA, b + 1)
                if b >= 2:
                    act.wait_ge(t_oA, b - 1)
                act.activation(attT[:, b % 2, :, :], bank4(4 + b % 2), ACT.Copy).then_inc(a_aA, 1)

            exp_A(0)
            exp_A(1)
            copy_rows(0, 0, [6, 7])
            copy_rows(0, 1, [6, 7])
            exp_A(2)
            exp_A(3)
            copy_rows(0, 2, [6, 7])
            copy_rows(0, 3, [6, 7])
            copy_att(0)
            copy_att(1)
            act.wait_ge(l_gate, 16)
            act.activation(junk[:, :], gate_raw[:, :, :].rearrange("p k n -> p (k n)"), ACT.Abs,
                           accum_out=absum[:, 0:1]).then_inc(a_abs, 1)
            copy_att(2)
            copy_att(3)
            act.wait_ge(l_down, 16)
            act.wait_ge(a_abs, 1)
            act.activation(junk[:, 0:5 * HID], down_raw[:, 0:5, :].rearrange("p k n -> p (k n)"), ACT.Abs,
                           accum_out=absum[:, 1:2]).then_inc(a_abs, 1)
            act.wait_ge(l_tail, 16)
            act.wait_ge(a_abs, 2)
            act.activation(junk[0:TAIL, 0:HID], down_raw[0:TAIL, 5, :], ACT.Abs,
                           accum_out=absum[0:TAIL, 2:3]).then_inc(a_abs, 1)

            def split_w(w, par):
                act.wait_ge(l_hqk, w * 16 + 16)
                wait(act, t_K, w * 4 - 4)
                wait(act, t_Q, w * 4 - 4)
                act.activation(wqk_hi[:, par, :], wqk_raw[:, :], ACT.Copy).then_inc(a_Whi, 1)

            act.wait_ge(pool_const, 8)
            act.wait_ge(v_gr, 1)
            act.activation(gate_t[:, :, :], gate_raw[:, :, :], ACT.Identity,
                           bias=minus_magic[:, 0:1]).then_inc(a_gw, 1)

            split_w(0, 0)
            act.wait_ge(l_ctx, 16)
            act.activation(ctx_hi[:, :, :], ctx_raw[:, :, :], ACT.Copy).then_inc(a_ctx, 1)
            act.activation(spare[:, :], tg[:, 0:1], ACT.Silu)

            def copy_q1(i):
                act.wait_ge(t_q1, i + 1)
                if i >= 2:
                    act.wait_ge(t_z1, i - 1)
                act.activation(qT[:, i % 2, :, :].rearrange("p k n -> p (k n)"),
                               bank[4 + i % 2][:, :].bitcast(BF16)[:, 0:HID], ACT.Copy).then_inc(a_q1, 1)

            copy_q1(0)
            for i in range(TILES):
                if i + 1 < TILES:
                    copy_q1(i + 1)
                act.wait_ge(t_y1, i + 1)
                if i >= 2:
                    act.wait_ge(v_h1, 2 * (i - 1))
                for c in range(2):
                    ins = act.activation(silu_g[:, i % 2, c * HALF:(c + 1) * HALF], bank[c][:, 0:HALF], ACT.Silu,
                                         scale=tinyB[:, 4, i:i + 1])
                ins.then_inc(a_s1, 1)
                if i >= 1:
                    act.wait_ge(v_h1, 2 * i)
                    act.activation(junk[:, 0:INTER], h_raw[:, (i - 1) % 2, :], ACT.Square,
                                   accum_out=sumh[:, i - 1:i]).then_inc(a_h1, 1)
                    act.wait_ge(a_h1, i)
            act.wait_ge(v_dr, 1)
            act.activation(down_t[0:TAIL, 5, :], down_raw[0:TAIL, 5, :], ACT.Identity,
                           bias=minus_magic[0:TAIL, 0:1])
            act.activation(down_t[:, 0:5, :], down_raw[:, 0:5, :], ACT.Identity,
                           bias=minus_magic[:, 0:1]).then_inc(a_dw, 1)
            act.wait_ge(v_h1, 2 * TILES)
            act.activation(junk[:, 0:INTER], h_raw[:, 1, :], ACT.Square,
                           accum_out=sumh[:, TILES - 1:TILES]).then_inc(a_h1, 1)

            def round_q2(i):
                act.wait_ge(v_r2, i + 1)
                if i >= 2:
                    act.wait_ge(t_q2, i - 1)
                act.activation(q2[:, i % 2, :], w2[:, i, :], ACT.Identity, bias=minus_magic[:, 0:1]).then_inc(a_r2, 1)

            round_q2(0)
            for i in range(TILES):
                if i + 1 < TILES:
                    round_q2(i + 1)
                act.wait_ge(t_q2, i + 1)
                if i >= 2:
                    act.wait_ge(t_y2, i - 1)
                bk = bank[6 + i % 2][:, :].bitcast(BF16)
                act.activation(hT[:, i % 2, 0:5, :].rearrange("p k n -> p (k n)"), bk[:, 0:5 * P], ACT.Copy)
                act.activation(hT[0:TAIL, i % 2, 5, :], bk[0:TAIL, 5 * P:6 * P], ACT.Copy).then_inc(a_q2, 1)

            def raw_q(b, n, bk=QBK):
                act.wait_ge(t_Q, n + 1)
                wait(act, t_TQ, n - 1)
                act.activation(q_raw[:, b % 2, :, :, :].rearrange("p t h d -> p (t h d)"), bank[bk][:, :],
                               ACT.Copy).then_inc(a_rawQ, 1)

            def square_q(b, n, bk=QBK):
                act.wait_ge(a_rawQ, n + 1)
                wait(act, v_msq, n - 1)
                for c in range(4):
                    sq = bank[bk][:, c * D:(c + 1) * D]
                    act.activation(sq, sq, ACT.Square,
                                   accum_out=ssq[:, b % 2, c:c + 1]).then_inc(a_sqQ, 1)

            def raw_k(b, n, bk=KBK):
                act.wait_ge(t_K, n + 1)
                wait(act, t_TK, n - 1)
                act.activation(k_raw[:, b % 2, :, :, :].rearrange("p t h d -> p (t h d)"), bank[bk][:, :],
                               ACT.Copy).then_inc(a_rawK, 1)

            def high_q(b, n):
                act.wait_ge(t_TQ, n + 1)
                wait(act, t_S, n * 2 - 6)
                act.activation(qh[:, :, b, :], bank4(QBK), ACT.Copy).then_inc(a_hiQ, 1)

            def high_k(b, n):
                act.wait_ge(t_TK, n + 1)
                wait(act, t_S, n * 2 - 6)
                act.activation(kh[:, :, b, :], bank4(KBK), ACT.Copy, scale=gk[:, 0:1]).then_inc(a_hiK, 1)

            def exps(b, g, h):
                act.wait_ge(v_shift_c, g + 1)
                wait(act, t_T, g * 2 - 2)
                for t in range(2):
                    act.activation(att[:, b % 2, h, t, :], bank4(SBK[h])[:, t, :], ACT.Exp,
                                   bias=shift[:, b % 2, t, h:h + 1], scale=rqk[:, b, t * 2 + h:t * 2 + h + 1],
                                   accum_out=rowsum[:, b % 2, t, h:h + 1]).then_inc(a_exp, 1)

            def high_m(p, par, bk):
                act.wait_ge(t_M, p + 1)
                wait(act, t_Y, p * 8 - 8)
                act.activation(m_hi[:, par, :, :], bank4(bk), ACT.Copy, scale=tg[:, 1:2]).then_inc(a_Mhi, 1)

            def split_e(par, turn, done=None, buffer=None):
                act.wait_ge(l_exp[par], turn * 16 + 16)
                if done is not None:
                    act.wait_ge(t_D, done)
                act.activation(e_hi[:, par if buffer is None else buffer, :], e_raw[:, par, :],
                               ACT.Copy).then_inc(a_Ehi, 1)

            def split_router():
                act.wait_ge(t_S, 2 * GROUPS)
                act.wait_ge(l_router, 16)
                act.activation(r_hi[:, :, :], r_raw[:, :, :], ACT.Copy).then_inc(a_rw, 1)

            def pair(p, par, last=False, more=True):
                for b in range(BATCH):
                    g = p * 4 + b
                    n = g + 4
                    if not (last and b >= 2):
                        high_q((b + 2) % 4, n - 2)
                    if b == 1 and not last:
                        high_m(p + 1, 1 - par, KBK)
                    for j in range(2):
                        act.wait_ge(t_T, g * 2 + j + 1)
                        wait(act, t_O, g)
                        act.activation(attT_hi[:, j, :, :], bank4(TBK[j]), ACT.Copy).then_inc(a_Thi, 1)
                    if not (last and b >= 2):
                        high_k((b + 2) % 4, n - 2)
                    if not (last and b == 3):
                        exps((b + 1) % 4, g + 1, 0)
                    if not last:
                        raw_q(b, n)
                    if not (last and b == 3):
                        exps((b + 1) % 4, g + 1, 1)
                    if not last:
                        square_q(b, n)
                    if last and b == 3:
                        split_e(0, 0, buffer=2)
                    act.wait_ge(t_O, g + 1)
                    wait(act, t_Y, g * 2)
                    act.activation(o_hi[:, :, :], bank4(OBK), ACT.Copy).then_inc(a_Ohi, 1)
                    if not last:
                        raw_k(b, n)
                    if last and b == 2:
                        split_router()
                    if b == 1 and more:
                        split_w(p + 2, par)

            act.activation(spare[:, :], tg[:, 0:1], ACT.Exp)
            high_m(0, 0, 0)
            raw_k(0, 0)
            copy_rows(1, 0, TBK)
            copy_rows(1, 1, TBK)
            raw_k(1, 1, 5)
            split_w(1, 1)
            raw_q(0, 0)
            square_q(0, 0)
            raw_q(1, 1, 4)
            square_q(1, 1, 4)
            copy_rows(1, 2, TBK)
            act.wait_ge(v_gk, 1)
            high_q(0, 0)
            copy_rows(1, 3, TBK)
            high_k(0, 0)
            raw_q(2, 2, 0)
            square_q(2, 2, 0)
            raw_k(2, 2, 1)
            high_q(1, 1)
            raw_q(3, 3, 4)
            square_q(3, 3, 4)
            high_k(1, 1)
            raw_k(3, 3, 5)
            for h in range(2):
                exps(0, 0, h)
            pair(0, 0)
            pair(1, 1)
            with act.Fori(1, PAIRS // 2 - 1) as i:
                pair(i * 2, 0)
                pair(i * 2 + 1, 1)
            pair(PAIRS - 2, 0, more=False)
            pair(PAIRS - 1, 1, last=True, more=False)

            def weight_exps(half):
                c = slice(half * 4, half * 4 + 4)
                act.wait_ge(v_shift, half + 1)
                act.activation(wexp[:, c, :], shifted[:, c, :], ACT.Exp).then_inc(a_wexp, 1)
                act.activation(shg[:, c], logits[:, c, EXPERTS], ACT.Tanh, scale=0.5).then_inc(a_wexp, 1)

            def silu(slot, s, early, rows):
                act.wait_ge(t_G, s + 1)
                if not early:
                    act.wait_ge(v_mul1, s - 1)
                act.activation(gate_s[0:rows, slot, :], bank[GB][0:rows, :], ACT.Silu).then_inc(a_silu, 1)

            def high_inter(slot, s, early, rows):
                act.wait_ge(v_mul2, s + 1)
                if not early:
                    act.wait_ge(t_D, s - 1)
                act.activation(inter_hi[0:rows, slot, :], inter[0:rows, slot, :], ACT.Copy).then_inc(a_Ihi, 1)

            def copy_x(j):
                act.wait_ge(t_xT, j + 1)
                act.activation(xT[:, :, j * 256:(j + 1) * 256], bank4(7), ACT.Copy).then_inc(a_xT, 1)

            def keep_weights(half):
                act.wait_ge(t_wT, half + 1)
                c = slice(half * 512, half * 512 + 512)
                act.activation(wT[:, c], bank[[WB, 6][half]][:, :], ACT.Copy)
                act.activation(shT[:, c], bank[3 + half][0:2, :], ACT.Copy).then_inc(a_wT, 1)

            def keep_rows(half):
                act.wait_ge(t_wk, half + 1)
                act.activation(w_keep[:, half * 512:half * 512 + 512], bank[7][0:EXPERTS, :],
                               ACT.Copy).then_inc(a_wk, 1)

            copy_rows(2, 0, [QBK, KBK])
            copy_rows(2, 1, [QBK, KBK])
            split_e(1, 0)
            weight_exps(0)
            silu(0, 0, True, P)
            copy_rows(2, 2, [QBK, KBK])
            copy_rows(2, 3, [QBK, KBK])
            silu(1, 1, True, P)
            keep_weights(0)
            keep_rows(0)
            high_inter(0, 0, True, P)
            weight_exps(1)
            high_inter(1, 1, True, P)
            split_e(0, 1)
            silu(0, 2, False, P)
            silu(1, 3, False, P)
            keep_weights(1)
            keep_rows(1)
            high_inter(0, 2, False, P)
            high_inter(1, 3, False, P)
            act.wait_ge(l_shared, 16)
            act.activation(s_hi[:, :, :, :], s_raw[:, :, :, :], ACT.Copy).then_inc(a_rw, 1)
            act.wait_ge(l_shdown, 16)
            act.activation(sdn_hi[:, :], sdn_raw[:, :], ACT.Copy).then_inc(a_rw, 1)

            def two_pairs(j, last=False):
                for par in range(2):
                    for t in range(2):
                        s = j * 4 + par * 2 + t
                        silu(t, s, False, P)
                        high_inter(t, s, False, P)
                        if t == 0 and not (last and par == 1):
                            split_e(1 - par, j + par, (j * 2 + par + 1) * 2 - 2)

            with act.Fori(1, EPAIRS // 2 - 1) as j:
                two_pairs(j)
            two_pairs(EPAIRS // 2 - 1, last=True)
            for t in range(2):
                silu(t, 2 * EPAIRS + t, False, EI)
                copy_x(2 * t)
                copy_x(2 * t + 1)
                high_inter(t, 2 * EPAIRS + t, False, EI)

        @block.vector
        def _(dve):
            def ask_pow():
                pow_n[0] += 1
                dve.wait_ge(g_pow, pow_n[0])

            def tile_stats(i0, i1):
                for i in range(i0, i1):
                    ins = dve.bn_stats(stats[:, i, :], x[:, i, :])
                link(dve, ins)
                for i in range(i0, i1):
                    ins = dve.bn_aggr(mv[:, i, :], stats[:, i, :])
                link(dve, ins)

            def ask_rstd(i0, i1):
                dve.tensor_scalar(vare[:, i0:i1], mv[:, i0:i1, 1], EPS, None, ALU.add).then_inc(v_pow, 1)

            def normalise(i0, i1):
                for i in range(i0, i1):
                    dve.tensor_scalar(u[:, i, :], x[:, i, :], mv[:, i, 0:1], rstd[:, i:i + 1], ALU.subtract,
                                      ALU.mult).then_inc(v_u, 1)

            def low_rows(first, j, banks):
                dve.wait_ge(a_u, (first - 1) * 4 + j + 1)
                c = slice(j * 256, (j + 1) * 256)
                dve.tensor_tensor(xnT_lo[:, :, c], bank4(banks[j % 2]), f(xnT_hi[:, :, c]),
                                  ALU.subtract).then_inc(c_u, 1)

            dve.wait_ge(l_x, 32)
            tile_stats(0, TILES)
            ask_rstd(0, TILES)
            dve.wait_ge(pool_const, 8)
            dve.tensor_copy(ident_b[:, :], ident[:, :]).then_inc(v_const, 1)
            dve.tensor_copy(ones_r[:, :], ones[:, 0:EI]).then_inc(v_const, 1)

            def max_A(b):
                dve.wait_ge(t_eA, b + 1)
                dve.tensor_reduce(nmA[:, b, :], bank4(b), AX.X, ALU.max, negate=True).then_inc(v_mA, 1)

            max_A(0)
            max_A(1)
            ask_pow()
            normalise(0, 4)
            max_A(2)
            max_A(3)
            normalise(4, TILES)

            def norm_A(b):
                dve.wait_ge(a_eA, 2 * b + 2)
                link(dve, dve.reciprocal(invA[:, b, :], sumA[:, b, :]))
                for m in range(2):
                    ins = dve.tensor_scalar(attA[:, b, m, :], attA[:, b, m, :], invA[:, b, m:m + 1], None,
                                            ALU.mult)
                ins.then_inc(v_nA, 1)

            def add_A(b):
                dve.wait_ge(t_oA, b + 1)
                if b == 0:
                    dve.wait_ge(a_tg, 1)
                xb = x[:, 2 * b:2 * b + 2, :]
                dve.scalar_tensor_tensor(xb, bank4(6 + b % 2), tg[:, 0:1], xb, ALU.mult, ALU.add).then_inc(v_xA, 1)

            def weight_scale(i, n):
                dve.wait_ge(t_abs, i + 1)
                dve.tensor_scalar(wsc[:, i:i + 1], bank[[3, 7][i]][:, 0:1], 1.0 / n, EPS, ALU.mult,
                                  ALU.max).then_inc(v_abs, 1)
                dve.wait_ge(v_abs, i + 1)
                link(dve, dve.reciprocal(wsi[:, i:i + 1], wsc[:, i:i + 1]))

            def clip_above(src, scale):
                return dve.tensor_scalar(src, src, scale, 1.0, ALU.mult, ALU.min)

            def clip_below(src):
                return dve.tensor_scalar(src, src, -1.0, MAGIC, ALU.max, ALU.add)

            for b in range(BATCH):
                norm_A(b)
            add_A(0)
            dve.wait_ge(v_xA, 1)
            tile_stats(0, 2)
            add_A(1)
            weight_scale(0, 2 * INTER * HID)
            link(dve, clip_above(gate_raw[:, :, :], wsi[:, 0:1]))
            add_A(2)
            clip_below(gate_raw[:, :, :]).then_inc(v_gr, 1)
            add_A(3)
            dve.wait_ge(v_xA, 4)
            tile_stats(2, TILES)

            T = tinyB
            dve.tensor_scalar(T[:, 0, :], mv[:, :, 1], 1.0 + EPS, EPS * EPS, ALU.mult, ALU.add).then_inc(v_pow, 1)
            dve.wait_ge(l_g1, 16)
            for i in range(TILES):
                ins = dve.scalar_tensor_tensor(w1[:, i, :], x[:, i, :], mv[:, i, 0:1], g1[:, :], ALU.subtract,
                                               ALU.mult)
            link(dve, ins)
            link(dve, dve.tensor_reduce(T[:, 3, :], w1[:, :, :], AX.X, ALU.max, apply_absolute_value=True))
            ask_pow()
            link(dve, dve.tensor_tensor(T[:, 5, :], T[:, 3, :], T[:, 1, :], ALU.mult))
            link(dve, dve.tensor_scalar(T[:, 6, :], T[:, 5, :], EPS, None, ALU.max))
            link(dve, dve.reciprocal(T[:, 7, :], T[:, 6, :]))
            link(dve, dve.scalar_tensor_tensor(T[:, 3, :], T[:, 7, :], 127.0, T[:, 1, :], ALU.mult, ALU.mult))
            dve.tensor_scalar(T[:, 4, :], T[:, 6, :], 1.0 / 127.0, wsc[:, 0:1], ALU.mult, ALU.mult)
            for i in range(TILES + 1):
                if i < TILES:
                    dve.tensor_scalar(w1[:, i, :], w1[:, i, :], T[:, 3, i:i + 1], MAGIC, ALU.mult,
                                      ALU.add).then_inc(v_r1, 1)
                if i:
                    dve.wait_ge(v_r1, i)
                    dve.tensor_scalar(q1[:, i - 1, :], w1[:, i - 1, :], MAGIC, None, ALU.subtract).then_inc(v_q1, 1)
            weight_scale(1, INTER * HID)

            def absmax(i):
                dve.wait_ge(g_w2, i + 1)
                dve.tensor_reduce(amax2[:, i:i + 1], w2[:, i, :], AX.X, ALU.max,
                                  apply_absolute_value=True).then_inc(v_amax, 1)

            def scale_up(i):
                dve.tensor_scalar(w2[:, i, :], w2[:, i, :], T[:, 2, i:i + 1], MAGIC, ALU.mult,
                                  ALU.add).then_inc(v_r2, 1)

            def ask_rms2(i0, i1):
                dve.wait_ge(a_h1, i1)
                dve.tensor_scalar(T[:, 5, i0:i1], sumh[:, i0:i1], 1.0 / INTER, EPS, ALU.mult,
                                  ALU.add).then_inc(v_pow, 1)

            def scales2(i0, i1):
                c = slice(i0, i1)
                dve.wait_ge(v_amax, i1)
                ask_pow()
                link(dve, dve.tensor_tensor(T[:, 2, c], T[:, 6, c], amax2[:, c], ALU.mult))
                link(dve, dve.tensor_scalar(T[:, 3, c], T[:, 2, c], EPS, None, ALU.max))
                link(dve, dve.reciprocal(T[:, 7, c], T[:, 3, c]))
                link(dve, dve.scalar_tensor_tensor(T[:, 2, c], T[:, 7, c], 127.0, T[:, 6, c], ALU.mult, ALU.mult))
                link(dve, dve.tensor_scalar(T[:, 5, c], T[:, 3, c], 1.0 / 127.0, wsc[:, 1:2], ALU.mult, ALU.mult))
                link(dve, dve.tensor_scalar(T[:, 7, c], T[:, 5, c], tg[:, 2:3], None, ALU.mult))

            for i in range(TILES):
                if i == 1:
                    clip_above(down_raw[0:TAIL, 5, :], wsi[0:TAIL, 1:2])
                    link(dve, clip_above(down_raw[:, 0:5, :], wsi[:, 1:2]))
                if i == 2:
                    clip_below(down_raw[0:TAIL, 5, :])
                    clip_below(down_raw[:, 0:5, :]).then_inc(v_dr, 1)
                dve.wait_ge(a_s1, i + 1)
                dve.wait_ge(t_z1, i + 1)
                if i >= 2:
                    dve.wait_ge(a_h1, i - 1)
                    dve.wait_ge(g_w2, i - 1)
                for c in range(2):
                    cs = slice(c * HALF, (c + 1) * HALF)
                    dve.scalar_tensor_tensor(h_raw[:, i % 2, cs], bank[2 + c][:, 0:HALF], T[:, 4, i:i + 1],
                                             silu_g[:, i % 2, cs], ALU.mult, ALU.mult).then_inc(v_h1, 1)
                if i == TILES - 1:
                    scales2(0, 4)
                    scale_up(0)
                if i:
                    absmax(i - 1)
                if i == 4:
                    ask_rms2(0, 4)
            scale_up(1)
            absmax(TILES - 1)
            ask_rms2(4, 8)

            def add_down(i):
                dve.wait_ge(t_y2, i + 1)
                dve.scalar_tensor_tensor(x[:, i, :], bank[4 + i % 2][:, 0:HID], T[:, 7, i:i + 1], x[:, i, :],
                                         ALU.mult, ALU.add).then_inc(v_xB, 1)

            for i in range(TILES + 2):
                if i == 2:
                    scales2(4, 8)
                if i + 2 < TILES:
                    scale_up(i + 2)
                if i >= 2:
                    add_down(i - 2)
                if i >= 4 and i % 2 == 0:
                    dve.wait_ge(v_xB, i - 2)
                    tile_stats(i - 4, i - 2)
                if i == 6:
                    ask_rstd(0, 4)
                if i == 8:
                    ask_pow()
                    normalise(0, 4)
            dve.wait_ge(v_xB, TILES)
            tile_stats(6, TILES)
            ask_rstd(4, TILES)
            dve.wait_ge(l_gqk, 16)
            dve.tensor_scalar(gk[:, :], gqk_raw[:, 0:1], gqk_raw[:, 1:2], float(D) ** -0.5, ALU.mult,
                              ALU.mult).then_inc(v_gk, 1)

            def low_q(b, n):
                dve.wait_ge(a_hiQ, n + 1)
                dve.tensor_tensor(ql[:, :, b, :], bank4(QBK), f(qh[:, :, b, :]), ALU.subtract).then_inc(v_Qlo, 1)

            def low_k(b, n):
                dve.wait_ge(a_hiK, n + 1)
                dve.scalar_tensor_tensor(kl[:, :, b, :], bank4(KBK), gk[:, 0:1], f(kh[:, :, b, :]), ALU.mult,
                                         ALU.subtract).then_inc(v_Klo, 1)

            def mean_squares(b, n):
                dve.wait_ge(a_rawK, n + 1)
                wait(dve, v_sqK, n * 4)
                for c in range(4):
                    k = k_raw[:, b % 2, c // 2, c % 2, :]
                    dve.tensor_tensor_reduce(out=k_sq[:, c // 2, c % 2, :], in0=k, in1=k, scale=1.0, scalar=0.0,
                                             op0=ALU.mult, op1=ALU.add,
                                             accum_out=ssq[:, b % 2, 4 + c:5 + c]).then_inc(v_sqK, 1)
                dve.wait_ge(a_sqQ, n * 4 + 4)
                wait(dve, g_rms, n)
                dve.wait_ge(v_sqK, n * 4 + 4)
                dve.tensor_scalar(msq[:, :], ssq[:, b % 2, :], 1.0 / D, EPS, ALU.mult, ALU.add).then_inc(v_msq, 1)

            def row_max(b, g, h):
                dve.wait_ge(t_S, g * 2 + h + 1)
                wait(dve, a_exp, g * 4 - 4)
                dve.tensor_reduce(rowmax[:, b % 2, :, h], bank4(SBK[h]), AX.X, ALU.max,
                                  negate=True).then_inc(v_max, 1)

            def row_shift(b, g):
                dve.wait_ge(v_max, g * 2 + 2)
                dve.wait_ge(g_rms, g + 1)
                dve.tensor_tensor(shift[:, b % 2, :, :].rearrange("p t h -> p (t h)"),
                                  rowmax[:, b % 2, :, :].rearrange("p t h -> p (t h)"), rqk[:, b, 0:4],
                                  ALU.mult).then_inc(v_shift_c, 1)

            def low_att(g, j):
                dve.wait_ge(a_Thi, g * 2 + j + 1)
                dve.tensor_tensor(attT_lo[:, j, :, :], bank4(TBK[j]), f(attT_hi[:, j, :, :]),
                                  ALU.subtract).then_inc(v_Tlo, 1)

            def row_inverse(b, g):
                dve.wait_ge(a_exp, g * 4 + 4)
                wait(dve, v_Y, g * 4 - 12)
                dve.reciprocal(rowinv[:, b, :, :], rowsum[:, b % 2, :, :]).then_inc(v_inv, 1)

            def add_output(b, g, h):
                dve.wait_ge(t_Y, g * 2 + h + 1)
                if h == 0:
                    dve.wait_ge(v_inv, g + 1)
                wait(dve, v_Y, g * 4 + 2 * h)
                for t in range(2):
                    xb = x[:, 2 * b + t, :]
                    dve.scalar_tensor_tensor(xb, bank4(YBK)[:, t, :], rowinv[:, b, t, h:h + 1], xb, ALU.mult,
                                             ALU.add).then_inc(v_Y, 1)

            def low_o(g):
                dve.wait_ge(a_Ohi, g + 1)
                dve.tensor_tensor(o_lo[:, :, :], bank4(OBK), f(o_hi[:, :, :]), ALU.subtract).then_inc(v_Olo, 1)

            def low_m(p, par, bk):
                dve.wait_ge(a_Mhi, p + 1)
                dve.scalar_tensor_tensor(m_lo[:, par, :, :], bank4(bk), tg[:, 1:2], f(m_hi[:, par, :, :]), ALU.mult,
                                         ALU.subtract).then_inc(v_Mlo, 1)

            def pair(p, par, first=False, last=False):
                for b in range(BATCH):
                    g = p * 4 + b
                    n = g + 4
                    start = first and b == 0
                    final_group = last and b == 3
                    turning = not (last and b >= 2)
                    if not final_group:
                        row_max((b + 1) % 4, g + 1, 0)
                    if not start:
                        low_o(g - 1)
                    if not final_group:
                        row_max((b + 1) % 4, g + 1, 1)
                    if turning:
                        low_q((b + 2) % 4, n - 2)
                    if b == 1 and not last:
                        low_m(p + 1, 1 - par, KBK)
                    low_att(g, 0)
                    if not final_group:
                        row_shift((b + 1) % 4, g + 1)
                    low_att(g, 1)
                    if final_group:
                        ask_pow()
                        normalise(0, 4)
                    if not start:
                        add_output((b + 3) % 4, g - 1, 0)
                    if turning:
                        low_k((b + 2) % 4, n - 2)
                    if not (last and b > 0):
                        mean_squares((b + 3) % 4, n - 1)
                    if not final_group:
                        row_inverse((b + 1) % 4, g + 1)
                    if not start:
                        add_output((b + 3) % 4, g - 1, 1)
                    if last and 0 < b < 3:
                        dve.wait_ge(v_Y, g * 4)
                        tile_stats(2 * b - 2, 2 * b)
                    if last and b == 2:
                        ask_rstd(0, 4)

            low_m(0, 0, 0)
            low_rows(1, 0, TBK)
            ask_pow()
            normalise(4, TILES)
            low_rows(1, 1, TBK)
            mean_squares(0, 0)
            mean_squares(1, 1)
            low_rows(1, 2, TBK)
            low_q(0, 0)
            low_rows(1, 3, TBK)
            low_k(0, 0)
            mean_squares(2, 2)
            low_q(1, 1)
            low_k(1, 1)
            for h in range(2):
                row_max(0, 0, h)
            row_shift(0, 0)
            row_inverse(0, 0)
            pair(0, 0, first=True)
            pair(1, 1)
            with dve.Fori(1, PAIRS // 2 - 1) as i:
                pair(i * 2, 0)
                pair(i * 2 + 1, 1)
            pair(PAIRS - 2, 0)
            pair(PAIRS - 1, 1, last=True)
            low_o(GROUPS - 1)

            def choose(half):
                c = slice(half * 4, half * 4 + 4)
                dve.wait_ge(t_log, half + 1)
                link(dve, dve.tensor_copy(logits[:, c, :],
                                          bank[3 + half][:, 0:4 * LOGC].rearrange("p (i n) -> p i n", i=4)))
                for i in range(half * 4, half * 4 + 4):
                    ins = dve.max(top8[:, i, :], logits[:, i, 0:EXPERTS])
                link(dve, ins)
                lg = logits[:, c, 0:EXPERTS]
                dve.tensor_tensor(shifted[:, c, :], lg, top8[:, c, 0:1].broadcast_to([P, 4, EXPERTS]),
                                  ALU.subtract).then_inc(v_shift, 1)
                for i in range(half * 4, half * 4 + 4):
                    ins = dve.match_replace(out=struck[:, i, :], in_to_replace=top8[:, i, :],
                                            in_values=logits[:, i, 0:EXPERTS], imm_value=LOWEST)
                link(dve, ins)
                link(dve, dve.tensor_tensor(chosen[:, c, :], struck[:, c, :], lg, ALU.not_equal))

            def weights(half):
                c = slice(half * 4, half * 4 + 4)
                dve.wait_ge(a_wexp, 2 * half + 2)
                link(dve, dve.tensor_tensor(chosen[:, c, :], chosen[:, c, :], wexp[:, c, :], ALU.mult))
                link(dve, dve.tensor_reduce(wsum[:, c], chosen[:, c, :], AX.X, ALU.add))
                dve.reciprocal(winv[:, c], wsum[:, c])
                link(dve, dve.tensor_scalar(shg[:, c], shg[:, c], 0.5, 0.5, ALU.mult, ALU.add))
                dve.tensor_tensor(chosen[:, c, :], chosen[:, c, :],
                                  winv[:, c].unsqueeze(2).broadcast_to([P, 4, EXPERTS]), ALU.mult)
                link(dve, dve.tensor_copy(shcat[:, c, 0].bitcast(F32R), shg[:, c]))
                dve.tensor_copy(wcat[:, c, 0:EXPERTS].bitcast(F32R), chosen[:, c, :])
                link(dve, dve.tensor_tensor(shcat[:, c, 1].bitcast(F32R), shg[:, c], shcat[:, c, 0],
                                            ALU.subtract))
                dve.tensor_tensor(wcat[:, c, EXPERTS:P].bitcast(F32R), chosen[:, c, :], wcat[:, c, 0:EXPERTS],
                                  ALU.subtract).then_inc(v_wcat, 1)

            def low_e(par, e):
                dve.wait_ge(a_Ehi, e + 1)
                dve.tensor_tensor(e_lo[:, par, :], e_raw[:, par, :], f(e_hi[:, par, :]),
                                  ALU.subtract).then_inc(v_Elo, 1)

            def select(par, e):
                dve.tensor_copy(selb[:, par, :].rearrange("p (a n) -> p a n", a=2),
                                expert_rows[:, bass.ds(e * 2, 2)].unsqueeze(2).broadcast_to([P, 2, EI])
                                ).then_inc(v_sel, 1)

            def times_up(slot, s, rows):
                dve.wait_ge(a_silu, s + 1)
                dve.wait_ge(t_U, s + 1)
                dve.tensor_tensor(prod[0:rows, slot, :], gate_s[0:rows, slot, :], bank[UB][0:rows, :],
                                  ALU.mult).then_inc(v_mul1, 1)

            def times_weight(slot, s, early, rows, spread):
                dve.wait_ge(v_mul1, s + 1)
                dve.wait_ge(t_W, spread)
                if not early:
                    dve.wait_ge(a_Ihi, s - 1)
                dve.tensor_tensor(inter[0:rows, slot, :], prod[0:rows, slot, :], bank[WB][0:rows, :],
                                  ALU.mult).then_inc(v_mul2, 1)

            def times_loaded(par, t, s, turn):
                dve.wait_ge(v_mul1, s + 1)
                dve.wait_ge(l_wall[par], turn * 32)
                dve.wait_ge(a_Ihi, s - 1)
                dve.tensor_tensor(inter[:, t, :], prod[:, t, :], w_all[:, par, t * 512:(t + 1) * 512],
                                  ALU.mult).then_inc(v_mul2, 1)

            def low_inter(slot, s, rows):
                dve.wait_ge(a_Ihi, s + 1)
                dve.tensor_tensor(inter_lo[0:rows, slot, :], inter[0:rows, slot, :], f(inter_hi[0:rows, slot, :]),
                                  ALU.subtract).then_inc(v_Ilo, 1)

            low_rows(2, 0, [QBK, KBK])
            low_rows(2, 1, [QBK, KBK])
            for h in range(2):
                add_output(3, GROUPS - 1, h)
            dve.wait_ge(v_Y, 4 * GROUPS)
            tile_stats(4, TILES)
            ask_rstd(4, TILES)
            select(0, 0)
            select(1, 1)
            choose(0)
            ask_pow()
            normalise(4, TILES)
            weights(0)
            low_rows(2, 2, [QBK, KBK])
            low_rows(2, 3, [QBK, KBK])
            times_up(0, 0, P)
            times_weight(0, 0, True, P, 1)
            times_up(1, 1, P)
            low_inter(0, 0, P)
            times_weight(1, 1, True, P, 2)
            choose(1)
            low_inter(1, 1, P)
            weights(1)
            times_up(0, 2, P)
            low_e(0, 2)
            times_up(1, 3, P)
            times_weight(0, 2, False, P, 3)
            low_inter(0, 2, P)
            times_weight(1, 3, False, P, 4)
            low_inter(1, 3, P)

            def two_pairs(j, last=False):
                for par in range(2):
                    for t in range(2):
                        s = j * 4 + par * 2 + t
                        times_up(t, s, P)
                        times_loaded(par, t, s, j)
                        low_inter(t, s, P)
                        if t == 0 and not (last and par == 1):
                            low_e(1 - par, j * 2 + par + 1)

            with dve.Fori(1, EPAIRS // 2 - 1) as j:
                two_pairs(j)
            two_pairs(EPAIRS // 2 - 1, last=True)
            for t in range(2):
                times_up(t, 2 * EPAIRS + t, EI)
                times_weight(t, 2 * EPAIRS + t, False, EI, 5 + t)
                low_inter(t, 2 * EPAIRS + t, EI)
            dve.wait_ge(a_xT, 4)
            for t in range(2):
                for hb in range(2):
                    dve.wait_ge(t_D, 2 * EPAIRS + 2 * t + hb + 1)
                    dve.scalar_tensor_tensor(final[:, hb, t, :], bank[ACC[hb][t]][:, :], tg[:, 3:4],
                                             xT[:, hb, t * 512:(t + 1) * 512], ALU.mult, ALU.add).then_inc(v_out, 1)


def kernel(**inputs):
    import numpy as np
    import concourse.bacc as bacc
    from concourse.bass_utils import run_bass_kernel_spmd

    a = {k: np.asarray(v) for k, v in inputs.items()}

    def tiles(v):
        return v.reshape(TILES, P, v.shape[-1]).transpose(1, 0, 2)

    def parts(v):
        return v.reshape(-1, P, v.shape[-1]).transpose(1, 0, 2)

    ctx2 = a["ctx_1024"].reshape(TOK, CDIM)
    wq = a["L1_xattn_Wq"].reshape(KH, P, PAIRS, 2, D).transpose(2, 1, 0, 3, 4).reshape(PAIRS, P, 512)
    wk = a["L1_xattn_Wk"].reshape(P, PAIRS, 2 * D).transpose(1, 0, 2)
    wv = a["L1_xattn_Wv"].reshape(CDIM, PAIRS, 2, D).transpose(1, 3, 2, 0).reshape(PAIRS, D, 2 * CDIM)
    wo = a["L1_xattn_Wo"].reshape(PAIRS, 2, D, HID).transpose(0, 2, 1, 3).reshape(PAIRS, D, 2 * HID)
    gu = a["L1_ffn_gu_w"].reshape(EPAIRS, 2, 2, EI, KH, P).transpose(0, 5, 2, 4, 1, 3).reshape(EPAIRS, P, 512)
    dp = a["L1_ffn_dp_w"].reshape(EPAIRS, 2, HID, EI).transpose(0, 1, 3, 2).reshape(EPAIRS, P, HID)
    router = np.concatenate([a["L1_ffn_gate_w"], a["L1_ffn_sh_gate1_w"],
                             np.zeros((1, HID), np.float32)], 0).T
    downT = a["L0_ffn_down_w"].T
    arrays = {
        "x_tok": tiles(a["x"].reshape(TOK, HID)),
        "ctx_tok": tiles(ctx2),
        "ctxT": ctx2.T,
        "qk0": np.stack([a["L0_xattn_Wq"].T, a["L0_xattn_Wk"].T], 1),
        "bias0": np.stack([a["L0_xattn_bq"], a["L0_xattn_bk"]], 1),
        "gains": np.broadcast_to(np.concatenate([a["g_xattn"], a["g_ffn"]])[None, :], (P, 4)),
        "gate_wT": parts(a["L0_ffn_gate_w"].T),
        "down_wT": parts(downT[:5 * P]),
        "down_tail": downT[5 * P:],
        "norm_g1": a["L0_ffn_gate_norm_w"],
        "norm_g2": a["L0_ffn_down_norm_w"],
        "gqk": np.stack([a["L1_xattn_gq"], a["L1_xattn_gk"]], 1),
        "head_qk": np.concatenate([wq, wk], 2),
        "head_vo": np.concatenate([wv, wo], 2),
        "router_w": parts(router),
        "expert_w": np.concatenate([gu, dp], 2),
        "shared_w": np.stack([parts(a["L1_ffn_sh_gate_w"].T), parts(a["L1_ffn_sh_up_w"].T)], 1),
        "shared_down": a["L1_ffn_sh_down_w"].T,
    }
    arrays = {k: np.ascontiguousarray(v) for k, v in arrays.items()}
    nc = bacc.Bacc("TRN2", target_bir_lowering=False, num_devices=1)
    aps = [nc.dram_tensor(f"in_{k}", v.shape, mybir.dt.from_np(v.dtype), kind="ExternalInput").ap()
           for k, v in arrays.items()]
    out = nc.dram_tensor("outT", (KH, P, TOK), F32, kind="ExternalOutput").ap()
    w_rows = nc.dram_tensor("w_rows", (EXPERTS, TOK), F32, kind="Internal").ap()
    flamingo_kernel(nc, *aps, out, w_rows)
    r = run_bass_kernel_spmd(nc, [{f"in_{k}": v for k, v in arrays.items()}], core_ids=[0])
    outT = r.results[0]["outT"]
    return np.ascontiguousarray(outT.reshape(HID, TOK).T).reshape(BATCH, SEQ, HID)
```
